# Optimizing a Trainium2 kernel written in Bass

```python
import numpy as np
import jax
import jax.numpy as jnp

def _softmax(x, axis=-1):
    return jax.nn.softmax(x, axis=axis)

def _gelu(x):
    return jax.nn.gelu(x, approximate=True)

def _silu(x):
    return jax.nn.silu(x)

def _sigmoid(x):
    return jax.nn.sigmoid(x)

def _layernorm(x, axis=-1, eps=1e-05):
    m = jnp.mean(x, axis=axis, keepdims=True)
    v = jnp.var(x, axis=axis, keepdims=True)
    return (x - m) / jnp.sqrt(v + eps)

def _scatter_add(tgt, idx, src, axis=0):
    return tgt.at[idx].add(src)

def _segment_sum(src, seg, n):
    return jax.ops.segment_sum(src, seg, n)
kernel_name = 'mk_recurrent_d2_jaxref_r8_560e1e'

def setup_inputs(seed: int=0):
    np.random.seed(seed)
    _w = jnp.asarray

    def _L0_attn_setup():
        import math
        import jax, jax.numpy as jnp
        import numpy as np
        B, S, D = (4, 256, 128)

        def _complex_proj(x, W, b):
            p = jnp.einsum('bsd,ed->bse', x, W) + b
            p = p.reshape(*x.shape[:-1], x.shape[-1], 2)
            return (p[..., 0], p[..., 1])
        key = jax.random.key(seed)
        ks = jax.random.split(key, 9)
        sd = 1.0 / math.sqrt(D)
        return {'hidden_states': jax.random.normal(ks[0], (B, S, D), jnp.float32), 'Wq': jax.random.normal(ks[1], (2 * D, D), jnp.float32) * sd, 'bq': jax.random.normal(ks[2], (2 * D,), jnp.float32) * 0.01, 'Wk': jax.random.normal(ks[3], (2 * D, D), jnp.float32) * sd, 'bk': jax.random.normal(ks[4], (2 * D,), jnp.float32) * 0.01, 'Wv': jax.random.normal(ks[5], (2 * D, D), jnp.float32) * sd, 'bv': jax.random.normal(ks[6], (2 * D,), jnp.float32) * 0.01, 'Wo': jax.random.normal(ks[7], (D, 2 * D), jnp.float32) * sd, 'bo': jax.random.normal(ks[8], (D,), jnp.float32) * 0.01}
    _L0_attn_in = _L0_attn_setup()

    def _L0_ffn_setup():
        import jax, jax.numpy as jnp
        import numpy as np
        TOP_K = 2
        key = jax.random.key(seed)
        ks = jax.random.split(key, 5)
        B, T, D, E, F = (2, 256, 128, 8, 256)
        scale_d = 1.0 / np.sqrt(D)
        scale_f = 1.0 / np.sqrt(F)
        return {'x': jax.random.normal(ks[0], (B, T, D), jnp.float32), 'kernel_router_DE': jax.random.normal(ks[1], (D, E), jnp.float32) * scale_d, 'kernel_gating_EDF': jax.random.normal(ks[2], (E, D, F), jnp.float32) * scale_d, 'kernel_up_EDF': jax.random.normal(ks[3], (E, D, F), jnp.float32) * scale_d, 'kernel_down_EFD': jax.random.normal(ks[4], (E, F, D), jnp.float32) * scale_f}
    _L0_ffn_in = _L0_ffn_setup()

    def _L1_attn_setup():
        import jax, jax.numpy as jnp
        import numpy as np
        N_SCALES = 11
        N_TAPS = 4
        OFFSETS = [(1 << j) * tau for j in range(N_SCALES) for tau in range(N_TAPS)]

        def _shift(a, off):
            N = a.shape[2]
            return jnp.pad(a[:, :, :N - off], ((0, 0), (0, 0), (off, 0), (0, 0)))
        key = jax.random.key(seed)
        ks = jax.random.split(key, 8)
        B, N, D, H = (4, 512, 128, 16)
        w_scale = 0.02
        return {'x': jax.random.normal(ks[0], (B, N, D), jnp.float32), 'w_qkv': jax.random.normal(ks[1], (D, 3 * D), jnp.float32) * w_scale, 'b_qkv': jnp.zeros((3 * D,), jnp.float32), 'w_out': jax.random.normal(ks[2], (D, D), jnp.float32) * w_scale, 'b_out': jnp.zeros((D,), jnp.float32), 'w_gate': jax.random.normal(ks[3], (D, D), jnp.float32) * w_scale, 'b_gate': 2.0 * jnp.ones((D,), jnp.float32), 'pos_bias': jax.random.normal(ks[4], (len(OFFSETS), H), jnp.float32) * 0.1}
    _L1_attn_in = _L1_attn_setup()

    def _L1_ffn_setup():
        import jax, jax.numpy as jnp
        import numpy as np
        T, Z, D_DIM = (8, 256, 128)
        N_EXP, P_SLOT, H = (64, 32, 128)
        LN_EPS = 1e-05
        key = jax.random.key(seed)
        k = jax.random.split(key, 5)
        s = 0.02
        return {'x': jax.random.normal(k[0], (T, Z, D_DIM), dtype=jnp.float32), 'phi_w': jax.random.normal(k[1], (N_EXP * P_SLOT, D_DIM), dtype=jnp.float32) * s, 'phi_b': jax.random.normal(k[2], (N_EXP * P_SLOT,), dtype=jnp.float32) * s, 'expert_w': jax.random.normal(k[3], (N_EXP, D_DIM, H), dtype=jnp.float32) * s, 'expert_b': jax.random.normal(k[4], (N_EXP, H), dtype=jnp.float32) * s}
    _L1_ffn_in = _L1_ffn_setup()
    _d = {'L0_attn_hidden_states': _L0_attn_in['hidden_states'], 'L0_attn_Wq': _L0_attn_in['Wq'], 'L0_attn_bq': _L0_attn_in['bq'], 'L0_attn_Wk': _L0_attn_in['Wk'], 'L0_attn_bk': _L0_attn_in['bk'], 'L0_attn_Wv': _L0_attn_in['Wv'], 'L0_attn_bv': _L0_attn_in['bv'], 'L0_attn_Wo': _L0_attn_in['Wo'], 'L0_attn_bo': _L0_attn_in['bo'], 'L0_ffn_kernel_router_DE': _L0_ffn_in['kernel_router_DE'], 'L0_ffn_kernel_gating_EDF': _L0_ffn_in['kernel_gating_EDF'], 'L0_ffn_kernel_up_EDF': _L0_ffn_in['kernel_up_EDF'], 'L0_ffn_kernel_down_EFD': _L0_ffn_in['kernel_down_EFD'], 'L1_attn_w_qkv': _L1_attn_in['w_qkv'], 'L1_attn_b_qkv': _L1_attn_in['b_qkv'], 'L1_attn_w_out': _L1_attn_in['w_out'], 'L1_attn_b_out': _L1_attn_in['b_out'], 'L1_attn_w_gate': _L1_attn_in['w_gate'], 'L1_attn_b_gate': _L1_attn_in['b_gate'], 'L1_attn_pos_bias': _L1_attn_in['pos_bias'], 'L1_ffn_phi_w': _L1_ffn_in['phi_w'], 'L1_ffn_phi_b': _L1_ffn_in['phi_b'], 'L1_ffn_expert_w': _L1_ffn_in['expert_w'], 'L1_ffn_expert_b': _L1_ffn_in['expert_b']}
    _x0 = _d['L0_attn_hidden_states']
    _d['L0_attn_hidden_states'] = jax.random.normal(jax.random.fold_in(jax.random.key(seed), 1), (8, 256, 128), dtype=_x0.dtype)
    del _x0
    return _d

def reference(L0_attn_hidden_states, L0_attn_Wq, L0_attn_bq, L0_attn_Wk, L0_attn_bk, L0_attn_Wv, L0_attn_bv, L0_attn_Wo, L0_attn_bo, L0_ffn_kernel_router_DE, L0_ffn_kernel_gating_EDF, L0_ffn_kernel_up_EDF, L0_ffn_kernel_down_EFD, L1_attn_w_qkv, L1_attn_b_qkv, L1_attn_w_out, L1_attn_b_out, L1_attn_w_gate, L1_attn_b_gate, L1_attn_pos_bias, L1_ffn_phi_w, L1_ffn_phi_b, L1_ffn_expert_w, L1_ffn_expert_b):

    def _L0_attn_ref(hidden_states, Wq, bq, Wk, bk, Wv, bv, Wo, bo):
        import math
        import jax, jax.numpy as jnp
        import numpy as np
        B, S, D = (4, 256, 128)

        def _complex_proj(x, W, b):
            p = jnp.einsum('bsd,ed->bse', x, W) + b
            p = p.reshape(*x.shape[:-1], x.shape[-1], 2)
            return (p[..., 0], p[..., 1])
        dim = hidden_states.shape[-1]
        qr, qi = _complex_proj(hidden_states, Wq, bq)
        kr, ki = _complex_proj(hidden_states, Wk, bk)
        vr, vi = _complex_proj(hidden_states, Wv, bv)
        scale = 1.0 / math.sqrt(dim)
        scores = (jnp.einsum('bsd,btd->bst', qr, kr) + jnp.einsum('bsd,btd->bst', qi, ki)) * scale
        w = jax.nn.softmax(scores, axis=-1)
        o_r = jnp.einsum('bst,btd->bsd', w, vr)
        o_i = jnp.einsum('bst,btd->bsd', w, vi)
        out = jnp.stack([o_r, o_i], axis=-1).reshape(*hidden_states.shape[:-1], 2 * dim)
        return jnp.einsum('bse,de->bsd', out, Wo) + bo

    def _L0_ffn_ref(x, kernel_router_DE, kernel_gating_EDF, kernel_up_EDF, kernel_down_EFD):
        import jax, jax.numpy as jnp
        import numpy as np
        TOP_K = 2
        E = kernel_router_DE.shape[-1]
        x = x.astype(jnp.float32)
        router_logits_BTE = jnp.einsum('BTD,DE->BTE', x, kernel_router_DE)
        probs_BTE = jax.nn.softmax(router_logits_BTE.astype(jnp.float32), axis=-1)
        weights_BTX, indices_BTX = jax.lax.top_k(probs_BTE, TOP_K)
        norm_weights_BTX = jax.nn.softmax(weights_BTX, axis=-1)
        one_hot_BTXE = jax.nn.one_hot(indices_BTX, num_classes=E, dtype=jnp.float32)
        full_weights_BTE = jnp.sum(one_hot_BTXE * norm_weights_BTX[..., None], axis=2)
        gating_BTEF = jnp.einsum('BTD,EDF->BTEF', x, kernel_gating_EDF)
        fuse_BTEF = jax.nn.silu(gating_BTEF) * jnp.einsum('BTD,EDF->BTEF', x, kernel_up_EDF)
        down_BTED = jnp.einsum('BTEF,EFD->BTED', fuse_BTEF, kernel_down_EFD)
        out_BTD = jnp.einsum('BTED,BTE->BTD', down_BTED, full_weights_BTE)
        return out_BTD.astype(jnp.float32)

    def _L1_attn_ref(x, w_qkv, b_qkv, w_out, b_out, w_gate, b_gate, pos_bias):
        import jax, jax.numpy as jnp
        import numpy as np
        N_SCALES = 11
        N_TAPS = 4
        OFFSETS = [(1 << j) * tau for j in range(N_SCALES) for tau in range(N_TAPS)]

        def _shift(a, off):
            N = a.shape[2]
            return jnp.pad(a[:, :, :N - off], ((0, 0), (0, 0), (off, 0), (0, 0)))
        B, N, D = x.shape
        H = pos_bias.shape[1]
        HD = D // H
        scale = HD ** (-0.5)
        qkv = x @ w_qkv + b_qkv
        q, k, v = jnp.split(qkv, 3, axis=-1)
        q = q.reshape(B, N, H, HD).transpose(0, 2, 1, 3)
        k = k.reshape(B, N, H, HD).transpose(0, 2, 1, 3)
        v = v.reshape(B, N, H, HD).transpose(0, 2, 1, 3)
        scores = []
        for off in OFFSETS:
            if off == 0:
                ks_ = k
            elif off >= N:
                ks_ = jnp.zeros_like(k)
            else:
                ks_ = _shift(k, off)
            scores.append(jnp.einsum('bhnd,bhnd->bhn', q, ks_) * scale)
        scores = jnp.stack(scores, axis=-1)
        scores = scores + pos_bias.T[None, :, None, :]
        attn = jax.nn.softmax(scores, axis=-1)
        out = jnp.zeros_like(q)
        for i, off in enumerate(OFFSETS):
            if off >= N:
                continue
            vs = v if off == 0 else _shift(v, off)
            out = out + attn[..., i:i + 1] * vs
        gathered = out.transpose(0, 2, 1, 3).reshape(B, N, D)
        gate = jax.nn.sigmoid(x @ w_gate + b_gate)
        return gathered * gate @ w_out + b_out

    def _L1_ffn_ref(x, phi_w, phi_b, expert_w, expert_b):
        import jax, jax.numpy as jnp
        import numpy as np
        T, Z, D_DIM = (8, 256, 128)
        N_EXP, P_SLOT, H = (64, 32, 128)
        LN_EPS = 1e-05
        t, z, d = x.shape
        n = expert_w.shape[0]
        p = phi_w.shape[0] // n
        logits = (jnp.einsum('tzd,ed->tze', x, phi_w) + phi_b).reshape(t, z, n, p)
        D = jax.nn.softmax(logits, axis=3)
        C = jax.nn.softmax(logits, axis=2)
        X_tilde = jnp.einsum('tznp,tzd->npd', D, x)
        X_tilde = jnp.clip(X_tilde, -33000.0, 65000.0)
        mu = jnp.mean(X_tilde, axis=-1, keepdims=True)
        var = jnp.mean(jnp.square(X_tilde - mu), axis=-1, keepdims=True)
        X_tilde = (X_tilde - mu) * jax.lax.rsqrt(var + LN_EPS)
        X_tilde = jnp.tanh(X_tilde)
        Y_tilde = jnp.einsum('npd,ndH->npH', X_tilde, expert_w) + expert_b[:, None, :]
        Y = jnp.einsum('tznp,npH->tzH', C, Y_tilde)
        return Y
    x = L0_attn_hidden_states
    xn = _layernorm(x, axis=-1)
    s = _L0_attn_ref(xn, L0_attn_Wq, L0_attn_bq, L0_attn_Wk, L0_attn_bk, L0_attn_Wv, L0_attn_bv, L0_attn_Wo, L0_attn_bo)
    g = _silu(_L0_ffn_ref(xn, L0_ffn_kernel_router_DE, L0_ffn_kernel_gating_EDF, L0_ffn_kernel_up_EDF, L0_ffn_kernel_down_EFD))
    x = x + s * g
    xn = _layernorm(x, axis=-1)
    s = _L1_attn_ref(xn, L1_attn_w_qkv, L1_attn_b_qkv, L1_attn_w_out, L1_attn_b_out, L1_attn_w_gate, L1_attn_b_gate, L1_attn_pos_bias)
    g = _silu(_L1_ffn_ref(xn, L1_ffn_phi_w, L1_ffn_phi_b, L1_ffn_expert_w, L1_ffn_expert_b))
    x = x + s * g
    return x

_drawn_inputs = setup_inputs


def setup_inputs(seed=0):
    import zlib

    import numpy as np

    out = dict(_drawn_inputs(seed))
    spreads = {'L1_attn_b_qkv': (0.0, 0.8), 'L1_attn_b_out': (0.0, 0.354), 'L1_attn_b_gate': (2.0, 0.6)}
    factors = {'L0_attn_bq': 46.922,
     'L0_attn_bk': 64.0,
     'L0_attn_bv': 8.0,
     'L0_attn_bo': 8.0,
     'L1_attn_w_qkv': 8.0,
     'L1_attn_w_out': 8.0,
     'L1_attn_w_gate': 8.0,
     'L1_attn_pos_bias': 8.0,
     'L1_ffn_phi_w': 8.0,
     'L1_ffn_phi_b': 8.0,
     'L1_ffn_expert_b': 8.0}
    for name, (base, spread) in spreads.items():
        noise = np.random.default_rng([zlib.crc32(name.encode()), seed]).standard_normal(out[name].shape)
        drawn = base * np.exp(spread * noise) if base else spread * noise
        out[name] = jnp.asarray(drawn.astype(out[name].dtype))
    for name, factor in factors.items():
        out[name] = (out[name] * factor).astype(out[name].dtype)
    return out
```

```python
import concourse.bass as bass
from concourse import mybir
from contextlib import ExitStack

F32 = mybir.dt.float32
BF16 = mybir.dt.bfloat16
ALU = mybir.AluOpType
ACT = mybir.ActivationFunctionType
AX = mybir.AxisListType

P = 128
BATCH, SEQ, D = 8, 256, 128
TOK = BATCH * SEQ
NT = TOK // P
TPB = SEQ // P
E2 = 2 * D
NE, FF = 8, 256
HEADS, HD = 16, 8
NX, SLOTS, HOUT = 64, 32, 128
NP = NX * SLOTS
NPT = NP // P
XPT = P // SLOTS
BANK = 512
EPS = 1e-5
SCALE0 = float(D) ** -0.5
SCALE1 = float(HD) ** -0.5

ALL_OFFSETS = [(1 << j) * tau for j in range(11) for tau in range(4)]
OFFS = sorted({o for o in ALL_OFFSETS if o < SEQ})
NO = len(OFFS)
NS = NO + 1
MEMBERS = [[i for i, o in enumerate(ALL_OFFSETS) if o == off] for off in OFFS]
MEMBERS.append([i for i, o in enumerate(ALL_OFFSETS) if o >= SEQ])
BIAS_ORDER = [i for m in MEMBERS for i in m]
BIAS_START = [sum(len(m) for m in MEMBERS[:s]) for s in range(NS)]

COLS = ["bq0", "bq1", "bk0", "bk1", "bv0", "bv1", "b1q", "b1k", "b1v", "bgate"]
COL = {n: i for i, n in enumerate(COLS)}
STAGE = None


def tiles(ap):
    return ap.rearrange("(t p) d -> p t d", p=P)


class Chain:

    def __init__(self, eng, sem):
        self.eng, self.sem, self.n = eng, sem, 0

    def __call__(self, ins):
        self.n += 1
        ins.then_inc(self.sem, 1)
        self.eng.wait_ge(self.sem, self.n)
        return self.n


def build(nc, a, out, dbg):
    ctx = ExitStack()
    with ctx:
        def sb(name, shape, dt=F32, c=None):
            return (c or ctx).enter_context(nc.sbuf_tensor(name, shape, dt))

        ident = sb("ident", [P, P])
        cols = sb("cols", [P, len(COLS)])
        x_res = sb("x_res", [P, NT, D])
        xn = sb("xn", [P, NT, D])
        xnT = sb("xnT", [P, TOK])
        s_att = sb("s_att", [P, NT, D])
        g_ffn = sb("g_ffn", [P, NT, D])

        def front_block(layer):
            with ExitStack() as c:
                sem = lambda n: c.enter_context(nc.semaphore(f"{n}_{layer}"))
                loaded, consts, dve_seq, centered, squared = map(sem, ("loaded", "consts", "dve_seq", "centered", "squared"))
                var_ready, rstd_ready, normed, transposed, act_done, silu_done = map(
                    sem, ("var_ready", "rstd_ready", "normed", "transposed", "act_done", "silu_done"))
                mean = sb(f"mean{layer}", [P, NT], c=c)
                var = sb(f"var{layer}", [P, NT], c=c)
                rstd = sb(f"rstd{layer}", [P, NT], c=c)
                half = sb(f"half{layer}", [P, 1], c=c)
                sq = sb(f"sq{layer}", [P, NT, D], c=c)
                tp = c.enter_context(nc.psum_tensor(f"tp{layer}", [P, 4, BANK], F32))
                with nc.Block() as block:
                    @block.sync
                    def _(sp):
                        if layer == 0:
                            sp.dma_start(x_res[:, :, :], tiles(a["x"])).then_inc(loaded, 16)
                            sp.dma_start(cols[:, :], a["cols"]).then_inc(loaded, 16)
                            sp.wait_ge(loaded, 32)

                    @block.gpsimd
                    def _(pool):
                        nc.gpsimd.memset(half[:, :], -0.5).then_inc(consts, 1)
                        if layer == 0:
                            nc.gpsimd.memset(ident[:, :], 0.0).then_inc(consts, 1)
                            pool.wait_ge(consts, 2)
                            nc.gpsimd.affine_select(out=ident[:, :], in_=ident[:, :], compare_op=ALU.not_equal, fill=1.0,
                                                    base=0, pattern=[[-1, P]], channel_multiplier=1).then_inc(consts, 1)
                        pool.wait_ge(consts, 3 if layer == 0 else 1)
                        pool.wait_ge(var_ready, 1)
                        nc.gpsimd.tensor_tensor(rstd[:, :], var[:, :], half[:, 0:1].to_broadcast([P, NT]),
                                                ALU.pow).then_inc(rstd_ready, 1)

                    @block.vector
                    def _(dve):
                        link = Chain(dve, dve_seq)
                        if layer == 0:
                            dve.wait_ge(loaded, 32)
                        else:
                            dve.wait_ge(silu_done, 1)
                            link(nc.vector.tensor_tensor(sq[:, :, :], g_ffn[:, :, :], s_att[:, :, :], ALU.mult))
                            link(nc.vector.tensor_tensor(x_res[:, :, :], x_res[:, :, :], sq[:, :, :], ALU.add))
                        link(nc.vector.tensor_reduce(mean[:, :], x_res[:, :, :], AX.X, ALU.add))
                        link(nc.vector.tensor_scalar(mean[:, :], mean[:, :], 1.0 / D, None, ALU.mult))
                        nc.vector.tensor_tensor(xn[:, :, :], x_res[:, :, :], mean[:, :].unsqueeze(2).broadcast_to([P, NT, D]),
                                                ALU.subtract).then_inc(centered, 1)
                        dve.wait_ge(squared, 1)
                        link(nc.vector.tensor_reduce(var[:, :], sq[:, :, :], AX.X, ALU.add))
                        nc.vector.tensor_scalar(var[:, :], var[:, :], 1.0 / D, EPS, ALU.mult, ALU.add).then_inc(var_ready, 1)
                        dve.wait_ge(rstd_ready, 1)
                        nc.vector.tensor_tensor(xn[:, :, :], xn[:, :, :], rstd[:, :].unsqueeze(2).broadcast_to([P, NT, D]),
                                                ALU.mult).then_inc(normed, 1)

                    @block.scalar
                    def _(act):
                        if layer == 1:
                            nc.scalar.activation(g_ffn[:, :, :], g_ffn[:, :, :], ACT.Silu).then_inc(silu_done, 1)
                        act.wait_ge(centered, 1)
                        nc.scalar.activation(sq[:, :, :], xn[:, :, :], ACT.Square).then_inc(squared, 1)
                        for q in range(4):
                            act.wait_ge(transposed, q + 1)
                            nc.scalar.activation(xnT[:, q * BANK:(q + 1) * BANK], tp[:, q, :], ACT.Copy).then_inc(act_done, 1)

                    @block.tensor
                    def _(pe):
                        pe.wait_ge(normed, 1)
                        if layer == 0:
                            pe.wait_ge(consts, 3)
                        for t in range(NT):
                            last = nc.tensor.transpose(tp[:, t // 4, (t % 4) * P:(t % 4 + 1) * P], xn[:, t, :], ident[:, :])
                            if t % 4 == 3:
                                last.then_inc(transposed, 1)

        def router_block(wroute, fw):
            with ExitStack() as c:
                sem = lambda n: c.enter_context(nc.semaphore(f"rt_{n}"))
                tri_ready, logits_ready, dve_seq, shifted, expd, p12, e2 = map(
                    sem, ("tri_ready", "logits_ready", "dve_seq", "shifted", "expd", "p12", "e2"))
                r = lambda n, s: sb(f"rt_{n}", s, c=c)
                z, pr = r("z", [P, NT, NE]), r("pr", [P, NT, NE])
                m, s = r("m", [P, NT]), r("s", [P, NT])
                g, q = r("g", [P, NT, NE, NE]), r("q", [P, NT, NE, NE])
                tri = r("tri", [P, NE, NE])
                rank, m1, m2 = r("rank", [P, NT, NE]), r("m1", [P, NT, NE]), r("m2", [P, NT, NE])
                pa, pb, w1, w2 = r("pa", [P, NT]), r("pb", [P, NT]), r("w1", [P, NT]), r("w2", [P, NT])
                lp = c.enter_context(nc.psum_tensor("rt_lp", [P, NT, NE], F32))
                bc = lambda v: v[:, :].unsqueeze(2).broadcast_to([P, NT, NE])
                with nc.Block() as block:
                    @block.tensor
                    def _(pe):
                        for t in range(NT):
                            last = nc.tensor.matmul(lp[:, t, :], xnT[:, t * P:(t + 1) * P], wroute[:, :], start=True, stop=True)
                        last.then_inc(logits_ready, 1)

                    @block.gpsimd
                    def _(pool):
                        nc.gpsimd.memset(tri[:, :, :], 1.0).then_inc(tri_ready, 1)
                        pool.wait_ge(tri_ready, 1)
                        nc.gpsimd.affine_select(out=tri[:, :, :], in_=tri[:, :, :], compare_op=ALU.is_gt, fill=0.0, base=0,
                                                pattern=[[1, NE], [-1, NE]], channel_multiplier=0).then_inc(tri_ready, 1)

                    @block.vector
                    def _(dve):
                        link = Chain(dve, dve_seq)
                        dve.wait_ge(logits_ready, 1)
                        link(nc.vector.tensor_reduce(m[:, :], lp[:, :, :], AX.X, ALU.max))
                        nc.vector.tensor_tensor(z[:, :, :], lp[:, :, :], bc(m), ALU.subtract).then_inc(shifted, 1)
                        dve.wait_ge(expd, 1)
                        link(nc.vector.tensor_reduce(s[:, :], pr[:, :, :], AX.X, ALU.add))
                        link(nc.vector.reciprocal(s[:, :], s[:, :]))
                        link(nc.vector.tensor_tensor(pr[:, :, :], pr[:, :, :], bc(s), ALU.mult))
                        pj = pr[:, :, :].unsqueeze(2).broadcast_to([P, NT, NE, NE])
                        pe_ = pr[:, :, :].unsqueeze(3).broadcast_to([P, NT, NE, NE])
                        link(nc.vector.tensor_tensor(g[:, :, :, :], pj, pe_, ALU.is_gt))
                        link(nc.vector.tensor_tensor(q[:, :, :, :], pj, pe_, ALU.is_equal))
                        dve.wait_ge(tri_ready, 2)
                        link(nc.vector.tensor_tensor(q[:, :, :, :], q[:, :, :, :],
                                                     tri[:, :, :].unsqueeze(1).broadcast_to([P, NT, NE, NE]), ALU.mult))
                        link(nc.vector.tensor_tensor(g[:, :, :, :], g[:, :, :, :], q[:, :, :, :], ALU.add))
                        link(nc.vector.tensor_reduce(rank[:, :, :], g[:, :, :, :], AX.X, ALU.add))
                        link(nc.vector.tensor_scalar(m1[:, :, :], rank[:, :, :], 0.0, None, ALU.is_equal))
                        link(nc.vector.tensor_scalar(m2[:, :, :], rank[:, :, :], 1.0, None, ALU.is_equal))
                        link(nc.vector.tensor_tensor(z[:, :, :], m1[:, :, :], pr[:, :, :], ALU.mult))
                        link(nc.vector.tensor_reduce(pa[:, :], z[:, :, :], AX.X, ALU.add))
                        link(nc.vector.tensor_tensor(z[:, :, :], m2[:, :, :], pr[:, :, :], ALU.mult))
                        link(nc.vector.tensor_reduce(pb[:, :], z[:, :, :], AX.X, ALU.add))
                        nc.vector.tensor_tensor(pb[:, :], pb[:, :], pa[:, :], ALU.subtract).then_inc(p12, 1)
                        dve.wait_ge(e2, 1)
                        link(nc.vector.tensor_scalar(w1[:, :], w2[:, :], 1.0, None, ALU.add))
                        link(nc.vector.reciprocal(w1[:, :], w1[:, :]))
                        link(nc.vector.tensor_tensor(w2[:, :], w2[:, :], w1[:, :], ALU.mult))
                        link(nc.vector.tensor_tensor(m1[:, :, :], m1[:, :, :], bc(w1), ALU.mult))
                        link(nc.vector.tensor_tensor(m2[:, :, :], m2[:, :, :], bc(w2), ALU.mult))
                        link(nc.vector.tensor_tensor(fw[:, :, :], m1[:, :, :], m2[:, :, :], ALU.add))

                    @block.scalar
                    def _(act):
                        act.wait_ge(shifted, 1)
                        nc.scalar.activation(pr[:, :, :], z[:, :, :], ACT.Exp).then_inc(expd, 1)
                        act.wait_ge(p12, 1)
                        nc.scalar.activation(w2[:, :], pb[:, :], ACT.Exp).then_inc(e2, 1)

        def attention0_block():
            with ExitStack() as c:
                sem = lambda n: c.enter_context(nc.semaphore(f"a0_{n}"))
                loaded, bvb_ready, folded, fold_out = map(sem, ("loaded", "bvb_ready", "folded", "fold_out"))
                xt_ready, xt_used = map(sem, ("xt_ready", "xt_used"))
                qg_ready, q_out, g_out, sc_ready, mx_ready, c_ready, t1_ready, nb_ready = map(
                    sem, ("qg_ready", "q_out", "g_out", "sc_ready", "mx_ready", "c_ready", "t1_ready", "nb_ready"))
                probs, rinv, pt_ready, pt_out, o_ready, o_out = map(
                    sem, ("probs", "rinv", "pt_ready", "pt_out", "o_ready", "o_out"))
                r = lambda n, s: sb(f"a0_{n}", s, c=c)
                wq, wk, wv, woT = (r(n, [P, 2, D]) for n in ("wq", "wk", "wv", "woT"))
                bo = r("bo", [P, D])
                bvb = r("bvb", [P, 2, P])
                bqb = r("bqb", [P, 2, P])
                Am, VO, bprime = r("Am", [P, D]), r("VO", [P, D]), r("bprime", [P, D])
                u, wc, bqbk = r("u", [P, 1]), r("wc", [P, 1]), r("bqbk", [P, 1])
                xt = r("xt", [P, 2, SEQ])
                qs, G, prob, pts = r("qs", [P, 2, SEQ]), r("G", [P, 2, TPB, D]), r("prob", [P, 2, TPB, SEQ]), r("pts", [P, 2, TPB, SEQ])
                mz, cs, t1, nb, rs, ri = (r(n, [P, 2, TPB]) for n in ("mz", "cs", "t1", "nb", "rs", "ri"))
                ps = c.enter_context(nc.psum_tensor("a0_ps", [P, 2, 4, BANK], F32))
                qp = lambda k: ps[:, k, 0, 0:SEQ]
                gp = lambda k: ps[:, k, 0, SEQ:2 * SEQ]
                sc = lambda k: ps[:, k, 1, :].rearrange("p (s t) -> p s t", s=TPB)
                pt = lambda k: ps[:, k, 2, :].rearrange("p (j s) -> p j s", j=TPB)
                op = lambda k: ps[:, k, 3, 0:TPB * D].rearrange("p (s o) -> p s o", s=TPB)
                cp = lambda k: ps[:, k, 3, TPB * D:TPB * D + TPB]
                with nc.Block() as block:
                    @block.sync
                    def _(sp):
                        for dst, name in ((wq, "wq"), (wk, "wk"), (wv, "wv"), (woT, "woT")):
                            sp.dma_start(dst[:, :, :], a[name].rearrange("(c p) d -> p c d", p=P)).then_inc(loaded, 16)
                        sp.dma_start(bo[:, :], a["bo"].broadcast_to([P, D])).then_inc(loaded, 16)

                    @block.gpsimd
                    def _(pool):
                        for cc in range(2):
                            nc.gpsimd.tensor_copy(bvb[:, cc, :], cols[:, COL["bv0"] + cc:COL["bv0"] + cc + 1].to_broadcast([P, P])).then_inc(bvb_ready, 1)
                            nc.gpsimd.tensor_copy(bqb[:, cc, :], cols[:, COL["bq0"] + cc:COL["bq0"] + cc + 1].to_broadcast([P, P])).then_inc(bvb_ready, 1)
                        with pool.Fori(0, BATCH // 2) as i:
                            for k in range(2):
                                pool.wait_ge(xt_used, 2 * i + k + 1)
                                nc.gpsimd.tensor_copy(xt[:, k, :], xnT[:, bass.ds((2 * i + k) * SEQ, SEQ)]).then_inc(xt_ready, 1)

                    @block.tensor
                    def _(pe):
                        pe.sem_inc(xt_used, 2)
                        pe.wait_ge(loaded, 80)
                        pe.wait_ge(bvb_ready, 4)
                        for n in range(2):
                            f = dict(start=n == 0, stop=n == 1)
                            nc.tensor.matmul(ps[:, 0, 0, 0:D], wq[:, n, :], wk[:, n, :], **f)
                        for n in range(2):
                            f = dict(start=n == 0, stop=n == 1)
                            nc.tensor.matmul(ps[:, 0, 1, 0:D], wv[:, n, :], woT[:, n, :], **f)
                        for n in range(2):
                            f = dict(start=n == 0, stop=n == 1)
                            nc.tensor.matmul(ps[:, 0, 2, 0:1], wk[:, n, :], cols[:, COL["bq0"] + n:COL["bq0"] + n + 1], **f)
                        for n in range(2):
                            f = dict(start=n == 0, stop=n == 1)
                            nc.tensor.matmul(ps[:, 0, 3, 0:1], wq[:, n, :], cols[:, COL["bk0"] + n:COL["bk0"] + n + 1], **f)
                        for n in range(2):
                            f = dict(start=n == 0, stop=n == 1)
                            nc.tensor.matmul(ps[:, 1, 0, 0:1], bqb[:, n, :], cols[:, COL["bk0"] + n:COL["bk0"] + n + 1], **f)
                        for n in range(2):
                            f = dict(start=n == 0, stop=n == 1)
                            last = nc.tensor.matmul(ps[:, 1, 1, 0:D], bvb[:, n, :], woT[:, n, :], **f)
                        last.then_inc(folded, 1)
                        pe.wait_ge(fold_out, 6)
                        with pe.Fori(0, BATCH // 2) as i:
                            for k in range(2):
                                b = 2 * i + k
                                pe.wait_ge(xt_ready, b + 1)
                                pe.wait_ge(g_out, b + 1)
                                pe.wait_ge(o_out, b + 1)
                                nc.tensor.matmul(qp(k), Am[:, :], xt[:, k, :], start=True, stop=True)
                                for s in range(TPB):
                                    nc.tensor.matmul(gp(k)[:, s * D:(s + 1) * D], xt[:, k, s * P:(s + 1) * P], VO[:, :], start=True, stop=True)
                                for s in range(TPB):
                                    last = nc.tensor.matmul(cp(k)[:, s:s + 1], xt[:, k, s * P:(s + 1) * P], wc[:, :], start=True, stop=True)
                                last.then_inc(qg_ready, 1)
                            for k in range(2):
                                b = 2 * i + k
                                pe.wait_ge(q_out, b + 1)
                                for s in range(TPB):
                                    last = nc.tensor.matmul(sc(k)[:, s, :], qs[:, k, s * P:(s + 1) * P], xt[:, k, :], start=True, stop=True)
                                last.then_inc(sc_ready, 1)
                            for k in range(2):
                                b = 2 * i + k
                                pe.wait_ge(probs, 2 * b + 2)
                                for s in range(TPB):
                                    for j in range(TPB):
                                        last = nc.tensor.transpose(pt(k)[:, j, s * P:(s + 1) * P], prob[:, k, s, j * P:(j + 1) * P], ident[:, :])
                                last.then_inc(pt_ready, 1)
                            for k in range(2):
                                b = 2 * i + k
                                pe.wait_ge(pt_out, b + 1)
                                for s in range(TPB):
                                    for j in range(TPB):
                                        last = nc.tensor.matmul(op(k)[:, s, :], pts[:, k, j, s * P:(s + 1) * P], G[:, k, j, :], start=j == 0, stop=j == TPB - 1)
                                last.then_inc(o_ready, 1)

                    @block.scalar
                    def _(act):
                        act.wait_ge(folded, 1)
                        nc.scalar.activation(Am[:, :], ps[:, 0, 0, 0:D], ACT.Copy).then_inc(fold_out, 1)
                        nc.scalar.activation(VO[:, :], ps[:, 0, 1, 0:D], ACT.Copy).then_inc(fold_out, 1)
                        nc.scalar.activation(u[:, :], ps[:, 0, 2, 0:1], ACT.Copy).then_inc(fold_out, 1)
                        nc.scalar.activation(wc[:, :], ps[:, 0, 3, 0:1], ACT.Copy, scale=SCALE0).then_inc(fold_out, 1)
                        nc.scalar.activation(bqbk[:, :], ps[:, 1, 0, 0:1], ACT.Copy, scale=SCALE0).then_inc(fold_out, 1)
                        act.sem_inc(g_out, 2)
                        act.wait_ge(fold_out, 6)
                        nc.scalar.preload_act_table(ACT.Exp)
                        with act.Fori(0, BATCH // 2) as i:
                            for k in range(2):
                                b = 2 * i + k
                                act.wait_ge(qg_ready, b + 1)
                                nc.scalar.activation(qs[:, k, :], qp(k), ACT.Identity, bias=u[:, 0:1]).then_inc(q_out, 1)
                                nc.scalar.activation(G[:, k, :, :].rearrange("p j o -> p (j o)"), gp(k), ACT.Copy).then_inc(g_out, 1)
                            for k in range(2):
                                b = 2 * i + k
                                act.wait_ge(nb_ready, b + 1)
                                for s in range(TPB):
                                    nc.scalar.activation(prob[:, k, s, :], sc(k)[:, s, :], ACT.Exp, bias=nb[:, k, s:s + 1], scale=SCALE0,
                                                         accum_out=rs[:, k, s:s + 1]).then_inc(probs, 1)
                            for k in range(2):
                                b = 2 * i + k
                                act.wait_ge(pt_ready, b + 1)
                                nc.scalar.activation(pts[:, k, :, :], pt(k), ACT.Copy).then_inc(pt_out, 1)

                    @block.vector
                    def _(dve):
                        dve.wait_ge(folded, 1)
                        dve.wait_ge(loaded, 80)
                        nc.vector.tensor_tensor(bprime[:, :], ps[:, 1, 1, 0:D], bo[:, :], ALU.add).then_inc(fold_out, 1)
                        dve.sem_inc(o_out, 2)
                        dve.wait_ge(fold_out, 6)
                        with dve.Fori(0, BATCH // 2) as i:
                            for k in range(2):
                                b = 2 * i + k
                                dve.wait_ge(qg_ready, b + 1)
                                nc.vector.tensor_scalar(cs[:, k, :], cp(k), bqbk[:, 0:1], None, ALU.add).then_inc(c_ready, 1)
                                dve.wait_ge(sc_ready, b + 1)
                                nc.vector.tensor_reduce(mz[:, k, :], sc(k), AX.X, ALU.max).then_inc(mx_ready, 1)
                                dve.wait_ge(mx_ready, b + 1)
                                dve.wait_ge(c_ready, b + 1)
                                nc.vector.scalar_tensor_tensor(t1[:, k, :], mz[:, k, :], SCALE0, cs[:, k, :], ALU.mult, ALU.add).then_inc(t1_ready, 1)
                                dve.wait_ge(t1_ready, b + 1)
                                nc.vector.tensor_tensor(nb[:, k, :], cs[:, k, :], t1[:, k, :], ALU.subtract).then_inc(nb_ready, 1)
                            for k in range(2):
                                b = 2 * i + k
                                dve.wait_ge(probs, 2 * b + 2)
                                nc.vector.reciprocal(ri[:, k, :], rs[:, k, :]).then_inc(rinv, 1)
                                dve.wait_ge(rinv, b + 1)
                                dve.wait_ge(o_ready, b + 1)
                                for s in range(TPB):
                                    last = nc.vector.scalar_tensor_tensor(s_att[:, bass.ds(TPB * b + s, 1), :].squeeze(1), op(k)[:, s, :], ri[:, k, s:s + 1], bprime[:, :],
                                                                          ALU.mult, ALU.add)
                                last.then_inc(o_out, 1)
                            dve.sem_inc(xt_used, 2)

        def experts0_block(fw, wgu, wd):
            with ExitStack() as c:
                sem = lambda n: c.enter_context(nc.semaphore(f"e0_{n}"))
                xt_ready, xt_used, gu_ready, sg_ready, fu_ready, ft_ready, ft_out, y_ready, y_out = map(
                    sem, ("xt_ready", "xt_used", "gu_ready", "sg_ready", "fu_ready", "ft_ready", "ft_out", "y_ready", "y_out"))
                r = lambda n, s: sb(f"e0_{n}", s, c=c)
                xt, sg, fu, ft = r("xt", [P, 2, P]), r("sg", [P, 2, FF]), r("fu", [P, 2, FF]), r("ft", [P, 2, FF])
                gu = c.enter_context(nc.psum_tensor("e0_gu", [P, 2, 2 * FF], F32))
                tp = c.enter_context(nc.psum_tensor("e0_tp", [P, 2, BANK], F32))
                yp = c.enter_context(nc.psum_tensor("e0_yp", [P, 2, BANK], F32))
                with nc.Block() as block:
                    @block.gpsimd
                    def _(pool):
                        with pool.Fori(0, NT // 2) as i:
                            for k in range(2):
                                pool.wait_ge(xt_used, 2 * i + k + 1)
                                nc.gpsimd.tensor_copy(xt[:, k, :], xnT[:, bass.ds((2 * i + k) * P, P)]).then_inc(xt_ready, 1)

                    @block.tensor
                    def _(pe):
                        with pe.Fori(0, NT // 2) as i:
                            for k in range(2):
                                t = 2 * i + k
                                pe.wait_ge(xt_ready, t + 1)
                                pe.wait_ge(y_out, t + 1)

                                def gate_up(e):
                                    pe.wait_ge(fu_ready, NE * t + e + 1)
                                    nc.tensor.matmul(gu[:, e % 2, :], xt[:, k, :], wgu[:, e, :], start=True, stop=True).then_inc(gu_ready, 1)

                                def flip(e):
                                    pe.wait_ge(fu_ready, NE * t + e + 3)
                                    pe.wait_ge(ft_out, NE * t + e + 1)
                                    for f in range(2):
                                        last = nc.tensor.transpose(tp[:, e % 2, f * P:(f + 1) * P], fu[:, e % 2, f * P:(f + 1) * P], ident[:, :])
                                    last.then_inc(ft_ready, 1)

                                def down(e):
                                    pe.wait_ge(ft_out, NE * t + e + 3)
                                    for f in range(2):
                                        last = nc.tensor.matmul(yp[:, k, 0:D], ft[:, e % 2, f * P:(f + 1) * P], wd[:, e, f, :],
                                                                start=e == 0 and f == 0, stop=e == NE - 1 and f == 1)
                                    return last

                                gate_up(0)
                                for e in range(NE):
                                    if e + 1 < NE:
                                        gate_up(e + 1)
                                    flip(e)
                                    last = down(e)
                                last.then_inc(y_ready, 1)

                    @block.scalar
                    def _(act):
                        act.sem_inc(ft_out, 2)
                        nc.scalar.preload_act_table(ACT.Silu)
                        with act.Fori(0, NT // 2) as i:
                            for k in range(2):
                                t = 2 * i + k
                                for e in range(NE):
                                    act.wait_ge(gu_ready, NE * t + e + 1)
                                    nc.scalar.activation(sg[:, e % 2, :], gu[:, e % 2, 0:FF], ACT.Silu).then_inc(sg_ready, 1)
                                    act.wait_ge(ft_ready, NE * t + e + 1)
                                    nc.scalar.activation(ft[:, e % 2, :], tp[:, e % 2, 0:FF], ACT.Copy).then_inc(ft_out, 1)

                    @block.vector
                    def _(dve):
                        dve.sem_inc(fu_ready, 2)
                        dve.sem_inc(y_out, 2)
                        dve.sem_inc(xt_used, 2)
                        with dve.Fori(0, NT // 2) as i:
                            for k in range(2):
                                t = 2 * i + k
                                for e in range(NE):
                                    dve.wait_ge(sg_ready, NE * t + e + 1)
                                    dve.wait_ge(ft_ready, NE * t + e - 1) if e >= 2 else None
                                    nc.vector.scalar_tensor_tensor(fu[:, e % 2, :], sg[:, e % 2, :], fw[:, bass.ds(t, 1), e:e + 1].squeeze(1),
                                                                   gu[:, e % 2, FF:2 * FF], ALU.mult, ALU.mult).then_inc(fu_ready, 1)
                                dve.wait_ge(y_ready, t + 1)
                                nc.vector.tensor_copy(g_ffn[:, bass.ds(t, 1), :].squeeze(1), yp[:, k, 0:D]).then_inc(y_out, 1)
                                dve.sem_inc(xt_used, 1)

        def attention1_block():
            qkv_d = nc.dram_tensor("a1_qkv_d", [3, HEADS, HD, BATCH, SEQ], F32, kind="Internal").ap()
            att_d = nc.dram_tensor("a1_att_d", [BATCH, HEADS, HD, SEQ], F32, kind="Internal").ap()
            with ExitStack() as c:
                r = lambda n, s: sb(f"a1_{n}", s, c=c)
                gate = r("gate", [P, TOK])
                wout = r("wout", [P, D])
                b_out = r("bout", [P, D])
                q, kk, v = r("q", [P, HD, SEQ]), r("k", [P, HD, SEQ]), r("v", [P, HD, SEQ])
                with ExitStack() as c1:
                    r1 = lambda n, s: sb(f"a1_{n}", s, c=c1)
                    sem = lambda n: c1.enter_context(nc.semaphore(f"a1_{n}"))
                    loaded, scaled, mm_ready, evac, stored, back = map(sem, ("loaded", "scaled", "mm_ready", "evac", "stored", "back"))
                    wqkv, wgate = r1("wqkv", [P, 3, P]), r1("wgate", [P, D])
                    bqs = r1("bqs", [P, 1])
                    qkvT = r1("qkvT", [P, 3, TOK])
                    pp = c1.enter_context(nc.psum_tensor("a1_pp", [P, 8, BANK], F32))
                    with nc.Block() as block:
                        @block.sync
                        def _(sp):
                            sp.dma_start(wqkv[:, :, :], a["w_qkv"].rearrange("d (j c) -> d j c", j=3)).then_inc(loaded, 16)
                            sp.dma_start(wgate[:, :], a["w_gate"]).then_inc(loaded, 16)
                            sp.dma_start(wout[:, :], a["w_out"]).then_inc(loaded, 16)
                            sp.dma_start(b_out[:, :], a["b_out"].broadcast_to([P, D])).then_inc(loaded, 16)
                            sp.wait_ge(evac, 16)
                            sp.dma_start(qkv_d.rearrange("j h d b n -> (h d) j (b n)"), qkvT[:, :, :]).then_inc(stored, 16)
                            sp.wait_ge(stored, 16)
                            for j, dst in enumerate((q, kk, v)):
                                for b in range(BATCH):
                                    sp.dma_start(dst[b * HEADS:(b + 1) * HEADS, :, :], qkv_d[j, :, :, b, :]).then_inc(back, 16)
                            sp.wait_ge(back, 16 * 24)

                        @block.vector
                        def _(dve):
                            nc.vector.tensor_scalar(bqs[:, :], cols[:, COL["b1q"]:COL["b1q"] + 1], SCALE1, None, ALU.mult).then_inc(scaled, 1)

                        @block.tensor
                        def _(pe):
                            pe.wait_ge(loaded, 64)
                            for n in range(TOK // BANK):
                                if n >= 2:
                                    pe.wait_ge(evac, 4 * (n - 1))
                                for j in range(4):
                                    w = wqkv[:, j, :] if j < 3 else wgate[:, :]
                                    nc.tensor.matmul(pp[:, 4 * (n % 2) + j, :], w, xnT[:, n * BANK:(n + 1) * BANK], start=True, stop=True).then_inc(mm_ready, 1)

                        @block.scalar
                        def _(act):
                            act.wait_ge(scaled, 1)
                            for n in range(TOK // BANK):
                                sl = slice(n * BANK, (n + 1) * BANK)
                                for j in range(4):
                                    act.wait_ge(mm_ready, 4 * n + j + 1)
                                    src = pp[:, 4 * (n % 2) + j, :]
                                    if j == 0:
                                        ins = nc.scalar.activation(qkvT[:, 0, sl], src, ACT.Identity, bias=bqs[:, 0:1], scale=SCALE1)
                                    elif j < 3:
                                        cc = COL["b1q"] + j
                                        ins = nc.scalar.activation(qkvT[:, j, sl], src, ACT.Identity, bias=cols[:, cc:cc + 1])
                                    else:
                                        ins = nc.scalar.activation(gate[:, sl], src, ACT.Sigmoid, bias=cols[:, COL["bgate"]:COL["bgate"] + 1])
                                    ins.then_inc(evac, 1)
                with ExitStack() as c2:
                    r2 = lambda n, s: sb(f"a1_{n}", s, c=c2)
                    sem = lambda n: c2.enter_context(nc.semaphore(f"a1b_{n}"))
                    loaded, zeroed, dve_seq, wexp, shifted, expd, stored, back, gated, pr_ready, att_ready = map(
                        sem, ("loaded", "zeroed", "dve_seq", "wexp", "shifted", "expd", "stored", "back", "gated", "pr_ready", "att_ready"))
                    pb, wb = r2("pb", [P, len(BIAS_ORDER)]), r2("wb", [P, len(BIAS_ORDER)])
                    mb, W = r2("mb", [P, NS]), r2("W", [P, NS])
                    prod = r2("prod", [P, HD, SEQ])
                    sc = r2("sc", [P, NS, SEQ])
                    m, den = r2("m", [P, SEQ]), r2("den", [P, SEQ])
                    acc = r2("acc", [P, HD, SEQ])
                    attT = r2("attT", [P, BATCH, SEQ])
                    pp = c2.enter_context(nc.psum_tensor("a1b_pp", [P, 4, 4, D], F32))
                    over_n = lambda x: x[:, :].unsqueeze(2).broadcast_to([P, NS, SEQ])
                    over_s = lambda x: x[:, :].unsqueeze(1).broadcast_to([P, NS, SEQ])
                    with nc.Block() as block:
                        @block.sync
                        def _(sp):
                            sp.dma_start(pb[:, :], a["pos_bias"]).then_inc(loaded, 16)
                            sp.wait_ge(att_ready, 1)
                            for_store = att_d.rearrange("b h d n -> (b h) d n")
                            sp.dma_start(for_store, acc[:, :, :]).then_inc(stored, 16)
                            sp.wait_ge(stored, 16)
                            for b in range(BATCH):
                                sp.dma_start(attT[:, b, :], att_d[b].rearrange("h d n -> (h d) n")).then_inc(back, 16)
                            sp.wait_ge(back, 16 * BATCH)

                        @block.gpsimd
                        def _(pool):
                            nc.gpsimd.memset(sc[:, :, :], 0.0).then_inc(zeroed, 1)

                        @block.scalar
                        def _(act):
                            act.wait_ge(shifted, 1)
                            nc.scalar.activation(wb[:, :], wb[:, :], ACT.Exp).then_inc(wexp, 1)
                            act.wait_ge(shifted, 2)
                            nc.scalar.activation(sc[:, :, :], sc[:, :, :], ACT.Exp).then_inc(expd, 1)

                        @block.vector
                        def _(dve):
                            link = Chain(dve, dve_seq)
                            dve.wait_ge(loaded, 16)
                            for s in range(NS):
                                i0, n = BIAS_START[s], len(MEMBERS[s])
                                last = nc.vector.tensor_reduce(mb[:, s:s + 1], pb[:, i0:i0 + n], AX.X, ALU.max)
                            link(last)
                            for s in range(NS):
                                i0, n = BIAS_START[s], len(MEMBERS[s])
                                last = nc.vector.tensor_scalar(wb[:, i0:i0 + n], pb[:, i0:i0 + n], mb[:, s:s + 1], None, ALU.subtract)
                            last.then_inc(shifted, 1)
                            dve.wait_ge(wexp, 1)
                            for s in range(NS):
                                i0, n = BIAS_START[s], len(MEMBERS[s])
                                last = nc.vector.tensor_reduce(W[:, s:s + 1], wb[:, i0:i0 + n], AX.X, ALU.add)
                            link(last)
                            dve.wait_ge(zeroed, 1)
                            for s, off in enumerate(OFFS):
                                w = SEQ - off
                                link(nc.vector.tensor_tensor(prod[:, :, 0:w], q[:, :, off:SEQ], kk[:, :, 0:w], ALU.mult))
                                link(nc.vector.tensor_reduce(sc[:, s, off:SEQ], prod[:, :, 0:w].rearrange("p d n -> p n d"), AX.X, ALU.add))
                            link(nc.vector.tensor_tensor(sc[:, :, :], sc[:, :, :], over_n(mb), ALU.add))
                            link(nc.vector.tensor_reduce(m[:, :], sc[:, :, :].rearrange("p s n -> p n s"), AX.X, ALU.max))
                            nc.vector.tensor_tensor(sc[:, :, :], sc[:, :, :], over_s(m), ALU.subtract).then_inc(shifted, 1)
                            dve.wait_ge(expd, 1)
                            link(nc.vector.tensor_tensor(sc[:, :, :], sc[:, :, :], over_n(W), ALU.mult))
                            link(nc.vector.tensor_reduce(den[:, :], sc[:, :, :].rearrange("p s n -> p n s"), AX.X, ALU.add))
                            link(nc.vector.reciprocal(den[:, :], den[:, :]))
                            for s, off in enumerate(OFFS):
                                w = SEQ - off
                                at = sc[:, s, off:SEQ].unsqueeze(1).broadcast_to([P, HD, w])
                                if s == 0:
                                    link(nc.vector.tensor_tensor(acc[:, :, :], at, v[:, :, :], ALU.mult))
                                else:
                                    link(nc.vector.tensor_tensor(prod[:, :, 0:w], at, v[:, :, 0:w], ALU.mult))
                                    link(nc.vector.tensor_tensor(acc[:, :, off:SEQ], acc[:, :, off:SEQ], prod[:, :, 0:w], ALU.add))
                            nc.vector.tensor_tensor(acc[:, :, :], acc[:, :, :], den[:, :].unsqueeze(1).broadcast_to([P, HD, SEQ]), ALU.mult).then_inc(att_ready, 1)
                            dve.wait_ge(back, 16 * BATCH)
                            nc.vector.tensor_tensor(attT[:, :, :], attT[:, :, :], gate[:, :].rearrange("p (b n) -> p b n", b=BATCH), ALU.mult).then_inc(gated, 1)
                            for t in range(4):
                                dve.wait_ge(pr_ready, t + 1)
                                nc.vector.tensor_tensor(s_att[:, 4 * t:4 * t + 4, :], pp[:, t, :, :], b_out[:, :].unsqueeze(1).broadcast_to([P, 4, D]), ALU.add)

                        @block.tensor
                        def _(pe):
                            pe.wait_ge(gated, 1)
                            flat = attT[:, :, :].rearrange("p b n -> p (b n)")
                            for t in range(NT):
                                last = nc.tensor.matmul(pp[:, t // 4, t % 4, :], flat[:, t * P:(t + 1) * P], wout[:, :], start=True, stop=True)
                                if t % 4 == 3:
                                    last.then_inc(pr_ready, 1)

        def soft_dispatch_block(L, slots_p, phiT, phib):
            with ExitStack() as c:
                sem = lambda n: c.enter_context(nc.semaphore(f"d_{n}"))
                xt_ready, xt_used, lg_ready, l_out, mx, zs, ex, sm, si, dn, acc_done = map(
                    sem, ("xt_ready", "xt_used", "lg_ready", "l_out", "mx", "zs", "ex", "sm", "si", "dn", "acc_done"))
                r = lambda n, s: sb(f"d_{n}", s, c=c)
                xt = r("xt", [P, 2, P])
                Z = r("Z", [P, 2, NX, SLOTS])
                am, ss, sr = r("am", [P, 2, NX]), r("ss", [P, 2, NX]), r("sr", [P, 2, NX])
                ones, zero = phib["ones"], phib["zero"]
                lg = c.enter_context(nc.psum_tensor("d_lg", [P, 4, BANK], F32))
                over_p = lambda x, k: x[:, k, :].unsqueeze(2).broadcast_to([P, NX, SLOTS])
                with nc.Block() as block:
                    @block.gpsimd
                    def _(pool):
                        with pool.Fori(0, NT // 2) as i:
                            for k in range(2):
                                t = 2 * i + k
                                pool.wait_ge(xt_used, t + 1)
                                nc.gpsimd.tensor_copy(xt[:, k, :], xnT[:, bass.ds(t * P, P)]).then_inc(xt_ready, 1)

                    @block.tensor
                    def _(pe):
                        for n in range(4):
                            nc.tensor.matmul(slots_p[:, n, :], zero[:, 0:P], zero[:, :], start=True, stop=True, skip_group_check=True)

                        def logits(t, k):
                            pe.wait_ge(xt_ready, t + 1)
                            for n in range(4):
                                pe.wait_ge(l_out, 4 * t + n + 1)
                                nc.tensor.matmul(lg[:, n, :], xt[:, k, :], phiT[:, n * BANK:(n + 1) * BANK], start=True, stop=False)
                                nc.tensor.matmul(lg[:, n, :], ones[:, :], phib["rows"][:, n * BANK:(n + 1) * BANK], start=False, stop=True).then_inc(lg_ready, 1)

                        def slot_inputs(t, k):
                            pe.wait_ge(dn, t + 1)
                            Zf = Z[:, k, :, :].rearrange("p n s -> p (n s)")
                            for j in range(NPT):
                                last = nc.tensor.matmul(slots_p[:, j // 4, (j % 4) * D:(j % 4 + 1) * D], Zf[:, j * P:(j + 1) * P],
                                                        xn[:, bass.ds(t, 1), :].squeeze(1) if not isinstance(t, int) else xn[:, t, :],
                                                        start=False, stop=True, skip_group_check=True)
                            last.then_inc(xt_used, 1)

                        logits(0, 0)
                        with pe.Fori(0, NT // 2 - 1) as i:
                            logits(2 * i + 1, 1)
                            slot_inputs(2 * i, 0)
                            logits(2 * i + 2, 0)
                            slot_inputs(2 * i + 1, 1)
                        logits(NT - 1, 1)
                        slot_inputs(NT - 2, 0)
                        slot_inputs(NT - 1, 1)

                    @block.scalar
                    def _(act):
                        act.sem_inc(l_out, 4)
                        nc.scalar.preload_act_table(ACT.Exp)

                        def copy_out(t, n):
                            act.wait_ge(lg_ready, 4 * t + n + 1)
                            dst = L[:, bass.ds(t, 1), n * BANK:(n + 1) * BANK].squeeze(1) if not isinstance(t, int) else L[:, t, n * BANK:(n + 1) * BANK]
                            nc.scalar.activation(dst, lg[:, n, :], ACT.Copy).then_inc(l_out, 1)

                        def expo(t, k):
                            act.wait_ge(zs, t + 1)
                            nc.scalar.activation(Z[:, k, :, :], Z[:, k, :, :], ACT.Exp).then_inc(ex, 1)

                        for n in range(4):
                            copy_out(0, n)
                        with act.Fori(0, NT // 2 - 1) as i:
                            for k in range(2):
                                for n in range(4):
                                    copy_out(2 * i + k + 1, n)
                                expo(2 * i + k, k)
                        for n in range(4):
                            copy_out(NT - 1, n)
                        expo(NT - 2, 0)
                        expo(NT - 1, 1)

                    @block.vector
                    def _(dve):
                        dve.sem_inc(xt_used, 2)

                        def front(t, k):
                            dve.wait_ge(l_out, 4 * t + 8)
                            Lt = (L[:, bass.ds(t, 1), :].squeeze(1) if not isinstance(t, int) else L[:, t, :]).rearrange("p (n s) -> p n s", s=SLOTS)
                            nc.vector.tensor_reduce(am[:, k, :], Lt, AX.X, ALU.max).then_inc(mx, 1)
                            dve.wait_ge(mx, t + 1)
                            dve.wait_ge(xt_used, t + 1)
                            nc.vector.tensor_tensor(Z[:, k, :, :], Lt, over_p(am, k), ALU.subtract).then_inc(zs, 1)

                        def back(t, k):
                            dve.wait_ge(ex, t + 1)
                            nc.vector.tensor_reduce(ss[:, k, :], Z[:, k, :, :], AX.X, ALU.add).then_inc(sm, 1)
                            dve.wait_ge(sm, t + 1)
                            nc.vector.reciprocal(sr[:, k, :], ss[:, k, :]).then_inc(si, 1)
                            dve.wait_ge(si, t + 1)
                            nc.vector.tensor_tensor(Z[:, k, :, :], Z[:, k, :, :], over_p(sr, k), ALU.mult).then_inc(dn, 1)

                        front(0, 0)
                        with dve.Fori(0, NT // 2 - 1) as i:
                            front(2 * i + 1, 1)
                            back(2 * i, 0)
                            front(2 * i + 2, 0)
                            back(2 * i + 1, 1)
                        front(NT - 1, 1)
                        back(NT - 2, 0)
                        back(NT - 1, 1)

        def slot_experts_block(slots_p, Y):
            with ExitStack() as c:
                sem = lambda n: c.enter_context(nc.semaphore(f"s_{n}"))
                loaded, dve_seq, cen, sqd, var_ready, rstd_ready, nrm, th, tr, ev, half_ready, y_ready, y_out = map(
                    sem, ("loaded", "dve_seq", "cen", "sqd", "var_ready", "rstd_ready", "nrm", "th", "tr", "ev", "half_ready", "y_ready", "y_out"))
                r = lambda n, s: sb(f"s_{n}", s, c=c)
                X, XT = xn, g_ffn
                sq = XT
                ew = r("ew", [P, NX, HOUT])
                mean, var, rstd, half = r("mean", [P, NPT]), r("var", [P, NPT]), r("rstd", [P, NPT]), r("half", [P, 1])
                yp = c.enter_context(nc.psum_tensor("s_yp", [P, 4, BANK], F32))
                over = lambda x: x[:, :].unsqueeze(2).broadcast_to([P, NPT, D])
                with nc.Block() as block:
                    @block.sync
                    def _(sp):
                        sp.dma_start(ew[:, :, :], a["expert_w"].rearrange("n d h -> d n h")).then_inc(loaded, 16)
                        for g in range(XPT):
                            sp.dma_start(Y[g * SLOTS:(g + 1) * SLOTS, :, :],
                                        
                                         a["expert_b"].rearrange("(j g) h -> g j h", g=XPT)[g:g + 1].broadcast_to([SLOTS, NPT, HOUT])).then_inc(loaded, 16)

                    @block.gpsimd
                    def _(pool):
                        nc.gpsimd.memset(half[:, :], -0.5).then_inc(half_ready, 1)
                        pool.wait_ge(half_ready, 1)
                        pool.wait_ge(var_ready, 1)
                        nc.gpsimd.tensor_tensor(rstd[:, :], var[:, :], half[:, 0:1].to_broadcast([P, NPT]), ALU.pow).then_inc(rstd_ready, 1)

                    @block.vector
                    def _(dve):
                        link = Chain(dve, dve_seq)
                        link(nc.vector.tensor_scalar(X[:, :, :].rearrange("p t d -> p (t d)"), slots_p[:, :, :].rearrange("p a b -> p (a b)"),
                                                     -33000.0, 65000.0, ALU.max, ALU.min))
                        link(nc.vector.tensor_reduce(mean[:, :], X[:, :, :], AX.X, ALU.add))
                        link(nc.vector.tensor_scalar(mean[:, :], mean[:, :], 1.0 / D, None, ALU.mult))
                        nc.vector.tensor_tensor(X[:, :, :], X[:, :, :], over(mean), ALU.subtract).then_inc(cen, 1)
                        dve.wait_ge(sqd, 1)
                        link(nc.vector.tensor_reduce(var[:, :], sq[:, :, :], AX.X, ALU.add))
                        nc.vector.tensor_scalar(var[:, :], var[:, :], 1.0 / D, EPS, ALU.mult, ALU.add).then_inc(var_ready, 1)
                        dve.wait_ge(rstd_ready, 1)
                        nc.vector.tensor_tensor(X[:, :, :], X[:, :, :], over(rstd), ALU.mult).then_inc(nrm, 1)
                        dve.wait_ge(loaded, 16 * (1 + XPT))
                        for q in range(4):
                            dve.wait_ge(y_ready, q + 1)
                            nc.vector.tensor_tensor(Y[:, 4 * q:4 * q + 4, :].rearrange("p t d -> p (t d)"), yp[:, q, :],
                                                    Y[:, 4 * q:4 * q + 4, :].rearrange("p t d -> p (t d)"), ALU.add)

                    @block.scalar
                    def _(act):
                        act.wait_ge(cen, 1)
                        nc.scalar.activation(sq[:, :, :], X[:, :, :], ACT.Square).then_inc(sqd, 1)
                        act.wait_ge(nrm, 1)
                        nc.scalar.activation(X[:, :, :], X[:, :, :], ACT.Tanh).then_inc(th, 1)
                        for q in range(4):
                            act.wait_ge(tr, q + 1)
                            nc.scalar.activation(XT[:, 4 * q:4 * q + 4, :].rearrange("p t d -> p (t d)"), yp[:, q, :], ACT.Copy).then_inc(ev, 1)

                    @block.tensor
                    def _(pe):
                        pe.wait_ge(th, 1)
                        for j in range(NPT):
                            last = nc.tensor.transpose(yp[:, j // 4, (j % 4) * P:(j % 4 + 1) * P], X[:, j, :], ident[:, :])
                            if j % 4 == 3:
                                last.then_inc(tr, 1)
                        pe.wait_ge(loaded, 16 * (1 + XPT))
                        for j in range(NPT):
                            if j % 4 == 0:
                                pe.wait_ge(ev, j // 4 + 1)
                            for g in range(XPT):
                                last = nc.tensor.matmul(yp[g * SLOTS:(g + 1) * SLOTS, j // 4, (j % 4) * HOUT:(j % 4 + 1) * HOUT],
                                                        XT[:, j, g * SLOTS:(g + 1) * SLOTS], ew[:, XPT * j + g, :], start=True, stop=True,
                                                        tile_position=(0, g * SLOTS))
                            if j % 4 == 3:
                                last.then_inc(y_ready, 1)

        def soft_combine_block(L, Y):
            with ExitStack() as c:
                sem = lambda n: c.enter_context(nc.semaphore(f"c_{n}"))
                mx, zs, ex, sm, si, rr, rt_ready, rt_out, tr, ct, y_ready, y_out, silu, fin, fin2, stored = map(
                    sem, ("mx", "zs", "ex", "sm", "si", "rr", "rt_ready", "rt_out", "tr", "ct", "y_ready", "y_out", "silu", "fin", "fin2", "stored"))
                r = lambda n, s: sb(f"c_{n}", s, c=c)
                EC = r("EC", [P, 2, NP])
                bm, rs, ri, rep, RT = r("bm", [P, 2, SLOTS]), r("rs", [P, 2, SLOTS]), r("ri", [P, 2, SLOTS]), r("rep", [P, 2, P]), r("RT", [P, 2, P])
                CT = r("CT", [P, NPT, P])
                tp = c.enter_context(nc.psum_tensor("c_tp", [P, 4, BANK], F32))
                rp = c.enter_context(nc.psum_tensor("c_rp", [P, 2, BANK], F32))
                yp = c.enter_context(nc.psum_tensor("c_yp", [P, 2, BANK], F32))
                with nc.Block() as block:
                    @block.gpsimd
                    def _(pool):
                        with pool.Fori(0, NT // 2) as i:
                            for k in range(2):
                                t = 2 * i + k
                                pool.wait_ge(mx, t + 1)
                                Lt = L[:, bass.ds(t, 1), :].squeeze(1).rearrange("p (n s) -> p n s", s=SLOTS)
                                nc.gpsimd.tensor_tensor(Lt, Lt, bm[:, k, :].unsqueeze(1).broadcast_to([P, NX, SLOTS]), ALU.subtract).then_inc(zs, 1)

                    @block.scalar
                    def _(act):
                        nc.scalar.preload_act_table(ACT.Exp)
                        with act.Fori(0, NT // 2) as i:
                            for k in range(2):
                                t = 2 * i + k
                                act.wait_ge(zs, t + 1)
                                act.wait_ge(tr, 4 * t + 1)
                                nc.scalar.activation(EC[:, k, :], L[:, bass.ds(t, 1), :].squeeze(1), ACT.Exp).then_inc(ex, 1)
                                act.wait_ge(rt_ready, t + 1)
                                nc.scalar.activation(RT[:, k, :], rp[:, k, 0:P], ACT.Copy).then_inc(rt_out, 1)

                    @block.vector
                    def _(dve):
                        def front(t, k):
                            Lt = (L[:, bass.ds(t, 1), :].squeeze(1) if not isinstance(t, int) else L[:, t, :]).rearrange("p (n s) -> p s n", s=SLOTS)
                            nc.vector.tensor_reduce(bm[:, k, :], Lt, AX.X, ALU.max).then_inc(mx, 1)

                        def back(t, k):
                            dve.wait_ge(ex, t + 1)
                            nc.vector.tensor_reduce(rs[:, k, :], EC[:, k, :].rearrange("p (n s) -> p s n", s=SLOTS), AX.X, ALU.add).then_inc(sm, 1)
                            dve.wait_ge(sm, t + 1)
                            nc.vector.reciprocal(ri[:, k, :], rs[:, k, :]).then_inc(si, 1)
                            dve.wait_ge(si, t + 1)
                            nc.vector.tensor_copy(rep[:, k, :].rearrange("p (g s) -> p g s", g=XPT), ri[:, k, :].unsqueeze(1).broadcast_to([P, XPT, SLOTS])).then_inc(rr, 1)

                        def weigh(t, k):
                            dve.wait_ge(rt_out, t + 1)
                            for n in range(4):
                                dve.wait_ge(tr, 4 * t + n + 9)
                                dve.wait_ge(y_ready, t + 1)
                                nc.vector.tensor_tensor(CT[:, 4 * n:4 * n + 4, :], tp[:, n, :].rearrange("p (j q) -> p j q", j=4),
                                                        RT[:, k, :].unsqueeze(1).broadcast_to([P, 4, P]), ALU.mult).then_inc(ct, 1)
                            dve.wait_ge(y_ready, t + 2)
                            dst = g_ffn[:, bass.ds(t, 1), :].squeeze(1) if not isinstance(t, int) else g_ffn[:, t, :]
                            nc.vector.tensor_copy(dst, yp[:, k, 0:HOUT]).then_inc(y_out, 1)

                        dve.sem_inc(y_out, 2)
                        dve.sem_inc(tr, 8)
                        dve.sem_inc(ct, 4)
                        dve.sem_inc(y_ready, 1)
                        front(0, 0)
                        with dve.Fori(0, NT // 2 - 1) as i:
                            front(2 * i + 1, 1)
                            back(2 * i, 0)
                            weigh(2 * i, 0)
                            front(2 * i + 2, 0)
                            back(2 * i + 1, 1)
                            weigh(2 * i + 1, 1)
                        front(NT - 1, 1)
                        back(NT - 2, 0)
                        weigh(NT - 2, 0)
                        back(NT - 1, 1)
                        weigh(NT - 1, 1)

                    @block.tensor
                    def _(pe):
                        with pe.Fori(0, NT // 2) as i:
                            for k in range(2):
                                t = 2 * i + k
                                pe.wait_ge(ex, t + 1)
                                for n in range(4):
                                    pe.wait_ge(ct, 4 * t + n + 1)
                                    for j in range(4):
                                        jj = 4 * n + j
                                        last = nc.tensor.transpose(tp[:, n, j * P:(j + 1) * P], EC[:, k, jj * P:(jj + 1) * P], ident[:, :])
                                    last.then_inc(tr, 1)
                                pe.wait_ge(rr, t + 1)
                                nc.tensor.transpose(rp[:, k, 0:P], rep[:, k, :], ident[:, :]).then_inc(rt_ready, 1)
                                pe.wait_ge(y_out, t + 1)
                                for n in range(4):
                                    pe.wait_ge(ct, 4 * t + n + 5)
                                    for j in range(4):
                                        jj = 4 * n + j
                                        last = nc.tensor.matmul(yp[:, k, 0:HOUT], CT[:, jj, :], Y[:, jj, :], start=jj == 0, stop=jj == NPT - 1)
                                last.then_inc(y_ready, 1)

            with ExitStack() as c:
                sem = lambda n: c.enter_context(nc.semaphore(f"f_{n}"))
                silu, m1, m2, stored = map(sem, ("silu", "m1", "m2", "stored"))
                with nc.Block() as block:
                    @block.scalar
                    def _(act):
                        nc.scalar.activation(g_ffn[:, :, :], g_ffn[:, :, :], ACT.Silu).then_inc(silu, 1)

                    @block.vector
                    def _(dve):
                        dve.wait_ge(silu, 1)
                        nc.vector.tensor_tensor(s_att[:, :, :], s_att[:, :, :], g_ffn[:, :, :], ALU.mult).then_inc(m1, 1)
                        dve.wait_ge(m1, 1)
                        nc.vector.tensor_tensor(x_res[:, :, :], x_res[:, :, :], s_att[:, :, :], ALU.add).then_inc(m2, 1)

                    @block.sync
                    def _(sp):
                        sp.wait_ge(m2, 1)
                        sp.dma_start(tiles(out), x_res[:, :, :]).then_inc(stored, 16)
                        sp.wait_ge(stored, 16)

        def finish(t):
            with nc.semaphore("dbg") as s, nc.Block() as block:
                @block.sync
                def _(sp):
                    sp.dma_start(tiles(out), t).then_inc(s, 16)
                    sp.wait_ge(s, 16)

        front_block(0)
        if STAGE == "xn":
            return finish(xn[:, :, :])
        with ExitStack() as c:
            wroute, fw = sb("wroute", [P, NE], c=c), sb("fw", [P, NT, NE], c=c)
            wgu, wd = sb("wgu", [P, NE, 2 * FF], c=c), sb("wd", [P, NE, 2, D], c=c)
            with nc.semaphore("ffn_loaded") as fl, nc.Block() as block:
                @block.sync
                def _(sp):
                    sp.dma_start(wroute[:, :], a["router"]).then_inc(fl, 16)
                    sp.dma_start(wgu[:, :, 0:FF], a["gating"].rearrange("e d f -> d e f")).then_inc(fl, 16)
                    sp.dma_start(wgu[:, :, FF:2 * FF], a["up"].rearrange("e d f -> d e f")).then_inc(fl, 16)
                    sp.dma_start(wd[:, :, :, :], a["down"].rearrange("e (c p) d -> p e c d", p=P)).then_inc(fl, 16)
                    sp.wait_ge(fl, 64)
            router_block(wroute, fw)
            attention0_block()
            if STAGE == "s0":
                return finish(s_att[:, :, :])
            experts0_block(fw, wgu, wd)
            if STAGE == "g0":
                return finish(g_ffn[:, :, :])
        front_block(1)
        if STAGE == "x1":
            return finish(x_res[:, :, :])
        attention1_block()
        if STAGE == "s1":
            return finish(s_att[:, :, :])
        with ExitStack() as c:
            L = sb("L", [P, NT, NP], c=c)
            Y = xnT[:, :].rearrange("p (j h) -> p j h", j=NPT)
            with ExitStack() as c1:
                slots_p = c1.enter_context(nc.psum_tensor("slots_p", [P, 4, BANK], F32))
                with ExitStack() as c2:
                    phiT = sb("phiT", [P, NP], c=c2)
                    rows = sb("phib_rows", [P, NP], BF16, c=c2)
                    ones = sb("phib_ones", [P, P], BF16, c=c2)
                    zero = sb("phib_zero", [P, BANK], BF16, c=c2)
                    with ExitStack() as c3:
                        pbf = sb("pbf", [P, NP], c=c3)
                        part = sb("pb_part", [P, NP], BF16, c=c3)
                        sem = lambda n: c3.enter_context(nc.semaphore(f"pb_{n}"))
                        loaded, zeroed, seq = map(sem, ("loaded", "zeroed", "seq"))
                        with nc.Block() as block:
                            @block.gpsimd
                            def _(pool):
                                nc.gpsimd.memset(pbf[:, :], 0.0).then_inc(zeroed, 1)
                                nc.gpsimd.memset(ones[:, :], 1.0).then_inc(zeroed, 1)
                                nc.gpsimd.memset(zero[:, :], 0.0).then_inc(zeroed, 1)
                                nc.gpsimd.memset(rows[:, :], 0.0).then_inc(zeroed, 1)

                            @block.sync
                            def _(sp):
                                sp.dma_start(phiT[:, :], a["phiT"]).then_inc(loaded, 16)
                                sp.wait_ge(zeroed, 1)
                                for q in range(3):
                                    sp.dma_start(pbf[32 * q:32 * q + 1, :], a["phi_b"]).then_inc(loaded, 16)
                                sp.wait_ge(loaded, 64)

                            @block.vector
                            def _(dve):
                                link = Chain(dve, seq)
                                dve.wait_ge(loaded, 64)
                                dve.wait_ge(zeroed, 4)
                                for q in range(3):
                                    link(nc.vector.tensor_copy(part[:, :], pbf[:, :]))
                                    link(nc.vector.tensor_copy(rows[32 * q:32 * q + 1, :], part[32 * q:32 * q + 1, :]))
                                    if q < 2:
                                        link(nc.vector.tensor_tensor(pbf[:, :], pbf[:, :], part[:, :], ALU.subtract))
                    soft_dispatch_block(L, slots_p, phiT, dict(rows=rows, ones=ones, zero=zero))
                slot_experts_block(slots_p, Y)
            if STAGE == "Y":
                return finish(Y)
            soft_combine_block(L, Y)


def kernel(L0_attn_hidden_states, L0_attn_Wq, L0_attn_bq, L0_attn_Wk, L0_attn_bk, L0_attn_Wv, L0_attn_bv, L0_attn_Wo,
           L0_attn_bo, L0_ffn_kernel_router_DE, L0_ffn_kernel_gating_EDF, L0_ffn_kernel_up_EDF, L0_ffn_kernel_down_EFD,
           L1_attn_w_qkv, L1_attn_b_qkv, L1_attn_w_out, L1_attn_b_out, L1_attn_w_gate, L1_attn_b_gate, L1_attn_pos_bias,
           L1_ffn_phi_w, L1_ffn_phi_b, L1_ffn_expert_w, L1_ffn_expert_b):
    import numpy as np
    import concourse.bacc as bacc
    from concourse.bass_utils import run_bass_kernel_spmd

    lay = lambda v: np.ascontiguousarray(v)
    halves = lambda v: list(np.asarray(v).reshape(-1, P))
    arrays = {
        "x": lay(np.asarray(L0_attn_hidden_states).reshape(TOK, D)),
        "wq": lay(L0_attn_Wq), "wk": lay(L0_attn_Wk), "wv": lay(L0_attn_Wv), "woT": lay(np.asarray(L0_attn_Wo).T),
        "bo": lay(np.asarray(L0_attn_bo).reshape(1, D)),
        "router": lay(L0_ffn_kernel_router_DE), "gating": lay(L0_ffn_kernel_gating_EDF),
        "up": lay(L0_ffn_kernel_up_EDF), "down": lay(L0_ffn_kernel_down_EFD),
        "w_qkv": lay(L1_attn_w_qkv), "w_gate": lay(L1_attn_w_gate), "w_out": lay(L1_attn_w_out),
        "b_out": lay(np.asarray(L1_attn_b_out).reshape(1, D)),
        "pos_bias": lay(np.tile(np.asarray(L1_attn_pos_bias)[BIAS_ORDER].T, (BATCH, 1))),
        "phiT": lay(np.asarray(L1_ffn_phi_w).T), "phi_b": lay(np.asarray(L1_ffn_phi_b).reshape(1, NP)),
        "expert_w": lay(L1_ffn_expert_w), "expert_b": lay(L1_ffn_expert_b),
        "cols": lay(np.stack(halves(L0_attn_bq) + halves(L0_attn_bk) + halves(L0_attn_bv) + halves(L1_attn_b_qkv)
                             + halves(L1_attn_b_gate), axis=1)),
    }
    nc = bacc.Bacc("TRN2", target_bir_lowering=False, num_devices=1)
    args = {n: nc.dram_tensor(f"in_{n}", v.shape, mybir.dt.from_np(v.dtype), kind="ExternalInput").ap() for n, v in arrays.items()}
    out = nc.dram_tensor("out_x", (TOK, D), F32, kind="ExternalOutput").ap()
    build(nc, args, out, None)
    r = run_bass_kernel_spmd(nc, [{f"in_{n}": v for n, v in arrays.items()}], core_ids=[0])
    return r.results[0]["out_x"].reshape(BATCH, SEQ, D)
```

```python
import concourse.bass as bass
from concourse import mybir
from contextlib import ExitStack

F32 = mybir.dt.float32
BF16 = mybir.dt.bfloat16
F32R = mybir.dt.float32r
I32 = mybir.dt.int32
ALU = mybir.AluOpType
ACT = mybir.ActivationFunctionType
AX = mybir.AxisListType

P = 128
BATCH, SEQ, D = 8, 256, 128
TOK = BATCH * SEQ
NT = TOK // P
TPB = SEQ // P
E2 = 2 * D
NE, FF = 8, 256
HEADS, HD = 16, 8
NX, SLOTS, HOUT = 64, 32, 128
NP = NX * SLOTS
NPT = NP // P
XPT = P // SLOTS
BANK = 512
EPS = 1e-5
SCALE0 = float(D) ** -0.5
SCALE1 = float(HD) ** -0.5

ALL_OFFSETS = [(1 << j) * tau for j in range(11) for tau in range(4)]
OFFS = sorted({o for o in ALL_OFFSETS if o < SEQ})
NO = len(OFFS)
NS = NO + 1
MEMBERS = [[i for i, o in enumerate(ALL_OFFSETS) if o == off] for off in OFFS]
MEMBERS.append([i for i, o in enumerate(ALL_OFFSETS) if o >= SEQ])
BIAS_ORDER = [i for m in MEMBERS for i in m]
BIAS_START = [sum(len(m) for m in MEMBERS[:s]) for s in range(NS)]

PAD = OFFS[-1]
QK_DVE = [s for s in range(NO) if s % 2]
QK_POOL = [s for s in range(NO) if s % 2 == 0]

COLS = ["bq0", "bq1", "bk0", "bk1", "bv0", "bv1", "b1q", "b1k", "b1v", "bgate"]
COL = {n: i for i, n in enumerate(COLS)}
STAGE = None


def tiles(ap):
    return ap.rearrange("(t p) d -> p t d", p=P)


class Chain:

    def __init__(self, eng, sem):
        self.eng, self.sem, self.n = eng, sem, 0

    def __call__(self, ins):
        self.n += 1
        ins.then_inc(self.sem, 1)
        self.eng.wait_ge(self.sem, self.n)
        return self.n


def build(nc, a, out, dbg):
    ctx = ExitStack()
    with ctx:
        def sb(name, shape, dt=F32, c=None):
            return (c or ctx).enter_context(nc.sbuf_tensor(name, shape, dt))

        ident = sb("ident", [P, P])
        cols = sb("cols", [P, len(COLS)])
        x_res = sb("x_res", [P, NT, D])
        xn = sb("xn", [P, NT, D])
        xnT = sb("xnT", [P, TOK])
        s_att = sb("s_att", [P, NT, D])
        g_ffn = sb("g_ffn", [P, NT, D])

        def front_block(layer):
            with ExitStack() as c:
                sem = lambda n: c.enter_context(nc.semaphore(f"{n}_{layer}"))
                loaded, consts, dve_seq, centered, squared = map(sem, ("loaded", "consts", "dve_seq", "centered", "squared"))
                var_ready, rstd_ready, normed, transposed, act_done, silu_done = map(
                    sem, ("var_ready", "rstd_ready", "normed", "transposed", "act_done", "silu_done"))
                mean = sb(f"mean{layer}", [P, NT], c=c)
                var = sb(f"var{layer}", [P, NT], c=c)
                rstd = sb(f"rstd{layer}", [P, NT], c=c)
                half = sb(f"half{layer}", [P, 1], c=c)
                sq = sb(f"sq{layer}", [P, NT, D], c=c)
                tp = c.enter_context(nc.psum_tensor(f"tp{layer}", [P, 4, BANK], F32))
                with nc.Block() as block:
                    @block.sync
                    def _(sp):
                        if layer == 0:
                            sp.dma_start(x_res[:, :, :], tiles(a["x"])).then_inc(loaded, 16)
                            sp.dma_start(cols[:, :], a["cols"]).then_inc(loaded, 16)
                            sp.wait_ge(loaded, 32)

                    @block.gpsimd
                    def _(pool):
                        nc.gpsimd.memset(half[:, :], -0.5).then_inc(consts, 1)
                        if layer == 0:
                            nc.gpsimd.memset(ident[:, :], 0.0).then_inc(consts, 1)
                            pool.wait_ge(consts, 2)
                            nc.gpsimd.affine_select(out=ident[:, :], in_=ident[:, :], compare_op=ALU.not_equal, fill=1.0,
                                                    base=0, pattern=[[-1, P]], channel_multiplier=1).then_inc(consts, 1)
                        pool.wait_ge(consts, 3 if layer == 0 else 1)
                        pool.wait_ge(var_ready, 1)
                        nc.gpsimd.tensor_tensor(rstd[:, :], var[:, :], half[:, 0:1].to_broadcast([P, NT]),
                                                ALU.pow).then_inc(rstd_ready, 1)

                    @block.vector
                    def _(dve):
                        link = Chain(dve, dve_seq)
                        if layer == 0:
                            dve.wait_ge(loaded, 32)
                        else:
                            dve.wait_ge(silu_done, 1)
                            link(nc.vector.tensor_tensor(sq[:, :, :], g_ffn[:, :, :], s_att[:, :, :], ALU.mult))
                            link(nc.vector.tensor_tensor(x_res[:, :, :], x_res[:, :, :], sq[:, :, :], ALU.add))
                        link(nc.vector.tensor_reduce(mean[:, :], x_res[:, :, :], AX.X, ALU.add))
                        link(nc.vector.tensor_scalar(mean[:, :], mean[:, :], 1.0 / D, None, ALU.mult))
                        nc.vector.tensor_tensor(xn[:, :, :], x_res[:, :, :], mean[:, :].unsqueeze(2).broadcast_to([P, NT, D]),
                                                ALU.subtract).then_inc(centered, 1)
                        dve.wait_ge(squared, 1)
                        link(nc.vector.tensor_reduce(var[:, :], sq[:, :, :], AX.X, ALU.add))
                        nc.vector.tensor_scalar(var[:, :], var[:, :], 1.0 / D, EPS, ALU.mult, ALU.add).then_inc(var_ready, 1)
                        dve.wait_ge(rstd_ready, 1)
                        nc.vector.tensor_tensor(xn[:, :, :], xn[:, :, :], rstd[:, :].unsqueeze(2).broadcast_to([P, NT, D]),
                                                ALU.mult).then_inc(normed, 1)

                    @block.scalar
                    def _(act):
                        if layer == 1:
                            nc.scalar.activation(g_ffn[:, :, :], g_ffn[:, :, :], ACT.Silu).then_inc(silu_done, 1)
                        act.wait_ge(centered, 1)
                        nc.scalar.activation(sq[:, :, :], xn[:, :, :], ACT.Square).then_inc(squared, 1)
                        for q in range(4):
                            act.wait_ge(transposed, q + 1)
                            nc.scalar.activation(xnT[:, q * BANK:(q + 1) * BANK], tp[:, q, :], ACT.Copy).then_inc(act_done, 1)

                    @block.tensor
                    def _(pe):
                        pe.wait_ge(normed, 1)
                        if layer == 0:
                            pe.wait_ge(consts, 3)
                        for t in range(NT):
                            last = nc.tensor.transpose(tp[:, t // 4, (t % 4) * P:(t % 4 + 1) * P], xn[:, t, :], ident[:, :])
                            if t % 4 == 3:
                                last.then_inc(transposed, 1)

        def router_block(wroute, fw):
            with ExitStack() as c:
                sem = lambda n: c.enter_context(nc.semaphore(f"rt_{n}"))
                tri_ready, logits_ready, dve_seq, shifted, expd, p12, e2 = map(
                    sem, ("tri_ready", "logits_ready", "dve_seq", "shifted", "expd", "p12", "e2"))
                r = lambda n, s: sb(f"rt_{n}", s, c=c)
                z, pr = r("z", [P, NT, NE]), r("pr", [P, NT, NE])
                m, s = r("m", [P, NT]), r("s", [P, NT])
                g, q = r("g", [P, NT, NE, NE]), r("q", [P, NT, NE, NE])
                tri = r("tri", [P, NE, NE])
                rank, m1, m2 = r("rank", [P, NT, NE]), r("m1", [P, NT, NE]), r("m2", [P, NT, NE])
                pa, pb, w1, w2 = r("pa", [P, NT]), r("pb", [P, NT]), r("w1", [P, NT]), r("w2", [P, NT])
                lp = c.enter_context(nc.psum_tensor("rt_lp", [P, NT, NE], F32))
                bc = lambda v: v[:, :].unsqueeze(2).broadcast_to([P, NT, NE])
                with nc.Block() as block:
                    @block.tensor
                    def _(pe):
                        for t in range(NT):
                            last = nc.tensor.matmul(lp[:, t, :], xnT[:, t * P:(t + 1) * P], wroute[:, :], start=True, stop=True)
                        last.then_inc(logits_ready, 1)

                    @block.gpsimd
                    def _(pool):
                        nc.gpsimd.memset(tri[:, :, :], 1.0).then_inc(tri_ready, 1)
                        pool.wait_ge(tri_ready, 1)
                        nc.gpsimd.affine_select(out=tri[:, :, :], in_=tri[:, :, :], compare_op=ALU.is_gt, fill=0.0, base=0,
                                                pattern=[[1, NE], [-1, NE]], channel_multiplier=0).then_inc(tri_ready, 1)

                    @block.vector
                    def _(dve):
                        link = Chain(dve, dve_seq)
                        dve.wait_ge(logits_ready, 1)
                        link(nc.vector.tensor_reduce(m[:, :], lp[:, :, :], AX.X, ALU.max))
                        nc.vector.tensor_tensor(z[:, :, :], lp[:, :, :], bc(m), ALU.subtract).then_inc(shifted, 1)
                        dve.wait_ge(expd, 1)
                        link(nc.vector.tensor_reduce(s[:, :], pr[:, :, :], AX.X, ALU.add))
                        link(nc.vector.reciprocal(s[:, :], s[:, :]))
                        link(nc.vector.tensor_tensor(pr[:, :, :], pr[:, :, :], bc(s), ALU.mult))
                        pj = pr[:, :, :].unsqueeze(2).broadcast_to([P, NT, NE, NE])
                        pe_ = pr[:, :, :].unsqueeze(3).broadcast_to([P, NT, NE, NE])
                        link(nc.vector.tensor_tensor(g[:, :, :, :], pj, pe_, ALU.is_gt))
                        link(nc.vector.tensor_tensor(q[:, :, :, :], pj, pe_, ALU.is_equal))
                        dve.wait_ge(tri_ready, 2)
                        link(nc.vector.tensor_tensor(q[:, :, :, :], q[:, :, :, :],
                                                     tri[:, :, :].unsqueeze(1).broadcast_to([P, NT, NE, NE]), ALU.mult))
                        link(nc.vector.tensor_tensor(g[:, :, :, :], g[:, :, :, :], q[:, :, :, :], ALU.add))
                        link(nc.vector.tensor_reduce(rank[:, :, :], g[:, :, :, :], AX.X, ALU.add))
                        link(nc.vector.tensor_scalar(m1[:, :, :], rank[:, :, :], 0.0, None, ALU.is_equal))
                        link(nc.vector.tensor_scalar(m2[:, :, :], rank[:, :, :], 1.0, None, ALU.is_equal))
                        link(nc.vector.tensor_tensor(z[:, :, :], m1[:, :, :], pr[:, :, :], ALU.mult))
                        link(nc.vector.tensor_reduce(pa[:, :], z[:, :, :], AX.X, ALU.add))
                        link(nc.vector.tensor_tensor(z[:, :, :], m2[:, :, :], pr[:, :, :], ALU.mult))
                        link(nc.vector.tensor_reduce(pb[:, :], z[:, :, :], AX.X, ALU.add))
                        nc.vector.tensor_tensor(pb[:, :], pb[:, :], pa[:, :], ALU.subtract).then_inc(p12, 1)
                        dve.wait_ge(e2, 1)
                        link(nc.vector.tensor_scalar(w1[:, :], w2[:, :], 1.0, None, ALU.add))
                        link(nc.vector.reciprocal(w1[:, :], w1[:, :]))
                        link(nc.vector.tensor_tensor(w2[:, :], w2[:, :], w1[:, :], ALU.mult))
                        link(nc.vector.tensor_tensor(m1[:, :, :], m1[:, :, :], bc(w1), ALU.mult))
                        link(nc.vector.tensor_tensor(m2[:, :, :], m2[:, :, :], bc(w2), ALU.mult))
                        link(nc.vector.tensor_tensor(fw[:, :, :], m1[:, :, :], m2[:, :, :], ALU.add))

                    @block.scalar
                    def _(act):
                        act.wait_ge(shifted, 1)
                        nc.scalar.activation(pr[:, :, :], z[:, :, :], ACT.Exp).then_inc(expd, 1)
                        act.wait_ge(p12, 1)
                        nc.scalar.activation(w2[:, :], pb[:, :], ACT.Exp).then_inc(e2, 1)

        def attention0_block():
            with ExitStack() as c:
                sem = lambda n: c.enter_context(nc.semaphore(f"a0_{n}"))
                loaded, bvb_ready, folded, fold_out = map(sem, ("loaded", "bvb_ready", "folded", "fold_out"))
                xt_ready, xt_used = map(sem, ("xt_ready", "xt_used"))
                qg_ready, q_out, g_out, sc_ready, mx_ready, c_ready, t1_ready, nb_ready = map(
                    sem, ("qg_ready", "q_out", "g_out", "sc_ready", "mx_ready", "c_ready", "t1_ready", "nb_ready"))
                probs, rinv, pt_ready, pt_out, o_ready, o_out = map(
                    sem, ("probs", "rinv", "pt_ready", "pt_out", "o_ready", "o_out"))
                r = lambda n, s: sb(f"a0_{n}", s, c=c)
                wq, wk, wv, woT = (r(n, [P, 2, D]) for n in ("wq", "wk", "wv", "woT"))
                bo = r("bo", [P, D])
                bvb = r("bvb", [P, 2, P])
                bqb = r("bqb", [P, 2, P])
                Am, VO, bprime = r("Am", [P, D]), r("VO", [P, D]), r("bprime", [P, D])
                u, wc, bqbk = r("u", [P, 1]), r("wc", [P, 1]), r("bqbk", [P, 1])
                xt = r("xt", [P, 2, SEQ])
                qs, G, prob, pts = r("qs", [P, 2, SEQ]), r("G", [P, 2, TPB, D]), r("prob", [P, 2, TPB, SEQ]), r("pts", [P, 2, TPB, SEQ])
                mz, cs, t1, nb, rs, ri = (r(n, [P, 2, TPB]) for n in ("mz", "cs", "t1", "nb", "rs", "ri"))
                ps = c.enter_context(nc.psum_tensor("a0_ps", [P, 2, 4, BANK], F32))
                qp = lambda k: ps[:, k, 0, 0:SEQ]
                gp = lambda k: ps[:, k, 0, SEQ:2 * SEQ]
                sc = lambda k: ps[:, k, 1, :].rearrange("p (s t) -> p s t", s=TPB)
                pt = lambda k: ps[:, k, 2, :].rearrange("p (j s) -> p j s", j=TPB)
                op = lambda k: ps[:, k, 3, 0:TPB * D].rearrange("p (s o) -> p s o", s=TPB)
                cp = lambda k: ps[:, k, 3, TPB * D:TPB * D + TPB]
                with nc.Block() as block:
                    @block.sync
                    def _(sp):
                        for dst, name in ((wq, "wq"), (wk, "wk"), (wv, "wv"), (woT, "woT")):
                            sp.dma_start(dst[:, :, :], a[name].rearrange("(c p) d -> p c d", p=P)).then_inc(loaded, 16)
                        sp.dma_start(bo[:, :], a["bo"].broadcast_to([P, D])).then_inc(loaded, 16)

                    @block.gpsimd
                    def _(pool):
                        for cc in range(2):
                            nc.gpsimd.tensor_copy(bvb[:, cc, :], cols[:, COL["bv0"] + cc:COL["bv0"] + cc + 1].to_broadcast([P, P])).then_inc(bvb_ready, 1)
                            nc.gpsimd.tensor_copy(bqb[:, cc, :], cols[:, COL["bq0"] + cc:COL["bq0"] + cc + 1].to_broadcast([P, P])).then_inc(bvb_ready, 1)
                        with pool.Fori(0, BATCH // 2) as i:
                            for k in range(2):
                                pool.wait_ge(xt_used, 2 * i + k + 1)
                                nc.gpsimd.tensor_copy(xt[:, k, :], xnT[:, bass.ds((2 * i + k) * SEQ, SEQ)]).then_inc(xt_ready, 1)

                    @block.tensor
                    def _(pe):
                        pe.sem_inc(xt_used, 2)
                        pe.wait_ge(loaded, 80)
                        pe.wait_ge(bvb_ready, 4)
                        for n in range(2):
                            f = dict(start=n == 0, stop=n == 1)
                            nc.tensor.matmul(ps[:, 0, 0, 0:D], wq[:, n, :], wk[:, n, :], **f)
                        for n in range(2):
                            f = dict(start=n == 0, stop=n == 1)
                            nc.tensor.matmul(ps[:, 0, 1, 0:D], wv[:, n, :], woT[:, n, :], **f)
                        for n in range(2):
                            f = dict(start=n == 0, stop=n == 1)
                            nc.tensor.matmul(ps[:, 0, 2, 0:1], wk[:, n, :], cols[:, COL["bq0"] + n:COL["bq0"] + n + 1], **f)
                        for n in range(2):
                            f = dict(start=n == 0, stop=n == 1)
                            nc.tensor.matmul(ps[:, 0, 3, 0:1], wq[:, n, :], cols[:, COL["bk0"] + n:COL["bk0"] + n + 1], **f)
                        for n in range(2):
                            f = dict(start=n == 0, stop=n == 1)
                            nc.tensor.matmul(ps[:, 1, 0, 0:1], bqb[:, n, :], cols[:, COL["bk0"] + n:COL["bk0"] + n + 1], **f)
                        for n in range(2):
                            f = dict(start=n == 0, stop=n == 1)
                            last = nc.tensor.matmul(ps[:, 1, 1, 0:D], bvb[:, n, :], woT[:, n, :], **f)
                        last.then_inc(folded, 1)
                        pe.wait_ge(fold_out, 6)
                        with pe.Fori(0, BATCH // 2) as i:
                            for k in range(2):
                                b = 2 * i + k
                                pe.wait_ge(xt_ready, b + 1)
                                pe.wait_ge(g_out, b + 1)
                                pe.wait_ge(o_out, b + 1)
                                nc.tensor.matmul(qp(k), Am[:, :], xt[:, k, :], start=True, stop=True)
                                for s in range(TPB):
                                    nc.tensor.matmul(gp(k)[:, s * D:(s + 1) * D], xt[:, k, s * P:(s + 1) * P], VO[:, :], start=True, stop=True)
                                for s in range(TPB):
                                    last = nc.tensor.matmul(cp(k)[:, s:s + 1], xt[:, k, s * P:(s + 1) * P], wc[:, :], start=True, stop=True)
                                last.then_inc(qg_ready, 1)
                            for k in range(2):
                                b = 2 * i + k
                                pe.wait_ge(q_out, b + 1)
                                for s in range(TPB):
                                    last = nc.tensor.matmul(sc(k)[:, s, :], qs[:, k, s * P:(s + 1) * P], xt[:, k, :], start=True, stop=True)
                                last.then_inc(sc_ready, 1)
                            for k in range(2):
                                b = 2 * i + k
                                pe.wait_ge(probs, 2 * b + 2)
                                for s in range(TPB):
                                    for j in range(TPB):
                                        last = nc.tensor.transpose(pt(k)[:, j, s * P:(s + 1) * P], prob[:, k, s, j * P:(j + 1) * P], ident[:, :])
                                last.then_inc(pt_ready, 1)
                            for k in range(2):
                                b = 2 * i + k
                                pe.wait_ge(pt_out, b + 1)
                                for s in range(TPB):
                                    for j in range(TPB):
                                        last = nc.tensor.matmul(op(k)[:, s, :], pts[:, k, j, s * P:(s + 1) * P], G[:, k, j, :], start=j == 0, stop=j == TPB - 1)
                                last.then_inc(o_ready, 1)

                    @block.scalar
                    def _(act):
                        act.wait_ge(folded, 1)
                        nc.scalar.activation(Am[:, :], ps[:, 0, 0, 0:D], ACT.Copy).then_inc(fold_out, 1)
                        nc.scalar.activation(VO[:, :], ps[:, 0, 1, 0:D], ACT.Copy).then_inc(fold_out, 1)
                        nc.scalar.activation(u[:, :], ps[:, 0, 2, 0:1], ACT.Copy).then_inc(fold_out, 1)
                        nc.scalar.activation(wc[:, :], ps[:, 0, 3, 0:1], ACT.Copy, scale=SCALE0).then_inc(fold_out, 1)
                        nc.scalar.activation(bqbk[:, :], ps[:, 1, 0, 0:1], ACT.Copy, scale=SCALE0).then_inc(fold_out, 1)
                        act.sem_inc(g_out, 2)
                        act.wait_ge(fold_out, 6)
                        nc.scalar.preload_act_table(ACT.Exp)
                        with act.Fori(0, BATCH // 2) as i:
                            for k in range(2):
                                b = 2 * i + k
                                act.wait_ge(qg_ready, b + 1)
                                nc.scalar.activation(qs[:, k, :], qp(k), ACT.Identity, bias=u[:, 0:1]).then_inc(q_out, 1)
                                nc.scalar.activation(G[:, k, :, :].rearrange("p j o -> p (j o)"), gp(k), ACT.Copy).then_inc(g_out, 1)
                            for k in range(2):
                                b = 2 * i + k
                                act.wait_ge(nb_ready, b + 1)
                                for s in range(TPB):
                                    nc.scalar.activation(prob[:, k, s, :], sc(k)[:, s, :], ACT.Exp, bias=nb[:, k, s:s + 1], scale=SCALE0,
                                                         accum_out=rs[:, k, s:s + 1]).then_inc(probs, 1)
                            for k in range(2):
                                b = 2 * i + k
                                act.wait_ge(pt_ready, b + 1)
                                nc.scalar.activation(pts[:, k, :, :], pt(k), ACT.Copy).then_inc(pt_out, 1)

                    @block.vector
                    def _(dve):
                        dve.wait_ge(folded, 1)
                        dve.wait_ge(loaded, 80)
                        nc.vector.tensor_tensor(bprime[:, :], ps[:, 1, 1, 0:D], bo[:, :], ALU.add).then_inc(fold_out, 1)
                        dve.sem_inc(o_out, 2)
                        dve.wait_ge(fold_out, 6)
                        with dve.Fori(0, BATCH // 2) as i:
                            for k in range(2):
                                b = 2 * i + k
                                dve.wait_ge(qg_ready, b + 1)
                                nc.vector.tensor_scalar(cs[:, k, :], cp(k), bqbk[:, 0:1], None, ALU.add).then_inc(c_ready, 1)
                                dve.wait_ge(sc_ready, b + 1)
                                nc.vector.tensor_reduce(mz[:, k, :], sc(k), AX.X, ALU.max).then_inc(mx_ready, 1)
                                dve.wait_ge(mx_ready, b + 1)
                                dve.wait_ge(c_ready, b + 1)
                                nc.vector.scalar_tensor_tensor(t1[:, k, :], mz[:, k, :], SCALE0, cs[:, k, :], ALU.mult, ALU.add).then_inc(t1_ready, 1)
                                dve.wait_ge(t1_ready, b + 1)
                                nc.vector.tensor_tensor(nb[:, k, :], cs[:, k, :], t1[:, k, :], ALU.subtract).then_inc(nb_ready, 1)
                            for k in range(2):
                                b = 2 * i + k
                                dve.wait_ge(probs, 2 * b + 2)
                                nc.vector.reciprocal(ri[:, k, :], rs[:, k, :]).then_inc(rinv, 1)
                                dve.wait_ge(rinv, b + 1)
                                dve.wait_ge(o_ready, b + 1)
                                for s in range(TPB):
                                    last = nc.vector.scalar_tensor_tensor(s_att[:, bass.ds(TPB * b + s, 1), :].squeeze(1), op(k)[:, s, :], ri[:, k, s:s + 1], bprime[:, :],
                                                                          ALU.mult, ALU.add)
                                last.then_inc(o_out, 1)
                            dve.sem_inc(xt_used, 2)

        def experts0_block(fw, xh, xl, wh, wl, wd):
            UNITS = 2 * NE
            GT = BANK // P
            RING = 3
            with ExitStack() as c:
                sem = lambda n: c.enter_context(nc.semaphore(f"e0_{n}"))
                gu_ready, sg_ready, fu_ready, y_ready, y_added = map(sem, ("gu_ready", "sg_ready", "fu_ready", "y_ready", "y_added"))
                sg = sb("e0_sg", [P, 2, BANK], c=c)
                fu = sb("e0_fu", [P, 2, 2, BANK], c=c)
                gu = c.enter_context(nc.psum_tensor("e0_gu", [P, RING, 2, BANK], F32))
                yp = c.enter_context(nc.psum_tensor("e0_yp", [P, 2, BANK], F32))

                def last_user(u):
                    return u - RING if u >= RING else max(v for v in range(UNITS) if v % RING == u % RING) - UNITS

                with nc.Block() as block:
                    @block.tensor
                    def _(pe):
                        with pe.Fori(0, NT // GT) as g:
                            def gate_up(u):
                                e, f = divmod(u, 2)
                                pe.wait_ge(fu_ready, UNITS * g + last_user(u) + 1 + UNITS)
                                cols_of = bass.ds(g * BANK, BANK)
                                for h in range(2):
                                    w = slice(h * FF + f * P, h * FF + (f + 1) * P)
                                    nc.tensor.matmul(gu[:, u % RING, h, :], wh[:, e, w], xh[:, cols_of], start=True, stop=False)
                                    nc.tensor.matmul(gu[:, u % RING, h, :], wh[:, e, w], xl[:, cols_of], start=False, stop=False)
                                    last = nc.tensor.matmul(gu[:, u % RING, h, :], wl[:, e, w], xh[:, cols_of], start=False, stop=True)
                                last.then_inc(gu_ready, 1)

                            def down(e):
                                pe.wait_ge(fu_ready, UNITS * g + 2 * e + 2 + UNITS)
                                pe.wait_ge(y_added, NE * g + e + 1)
                                for j in range(GT):
                                    for f in range(2):
                                        last = nc.tensor.matmul(yp[:, e % 2, j * D:(j + 1) * D], fu[:, e % 2, f, j * P:(j + 1) * P], wd[:, e, f, :],
                                                                start=f == 0, stop=f == 1)
                                last.then_inc(y_ready, 1)

                            for e in range(NE):
                                gate_up(2 * e)
                                gate_up(2 * e + 1)
                                if e > 0:
                                    down(e - 1)
                            down(NE - 1)

                    @block.scalar
                    def _(act):
                        nc.scalar.preload_act_table(ACT.Silu)
                        with act.Fori(0, NT // GT) as g:
                            for u in range(UNITS):
                                act.wait_ge(gu_ready, UNITS * g + u + 1)
                                act.wait_ge(fu_ready, UNITS * g + u - 1 + UNITS)
                                nc.scalar.activation(sg[:, u % 2, :], gu[:, u % RING, 0, :], ACT.Silu).then_inc(sg_ready, 1)

                    @block.vector
                    def _(dve):
                        dve.sem_inc(fu_ready, UNITS)
                        dve.sem_inc(y_added, 2)
                        with dve.Fori(0, NT // GT) as g:
                            def fuse(u):
                                e, f = divmod(u, 2)
                                dve.wait_ge(sg_ready, UNITS * g + u + 1)
                                if e >= 2:
                                    dve.wait_ge(y_ready, NE * g + e - 1)
                                nc.vector.tensor_tensor(fu[:, e % 2, f, :], sg[:, u % 2, :], gu[:, u % RING, 1, :], ALU.mult).then_inc(fu_ready, 1)

                            def add(e):
                                dve.wait_ge(y_ready, NE * g + e + 1)
                                if e > 0:
                                    dve.wait_ge(y_added, NE * g + e + 2)
                                for j in range(GT):
                                    dst = g_ffn[:, bass.ds(GT * g + j, 1), :].squeeze(1)
                                    w = fw[:, bass.ds(GT * g + j, 1), e:e + 1].squeeze(1)
                                    y = yp[:, e % 2, j * D:(j + 1) * D]
                                    if e == 0:
                                        last = nc.vector.tensor_scalar(dst, y, w, None, ALU.mult)
                                    else:
                                        last = nc.vector.scalar_tensor_tensor(dst, y, w, dst, ALU.mult, ALU.add)
                                last.then_inc(y_added, 1)

                            for e in range(NE):
                                fuse(2 * e)
                                fuse(2 * e + 1)
                                if e > 0:
                                    add(e - 1)
                            add(NE - 1)

        def layer1_block():
            qkv_d = nc.dram_tensor("a1_qkv_d", [3, HEADS, HD, BATCH, SEQ], F32, kind="Internal").ap()
            att_d = nc.dram_tensor("a1_att_d", [BATCH, HEADS, HD, SEQ], F32, kind="Internal").ap()
            with ExitStack() as c:
                r = lambda n, s, dt=F32: sb(f"l1_{n}", s, dt, c=c)
                sem = lambda n: c.enter_context(nc.semaphore(f"l1_{n}"))
                xh, xl = r("xh", [P, TOK], F32R), r("xl", [P, TOK], F32R)
                ph, pl = r("ph", [P, NP], F32R), r("pl", [P, NP], F32R)
                rows = r("rows", [P, NP], BF16)
                onerow = r("onerow", [P, P], BF16)
                zero = r("zero", [P, P], BF16)
                identb = r("identb", [P, P], BF16)
                Z = r("Z", [P, 2, NP])
                wl = r("wl", [P, 4, P], F32R)
                xth, xtl = wl[:, 0:2, :], wl[:, 2:4, :]
                xs = r("xs", [P, 2, D])
                am, sr = r("am", [P, 2, NX]), r("sr", [P, 2, NX])
                spare = g_ffn[:, :, :].rearrange("p t d -> p (t d)")
                bm = spare[:, 0:NT * 2 * SLOTS].rearrange("p (t h s) -> p t h s", t=NT, h=2)
                brow = spare[:, NT * 2 * SLOTS:].bitcast(BF16).rearrange("p (t c) -> p t c", t=NT)
                bT = r("bT", [P, NT, P], BF16)
                q, kp, vp = r("q", [P, HD, SEQ]), r("kp", [P, HD, PAD + SEQ]), r("vp", [P, HD, PAD + SEQ])
                acc = q
                prod = r("prod", [P, 2, HD, SEQ])
                sc = r("sc", [P, NS, SEQ])
                m = r("m", [P, SEQ])
                den = m
                pb, wb = r("pb", [P, len(BIAS_ORDER)]), r("wb", [P, len(BIAS_ORDER)])
                mb, W = r("mb", [P, NS]), r("W", [P, NS])
                bqs, half = r("bqs", [P, 1]), r("half", [P, 1])
                mean, var, rstd = r("mean", [P, NT]), r("var", [P, NT]), r("rstd", [P, NT])
                mean2, var2, rstd2 = r("mean2", [P, NT]), r("var2", [P, NT]), r("rstd2", [P, NT])
                starts = r("starts", [1, NO], I32)
                ew = r("ew", [P, NX, HOUT])
                flat_ew = ew[:, :, :].rearrange("p n h -> p (n h)")
                wraw = flat_ew[:, 0:4 * P].rearrange("p (j c) -> p j c", j=4)
                wh = r("wh", [P, 4, P], F32R)
                same_slot = r("same_slot", [P, XPT, SLOTS])
                gate = xnT
                Y = s_att
                qkT = sc[:, 0:HD * 2, :].rearrange("p (j a) n -> p j (a n)", j=2)
                vT = prod[:, 0, :, :].rearrange("p d n -> p (d n)")
                sq = prod[:, 1, :, :].rearrange("p d (a n) -> p (d a) n", n=D)
                attT = prod[:, 0, :, :].rearrange("p d n -> p (d n)").rearrange("p (b n) -> p b n", b=BATCH)
                s2 = prod[:, 1, :, :].rearrange("p d n -> p (d n)").rearrange("p (t d) -> p t d", t=NT)
                tmpb = vT.bitcast(BF16).rearrange("p (j n) -> p j n", j=2)
                rowsel = ident[:, 96:99]
                X2 = Z[:, 1, :].rearrange("p (j d) -> p j d", j=NPT)
                XT0 = Z[:, 0, :].rearrange("p (j d) -> p j d", j=NPT)
                acc_p = c.enter_context(nc.psum_tensor("l1_acc", [P, 4, BANK], F32))
                lg = c.enter_context(nc.psum_tensor("l1_lg", [P, 4, BANK], F32))

                NC, CH = TOK // 256, 256
                E = (Z[:, :, :].rearrange("p k z -> p (k z)").rearrange("p (j q) -> p j q", j=NPT),
                     flat_ew[:, 0:NPT * CH].rearrange("p (j q) -> p j q", j=NPT))
                esum, inv = (flat_ew[:, (NPT + 2 * n) * CH:(NPT + 2 * n + 2) * CH].rearrange("p (k q) -> p k q", k=2) for n in range(2))
                wout, b_out = (flat_ew[:, (NPT + 4) * CH + n * D:(NPT + 4) * CH + (n + 1) * D] for n in range(2))
                den_p = acc_p[:, 0, 0:CH]
                y_p = lambda k: acc_p[:, 1 + k, 0:2 * HOUT]
                lgb = lambda n: lg[:, 2 * (n % 2):2 * (n % 2) + 2, :].rearrange("p b q -> p (b q)")

                (loaded, ew_loaded, eb_loaded, consts, dve_seq, pool_seq, silu1, x1_ready, centered, squared, var_ready,
                 rstd_ready, normed, xT_ready, xh_ready, xl_ready, ph_ready, w_ready, qkv_ready, qkv_out, att_stored, qkv_back) = map(sem, (
                    "loaded", "ew_loaded", "eb_loaded", "consts", "dve_seq", "pool_seq", "silu1", "x1_ready", "centered", "squared", "var_ready",
                    "rstd_ready", "normed", "xT_ready", "xh_ready", "xl_ready", "ph_ready", "w_ready", "qkv_ready", "qkv_out", "att_stored", "qkv_back"))
                stored = [sem(f"stored_{n}") for n in "qkv"]
                (xt_ready, lg_ready, z_copied, xs_ready, mx, zs, ex, sm, si, dn, xd) = map(sem, (
                    "xt_ready", "lg_ready", "z_copied", "xs_ready", "mx", "zs", "ex", "sm", "si", "dn", "xd"))
                (clipped, slot_tr, cen2, sq2, var2_ready, rstd2_ready, nrm2, tanhed, slot_tr2, xt_out, y_prod, y_ready,
                 br_ready, bT_tr, bT_out, qk_prod, qk_red, w_sub, w_exp, sc_sub, sc_exp, sc_ready) = map(sem, (
                    "clipped", "slot_tr", "cen2", "sq2", "var2_ready", "rstd2_ready", "nrm2", "tanhed", "slot_tr2", "xt_out", "y_prod", "y_ready",
                    "br_ready", "bT_tr", "bT_out", "qk_prod", "qk_red", "w_sub", "w_exp", "sc_sub", "sc_exp", "sc_ready"))
                (lgb_ready, exb, sum_ready, den_ready, inv_ready, ct, yb_ready, yb_out, pv_prod, pv_add,
                 att_ready, att_back, gated, proj, silu2, fin, out_stored, wout_loaded) = map(sem, (
                    "lgb_ready", "exb", "sum_ready", "den_ready", "inv_ready", "ct", "yb_ready", "yb_out", "pv_prod", "pv_add",
                    "att_ready", "att_back", "gated", "proj", "silu2", "fin", "out_stored", "wout_loaded"))

                over_d = lambda x: x[:, :].unsqueeze(2).broadcast_to([P, NT, D])
                over_n = lambda x: x[:, :].unsqueeze(2).broadcast_to([P, NS, SEQ])
                over_s = lambda x: x[:, :].unsqueeze(1).broadcast_to([P, NS, SEQ])
                HX = NX // 2
                HALVES = 2 * NT
                part_of = lambda buf, v: buf[:, v // 2, (v % 2) * HX:(v % 2 + 1) * HX]
                over_slots = lambda buf, v: part_of(buf, v).unsqueeze(2).broadcast_to([P, HX, SLOTS])
                zflat = lambda v: Z[:, v // 2, (v % 2) * NP // 2:(v % 2 + 1) * NP // 2]
                zhalf = lambda v: zflat(v).rearrange("p (n s) -> p n s", s=SLOTS)
                lg_half = lambda v: lg[:, 2 * (v % 2):2 * (v % 2) + 2, :].rearrange("p b q -> p (b q)")
                at_most = lambda u: not isinstance(u, int) or u < HALVES
                tile_index = lambda u, v: (u - v % 2) // 2

                def all_halves(eng, step):
                    with eng.Fori(0, HALVES // 4 - 1) as i:
                        for v in range(4):
                            step(4 * i + v, v)
                    for v in range(4):
                        step(HALVES - 4 + v, v)

                def tile_of(buf, t):
                    return buf[:, t, :] if isinstance(t, int) else buf[:, bass.ds(t, 1), :].squeeze(1)

                with nc.Block() as block:
                    @block.sync
                    def _(sp):
                        sp.dma_start(wraw[:, 0:3, :], a["w_qkv"].rearrange("d (j c) -> d j c", j=3)).then_inc(loaded, 16)
                        sp.dma_start(wraw[:, 3, :], a["w_gate"]).then_inc(loaded, 16)
                        sp.dma_start(Z[:, 0, :], a["phiT"]).then_inc(loaded, 16)
                        sp.dma_start(Z[96:99, 1, :], a["phi_b"].broadcast_to([3, NP])).then_inc(loaded, 16)
                        sp.dma_start(pb[:, :], a["pos_bias"]).then_inc(loaded, 16)
                        sp.dma_start(starts[:, :], a["starts"]).then_inc(loaded, 16)
                        for j, dst in enumerate((q[:, :, :], kp[:, :, PAD:], vp[:, :, PAD:])):
                            sp.wait_ge(qkv_out, 4 * j + 4)
                            src = qkT[:, j, :] if j < 2 else vT
                            sp.dma_start(qkv_d[j].rearrange("h d b n -> (h d) (b n)"), src).then_inc(stored[j], 16)
                        for j, dst in enumerate((q[:, :, :], kp[:, :, PAD:], vp[:, :, PAD:])):
                            sp.wait_ge(stored[j], 16)
                            for b in range(BATCH):
                                sp.dma_start(dst[b * HEADS:(b + 1) * HEADS, :, :], qkv_d[j, :, :, b, :]).then_inc(qkv_back, 16)
                        sp.wait_ge(qkv_ready, 16)
                        sp.dma_start(ew[:, :, :], a["expert_w"].rearrange("n d h -> d n h")).then_inc(ew_loaded, 16)
                        sp.wait_ge(x1_ready, 1)
                        for g in range(XPT):
                            sp.dma_start(Y[g * SLOTS:(g + 1) * SLOTS, :, :],
                                         a["expert_b"].rearrange("(j g) h -> g j h", g=XPT)[g:g + 1].broadcast_to([SLOTS, NPT, HOUT])).then_inc(eb_loaded, 16)
                        sp.wait_ge(y_prod, 4)
                        sp.dma_start(wout, a["w_out"]).then_inc(wout_loaded, 16)
                        sp.dma_start(b_out, a["b_out"].broadcast_to([P, D])).then_inc(wout_loaded, 16)
                        sp.wait_ge(att_ready, 1)
                        sp.dma_start(att_d.rearrange("b h d n -> (b h) d n"), acc[:, :, :]).then_inc(att_stored, 16)
                        sp.wait_ge(att_stored, 16)
                        for b in range(BATCH):
                            sp.dma_start(attT[:, b, :], att_d[b].rearrange("h d n -> (h d) n")).then_inc(att_back, 16)
                        for n in range(4):
                            sp.wait_ge(fin, n + 1)
                            sp.dma_start(tiles(out)[:, 4 * n:4 * n + 4, :], x_res[:, 4 * n:4 * n + 4, :]).then_inc(out_stored, 16)
                        sp.wait_ge(out_stored, 64)

                    @block.gpsimd
                    def _(pool):
                        link = Chain(pool, pool_seq)
                        nc.gpsimd.memset(half[:, :], -0.5)
                        link(nc.gpsimd.memset(same_slot[:, :, :], 0.0))
                        for g in range(XPT):
                            link(nc.gpsimd.affine_select(out=same_slot[:, :, :], in_=same_slot[:, :, :], compare_op=ALU.not_equal, fill=1.0,
                                                         base=-g * SLOTS, pattern=[[0, XPT], [-1, SLOTS]], channel_multiplier=1))
                        nc.gpsimd.memset(zero[:, :], 0.0)
                        nc.gpsimd.memset(kp[:, :, 0:PAD], 0.0)
                        nc.gpsimd.memset(vp[:, :, 0:PAD], 0.0)
                        nc.gpsimd.memset(onerow[:, :], 0.0)
                        link(nc.gpsimd.memset(rows[:, :], 0.0))
                        link(nc.gpsimd.memset(onerow[96:99, :], 1.0))
                        link(nc.gpsimd.tensor_copy(identb[:, :], ident[:, :]))
                        for g in range(3):
                            nc.gpsimd.affine_select(out=rows[32 * g:32 * g + 32, :], in_=rows[32 * g:32 * g + 32, :], compare_op=ALU.not_equal,
                                                    fill=1.0, base=0, pattern=[[0, NX], [1, SLOTS]], channel_multiplier=-1).then_inc(consts, 1)
                            pool.wait_ge(consts, g + 1)
                        pool.wait_ge(loaded, 96)
                        link(nc.gpsimd.tensor_copy(ph[:, :], Z[:, 0, :]))
                        nc.gpsimd.tensor_tensor(pl[:, :], Z[:, 0, :], ph[:, :].bitcast(F32), ALU.subtract).then_inc(ph_ready, 1)
                        pool.wait_ge(var_ready, 1)
                        nc.gpsimd.tensor_tensor(rstd[:, :], var[:, :], half[:, 0:1].to_broadcast([P, NT]), ALU.pow).then_inc(rstd_ready, 1)
                        pool.wait_ge(x1_ready, 1)

                        def load_xt(t, k, ready):
                            nc.gpsimd.tensor_copy(xth[:, k, :], xh[:, bass.ds(t * P, P)].bitcast(F32))
                            nc.gpsimd.tensor_copy(xtl[:, k, :], xl[:, bass.ds(t * P, P)].bitcast(F32)).then_inc(ready, 1)

                        link(nc.gpsimd.memset(brow, 0.0))
                        nc.gpsimd.memset(brow[:, :, 96:99], 1.0).then_inc(consts, 1)

                        def shift(u, v):
                            pool.wait_ge(mx, u + 1)
                            nc.gpsimd.tensor_tensor(zhalf(v), zhalf(v), over_slots(am, v), ALU.subtract).then_inc(zs, 1)

                        def scale(u, v):
                            pool.wait_ge(si, u + 1)
                            nc.gpsimd.tensor_tensor(zhalf(v), zhalf(v), over_slots(sr, v), ALU.mult).then_inc(dn, 1)

                        def step(u, v):
                            shift(u + 1, (v + 1) % 4) if at_most(u + 1) else None
                            scale(u, v)

                        shift(0, 0)
                        all_halves(pool, step)

                        for n, s in enumerate(QK_POOL):
                            off = OFFS[s]
                            w = SEQ - off
                            if n == 0:
                                pool.wait_ge(qkv_back, 16 * 3 * BATCH)
                            else:
                                pool.wait_ge(qk_red, n)
                            nc.gpsimd.tensor_tensor(prod[:, 0, :, 0:w], q[:, :, off:SEQ], kp[:, :, PAD:PAD + w], ALU.mult).then_inc(qk_prod, 1)
                            if n == 2:
                                pool.wait_ge(var2_ready, 1)
                                nc.gpsimd.tensor_tensor(rstd2[:, :], var2[:, :], half[:, 0:1].to_broadcast([P, NPT]), ALU.pow).then_inc(rstd2_ready, 1)

                        pool.wait_ge(sc_ready, 1)

                        def value_products(t, k):
                            start = pool.value_load(starts[0:1, bass.ds(t, 1)], min_val=0, max_val=PAD)
                            pool.wait_ge(pv_add, t + 1)
                            nc.gpsimd.tensor_tensor(prod[:, k, :, :], sc[:, bass.ds(t, 1), :].broadcast_to([P, HD, SEQ]),
                                                    vp[:, :, bass.ds(start, SEQ)], ALU.mult).then_inc(pv_prod, 1)

                        with pool.Fori(0, NC // 2) as i:
                            for k in range(2):
                                c = 2 * i + k
                                value_products(2 * c, 0)
                                value_products(2 * c + 1, 1)

                    @block.scalar
                    def _(act):
                        nc.scalar.activation(g_ffn[:, :, :], g_ffn[:, :, :], ACT.Silu).then_inc(silu1, 1)
                        act.wait_ge(centered, 1)
                        nc.scalar.activation(sq, xn[:, :, :], ACT.Square).then_inc(squared, 1)
                        act.wait_ge(loaded, 96)
                        nc.scalar.activation(wh[:, :, :], wraw[:, :, :], ACT.Copy).then_inc(w_ready, 1)
                        for n in range(4):
                            act.wait_ge(xT_ready, n + 1)
                            nc.scalar.activation(xh[:, n * BANK:(n + 1) * BANK], lg[:, n, :], ACT.Copy).then_inc(xh_ready, 1)
                        act.wait_ge(w_ready, 3)
                        for j in range(4):
                            for n in range(4):
                                sl = slice(n * BANK, (n + 1) * BANK)
                                act.wait_ge(qkv_ready, 4 * j + n + 1)
                                src = (acc_p if j % 2 == 0 else lg)[:, n, :]
                                if j == 0:
                                    ins = nc.scalar.activation(qkT[:, 0, sl], src, ACT.Identity, bias=bqs[:, 0:1], scale=SCALE1)
                                elif j == 1:
                                    ins = nc.scalar.activation(qkT[:, 1, sl], src, ACT.Identity, bias=cols[:, COL["b1k"]:COL["b1k"] + 1])
                                elif j == 2:
                                    ins = nc.scalar.activation(vT[:, sl], src, ACT.Identity, bias=cols[:, COL["b1v"]:COL["b1v"] + 1])
                                else:
                                    ins = nc.scalar.activation(gate[:, sl], src, ACT.Sigmoid, bias=cols[:, COL["bgate"]:COL["bgate"] + 1])
                                ins.then_inc(qkv_out, 1)
                        act.sem_inc(z_copied, 2)
                        nc.scalar.preload_act_table(ACT.Exp)

                        def load_xt(t, k):
                            cols_of = slice(t * P, (t + 1) * P) if isinstance(t, int) else bass.ds(t * P, P)
                            nc.scalar.activation(xth[:, k, :], xh[:, cols_of].bitcast(F32), ACT.Copy)
                            nc.scalar.activation(xtl[:, k, :], xl[:, cols_of].bitcast(F32), ACT.Copy).then_inc(xt_ready, 1)

                        def copy_out(u, v):
                            act.wait_ge(lg_ready, u + 1)
                            act.wait_ge(xd, u + 1)
                            nc.scalar.activation(zflat(v), lg_half(v), ACT.Copy).then_inc(z_copied, 1)
                            if v % 2:
                                t = u // 2 if isinstance(u, int) else tile_index(u, v)
                                nc.scalar.activation(xs[:, v // 2, :], tile_of(xn, t), ACT.Copy).then_inc(xs_ready, 1)

                        def expo(u, v):
                            act.wait_ge(zs, u + 1)
                            nc.scalar.activation(zhalf(v), zhalf(v), ACT.Exp).then_inc(ex, 1)

                        def step(u, v):
                            copy_out(u + 2, (v + 2) % 4) if at_most(u + 2) else None
                            expo(u + 1, (v + 1) % 4) if at_most(u + 1) else None
                            if v % 2 == 0 and at_most(u + 4):
                                act.wait_ge(lg_ready, u + 2)
                                load_xt(tile_index(u, v) + 2, v // 2)

                        act.wait_ge(xl_ready, 4)
                        load_xt(0, 0)
                        load_xt(1, 1)
                        act.wait_ge(ph_ready, 2)
                        copy_out(0, 0)
                        copy_out(1, 1)
                        expo(0, 0)
                        all_halves(act, step)
                        act.wait_ge(w_sub, 1)
                        nc.scalar.activation(wb[:, :], wb[:, :], ACT.Exp).then_inc(w_exp, 1)
                        for n in range(2):
                            act.wait_ge(bT_tr, n + 1)
                            nc.scalar.activation(bT[:, 8 * n:8 * n + 8, :].rearrange("p t q -> p (t q)"),
                                                 acc_p[:, 2 + n, :].bitcast(BF16), ACT.Copy).then_inc(bT_out, 1)
                        act.wait_ge(cen2, 1)
                        nc.scalar.activation(XT0, X2, ACT.Square).then_inc(sq2, 1)
                        act.wait_ge(nrm2, 1)
                        nc.scalar.activation(X2, X2, ACT.Tanh).then_inc(tanhed, 1)
                        for n in range(4):
                            act.wait_ge(slot_tr2, n + 1)
                            nc.scalar.activation(Z[:, 0, n * BANK:(n + 1) * BANK], acc_p[:, n, :], ACT.Copy).then_inc(xt_out, 1)
                        act.wait_ge(sc_sub, 1)
                        nc.scalar.activation(sc[:, :, :], sc[:, :, :], ACT.Exp).then_inc(sc_exp, 1)
                        act.wait_ge(y_prod, 4)

                        def exp_b(c, k):
                            for n in range(4):
                                act.wait_ge(lgb_ready, 4 * c + n + 1)
                                act.wait_ge(yb_ready, c + 1) if n == 0 else None
                                nc.scalar.activation(E[k][:, 4 * n:4 * n + 4, :].rearrange("p j q -> p (j q)"), lgb(n), ACT.Exp).then_inc(exb, 1)

                        def y_copy(c, k):
                            act.wait_ge(yb_ready, c + 3)
                            dst = g_ffn[:, 2 * c:2 * c + 2, :] if isinstance(c, int) else g_ffn[:, bass.ds(2 * c, 2), :]
                            nc.scalar.activation(dst, y_p(k).rearrange("p (j d) -> p j d", j=2), ACT.Copy).then_inc(yb_out, 1)

                        exp_b(0, 0)
                        with act.Fori(0, NC // 2 - 1) as i:
                            for k in range(2):
                                c = 2 * i + k
                                exp_b(c + 1, 1 - k)
                                y_copy(c, k)
                        exp_b(NC - 1, 1)
                        y_copy(NC - 2, 0)
                        y_copy(NC - 1, 1)
                        act.wait_ge(yb_out, NC + 2)
                        nc.scalar.activation(g_ffn[:, :, :], g_ffn[:, :, :], ACT.Silu).then_inc(silu2, 1)

                    @block.vector
                    def _(dve):
                        link = Chain(dve, dve_seq)
                        dve.wait_ge(silu1, 1)
                        link(nc.vector.tensor_tensor(g_ffn[:, :, :], g_ffn[:, :, :], s_att[:, :, :], ALU.mult))
                        link(nc.vector.tensor_tensor(x_res[:, :, :], x_res[:, :, :], g_ffn[:, :, :], ALU.add))
                        nc.vector.tensor_reduce(mean[:, :], x_res[:, :, :], AX.X, ALU.add).then_inc(x1_ready, 1)
                        dve.wait_ge(x1_ready, 1)
                        link(nc.vector.tensor_scalar(mean[:, :], mean[:, :], 1.0 / D, None, ALU.mult))
                        nc.vector.tensor_tensor(xn[:, :, :], x_res[:, :, :], over_d(mean), ALU.subtract).then_inc(centered, 1)
                        dve.wait_ge(loaded, 96)
                        nc.vector.tensor_scalar(bqs[:, :], cols[:, COL["b1q"]:COL["b1q"] + 1], SCALE1, None, ALU.mult).then_inc(w_ready, 1)
                        PBr, part, mid = Z[96:99, 1, :], tmpb[96:99, 0, :], tmpb[96:99, 1, :]
                        link(nc.vector.tensor_copy(part, PBr))
                        dve.wait_ge(consts, 3)
                        link(nc.vector.tensor_scalar(rows[96:99, :], part, rowsel[96:99, 0:1], None, ALU.mult))
                        link(nc.vector.tensor_tensor(PBr, PBr, part, ALU.subtract))
                        link(nc.vector.tensor_copy(part, PBr))
                        link(nc.vector.tensor_scalar(mid, part, rowsel[96:99, 1:2], None, ALU.mult))
                        link(nc.vector.tensor_tensor(rows[96:99, :], rows[96:99, :], mid, ALU.add))
                        link(nc.vector.tensor_tensor(PBr, PBr, part, ALU.subtract))
                        link(nc.vector.tensor_copy(part, PBr))
                        link(nc.vector.tensor_scalar(mid, part, rowsel[96:99, 2:3], None, ALU.mult))
                        nc.vector.tensor_tensor(rows[96:99, :], rows[96:99, :], mid, ALU.add).then_inc(ph_ready, 1)
                        dve.wait_ge(squared, 1)
                        link(nc.vector.tensor_reduce(var[:, :], sq, AX.X, ALU.add))
                        nc.vector.tensor_scalar(var[:, :], var[:, :], 1.0 / D, EPS, ALU.mult, ALU.add).then_inc(var_ready, 1)
                        dve.wait_ge(rstd_ready, 1)
                        nc.vector.tensor_tensor(xn[:, :, :], xn[:, :, :], over_d(rstd), ALU.mult).then_inc(normed, 1)
                        dve.wait_ge(w_ready, 2)
                        nc.vector.tensor_tensor(wl[:, :, :], wraw[:, :, :], wh[:, :, :].bitcast(F32), ALU.subtract).then_inc(w_ready, 1)
                        for n in range(4):
                            dve.wait_ge(xh_ready, n + 1)
                            sl = slice(n * BANK, (n + 1) * BANK)
                            nc.vector.tensor_tensor(xl[:, sl], lg[:, n, :], xh[:, sl].bitcast(F32), ALU.subtract).then_inc(xl_ready, 1)

                        def maxima(u, v):
                            dve.wait_ge(z_copied, u + 3)
                            nc.vector.tensor_reduce(part_of(am, v), zhalf(v), AX.X, ALU.max)
                            t = tile_index(u, v)
                            bh = bm[:, t, v % 2, :] if isinstance(t, int) else bm[:, bass.ds(t, 1), v % 2, :].squeeze(1)
                            nc.vector.tensor_reduce(bh, zhalf(v).rearrange("p n s -> p s n"), AX.X, ALU.max).then_inc(mx, 1)

                        def sums(u, v):
                            dve.wait_ge(ex, u + 1)
                            nc.vector.tensor_reduce(part_of(sr, v), zhalf(v), AX.X, ALU.add).then_inc(sm, 1)
                            dve.wait_ge(sm, u + 1)
                            nc.vector.reciprocal(part_of(sr, v), part_of(sr, v)).then_inc(si, 1)

                        def step(u, v):
                            maxima(u + 1, (v + 1) % 4) if at_most(u + 1) else None
                            sums(u, v)

                        maxima(0, 0)
                        all_halves(dve, step)

                        dve.wait_ge(xd, 2 * NT + 4)
                        for n in range(4):
                            nc.vector.tensor_scalar(Z[:, 0, n * BANK:(n + 1) * BANK], acc_p[:, n, :], -33000.0, 65000.0, ALU.max, ALU.min).then_inc(clipped, 1)
                        bn, bres = bm[:, :, 0, :], bm[:, :, 1, :]
                        link(nc.vector.tensor_tensor(bn, bn, bres, ALU.max))
                        link(nc.vector.tensor_scalar(brow[:, :, 0:SLOTS], bn, -1.0, None, ALU.mult))
                        link(nc.vector.scalar_tensor_tensor(bres, bn, -1.0, brow[:, :, 0:SLOTS], ALU.mult, ALU.subtract))
                        link(nc.vector.tensor_copy(brow[:, :, SLOTS:2 * SLOTS], bres))
                        link(nc.vector.tensor_tensor(bres, bres, brow[:, :, SLOTS:2 * SLOTS], ALU.subtract))
                        nc.vector.tensor_copy(brow[:, :, 2 * SLOTS:3 * SLOTS], bres).then_inc(br_ready, 1)
                        for s in range(NS):
                            i0, n = BIAS_START[s], len(MEMBERS[s])
                            last = nc.vector.tensor_reduce(mb[:, s:s + 1], pb[:, i0:i0 + n], AX.X, ALU.max)
                        link(last)
                        for s in range(NS):
                            i0, n = BIAS_START[s], len(MEMBERS[s])
                            last = nc.vector.tensor_scalar(wb[:, i0:i0 + n], pb[:, i0:i0 + n], mb[:, s:s + 1], None, ALU.subtract)
                        last.then_inc(w_sub, 1)

                        mine = list(QK_DVE)
                        theirs = list(enumerate(QK_POOL))

                        def own_scores():
                            if mine:
                                s = mine.pop(0)
                                off = OFFS[s]
                                w = SEQ - off
                                link(nc.vector.tensor_tensor(prod[:, 1, :, 0:w], q[:, :, off:SEQ], kp[:, :, PAD:PAD + w], ALU.mult))
                                link(nc.vector.tensor_reduce(sc[:, s, off:SEQ], prod[:, 1, :, 0:w].rearrange("p d n -> p n d"), AX.X, ALU.add))

                        def pool_scores():
                            if theirs:
                                n, s = theirs.pop(0)
                                off = OFFS[s]
                                w = SEQ - off
                                dve.wait_ge(qk_prod, n + 1)
                                nc.vector.tensor_reduce(sc[:, s, off:SEQ], prod[:, 0, :, 0:w].rearrange("p d n -> p n d"), AX.X, ALU.add).then_inc(qk_red, 1)

                        dve.wait_ge(qkv_back, 16 * 3 * BATCH)
                        link(nc.vector.memset(sc[:, :, :], 0.0))
                        pool_scores()
                        dve.wait_ge(slot_tr, 4)
                        lgj = lg[:, :, :].rearrange("p b (j d) -> p (b j) d", d=D)
                        link(nc.vector.tensor_reduce(mean2[:, :], lgj, AX.X, ALU.add))
                        link(nc.vector.tensor_scalar(mean2[:, :], mean2[:, :], 1.0 / D, None, ALU.mult))
                        nc.vector.tensor_tensor(X2, lgj, over_d(mean2), ALU.subtract).then_inc(cen2, 1)
                        own_scores()
                        dve.wait_ge(sq2, 1)
                        link(nc.vector.tensor_reduce(var2[:, :], XT0, AX.X, ALU.add))
                        nc.vector.tensor_scalar(var2[:, :], var2[:, :], 1.0 / D, EPS, ALU.mult, ALU.add).then_inc(var2_ready, 1)
                        pool_scores()
                        own_scores()
                        pool_scores()
                        dve.wait_ge(rstd2_ready, 1)
                        nc.vector.tensor_tensor(X2, X2, over_d(rstd2), ALU.mult).then_inc(nrm2, 1)
                        while mine or theirs:
                            own_scores()
                            pool_scores()
                        dve.wait_ge(w_exp, 1)
                        for s in range(NS):
                            i0, n = BIAS_START[s], len(MEMBERS[s])
                            last = nc.vector.tensor_reduce(W[:, s:s + 1], wb[:, i0:i0 + n], AX.X, ALU.add)
                        last.then_inc(qk_red, 1)
                        dve.wait_ge(qk_red, len(QK_POOL) + 1)
                        link(nc.vector.tensor_tensor(sc[:, :, :], sc[:, :, :], over_n(mb), ALU.add))
                        link(nc.vector.tensor_reduce(m[:, :], sc[:, :, :].rearrange("p s n -> p n s"), AX.X, ALU.max))
                        nc.vector.tensor_tensor(sc[:, :, :], sc[:, :, :], over_s(m), ALU.subtract).then_inc(sc_sub, 1)
                        dve.wait_ge(eb_loaded, 16 * XPT)
                        for n in range(4):
                            dve.wait_ge(y_prod, n + 1)
                            Yn = Y[:, 4 * n:4 * n + 4, :].rearrange("p t d -> p (t d)")
                            nc.vector.tensor_tensor(Yn, lg[:, n, :], Yn, ALU.add).then_inc(y_ready, 1)
                        dve.wait_ge(sc_exp, 1)
                        nc.vector.tensor_tensor(sc[:, :, :], sc[:, :, :], over_n(W), ALU.mult).then_inc(sc_ready, 1)
                        dve.wait_ge(sc_ready, 1)
                        link(nc.vector.tensor_reduce(den[:, :], sc[:, :, :].rearrange("p s n -> p n s"), AX.X, ALU.add))
                        link(nc.vector.reciprocal(den[:, :], den[:, :]))
                        dve.sem_inc(pv_add, 1)
                        nc.vector.memset(acc[:, :, :], 0.0).then_inc(pv_add, 1)

                        def add_pv(t, k):
                            dve.wait_ge(pv_prod, t + 1)
                            dve.wait_ge(pv_add, t + 2)
                            nc.vector.tensor_tensor(acc[:, :, :], acc[:, :, :], prod[:, k, :, :], ALU.add).then_inc(pv_add, 1)

                        with dve.Fori(0, NC // 2) as i:
                            for k in range(2):
                                c = 2 * i + k
                                dve.wait_ge(exb, 4 * c + 4)
                                nc.vector.tensor_reduce(esum[:, k, :], E[k].rearrange("p j q -> p q j"), AX.X, ALU.add).then_inc(sum_ready, 1)
                                add_pv(2 * c, 0)
                                dve.wait_ge(den_ready, c + 1)
                                nc.vector.reciprocal(inv[:, k, :], den_p).then_inc(inv_ready, 1)
                                dve.wait_ge(inv_ready, c + 2)
                                for n in range(4):
                                    part = E[k][:, 4 * n:4 * n + 4, :]
                                    nc.vector.tensor_tensor(part, part, inv[:, k, :].unsqueeze(1).broadcast_to([P, 4, CH]), ALU.mult).then_inc(ct, 1)
                                add_pv(2 * c + 1, 1)
                        dve.wait_ge(pv_add, NT + 2)
                        nc.vector.tensor_tensor(acc[:, :, :], acc[:, :, :], den[:, :].unsqueeze(1).broadcast_to([P, HD, SEQ]), ALU.mult).then_inc(att_ready, 1)
                        dve.wait_ge(att_back, 16 * BATCH)
                        nc.vector.tensor_tensor(attT, attT, gate[:, :].rearrange("p (b n) -> p b n", b=BATCH), ALU.mult).then_inc(gated, 1)
                        dve.wait_ge(silu2, 1)
                        for n in range(4):
                            dve.wait_ge(proj, n + 1)
                            sl = slice(4 * n, 4 * n + 4)
                            link(nc.vector.tensor_tensor(s2[:, sl, :], lg[:, n, :].rearrange("p (j d) -> p j d", j=4), b_out.unsqueeze(1).broadcast_to([P, 4, D]), ALU.add))
                            link(nc.vector.tensor_tensor(s2[:, sl, :], s2[:, sl, :], g_ffn[:, sl, :], ALU.mult))
                            nc.vector.tensor_tensor(x_res[:, sl, :], x_res[:, sl, :], s2[:, sl, :], ALU.add).then_inc(fin, 1)

                    @block.tensor
                    def _(pe):
                        pe.wait_ge(normed, 1)
                        for t in range(NT):
                            last = nc.tensor.transpose(lg[:, t // 4, (t % 4) * P:(t % 4 + 1) * P], xn[:, t, :], ident[:, :])
                            if t % 4 == 3:
                                last.then_inc(xT_ready, 1)
                        pe.wait_ge(w_ready, 3)
                        for j in range(4):
                            for n in range(4):
                                sl = slice(n * BANK, (n + 1) * BANK)
                                pe.wait_ge(xl_ready, n + 1)
                                if j >= 2:
                                    pe.wait_ge(qkv_out, 4 * (j - 2) + n + 1)
                                dst = (acc_p if j % 2 == 0 else lg)[:, n, :]
                                if j == 1:
                                    pe.wait_ge(xl_ready, 4)
                                nc.tensor.matmul(dst, wh[:, j, :], xh[:, sl], start=True, stop=False)
                                nc.tensor.matmul(dst, wh[:, j, :], xl[:, sl], start=False, stop=False)
                                nc.tensor.matmul(dst, wl[:, j, :], xh[:, sl], start=False, stop=True).then_inc(qkv_ready, 1)
                        pe.wait_ge(ph_ready, 2)
                        pe.wait_ge(qkv_out, 12)
                        for n in range(4):
                            nc.tensor.matmul(acc_p[:, n, :], zero[:, :], rows[:, n * BANK:(n + 1) * BANK], start=True, stop=True, skip_group_check=True)
                        pe.wait_ge(ph_ready, 2)
                        pe.wait_ge(qkv_out, 16)
                        pe.sem_inc(xd, 4)

                        def logits(u, v):
                            if v % 2 == 0:
                                pe.wait_ge(xt_ready, tile_index(u, v) + 1)
                            pe.wait_ge(z_copied, u + 1)
                            k = v // 2
                            for n in (2 * (v % 2), 2 * (v % 2) + 1):
                                sl = slice(n * BANK, (n + 1) * BANK)
                                nc.tensor.matmul(lg[:, n, :], xth[:, k, :], ph[:, sl], start=True, stop=False)
                                nc.tensor.matmul(lg[:, n, :], xth[:, k, :], pl[:, sl], start=False, stop=False)
                                nc.tensor.matmul(lg[:, n, :], xtl[:, k, :], ph[:, sl], start=False, stop=False)
                                last = nc.tensor.matmul(lg[:, n, :], onerow[:, :], rows[:, sl], start=False, stop=True)
                            last.then_inc(lg_ready, 1)

                        def slot_inputs(u, v):
                            if v % 2 == 0:
                                pe.wait_ge(xs_ready, tile_index(u, v) + 1)
                            pe.wait_ge(dn, u + 1)
                            k = v // 2
                            for n in (2 * (v % 2), 2 * (v % 2) + 1):
                                last = nc.tensor.matmul(acc_p[:, n, :], xs[:, k, :], Z[:, k, n * BANK:(n + 1) * BANK], start=False, stop=True, skip_group_check=True)
                            last.then_inc(xd, 1)

                        def step(u, v):
                            logits(u + 3, (v + 3) % 4) if at_most(u + 3) else None
                            slot_inputs(u, v)

                        for u in range(3):
                            logits(u, u)
                        all_halves(pe, step)

                        pe.wait_ge(z_copied, 2 * NT + 2)
                        for j in range(NPT):
                            if j % 4 == 0:
                                pe.wait_ge(clipped, j // 4 + 1)
                            last = nc.tensor.transpose(lg[:, j // 4, (j % 4) * P:(j % 4 + 1) * P], Z[:, 0, j * P:(j + 1) * P], ident[:, :])
                            last.then_inc(slot_tr, 1) if j % 4 == 3 else None
                        pe.wait_ge(br_ready, 1)
                        for n in range(2):
                            bank = acc_p[:, 2 + n, :].bitcast(BF16)
                            for t in range(8):
                                last = nc.tensor.transpose(bank[:, t * P:(t + 1) * P], brow[:, 8 * n + t, :], identb[:, :])
                            last.then_inc(bT_tr, 1)
                        pe.wait_ge(tanhed, 1)
                        pe.wait_ge(bT_out, 2)
                        for j in range(NPT):
                            last = nc.tensor.transpose(acc_p[:, j // 4, (j % 4) * P:(j % 4 + 1) * P], X2[:, j, :], ident[:, :])
                            last.then_inc(slot_tr2, 1) if j % 4 == 3 else None
                        pe.wait_ge(ew_loaded, 16)
                        for j in range(NPT):
                            if j % 4 == 0:
                                pe.wait_ge(xt_out, j // 4 + 1)
                            for g in range(XPT):
                                last = nc.tensor.matmul(lg[g * SLOTS:(g + 1) * SLOTS, j // 4, (j % 4) * HOUT:(j % 4 + 1) * HOUT],
                                                        XT0[:, j, g * SLOTS:(g + 1) * SLOTS], ew[:, XPT * j + g, :], start=True, stop=True,
                                                        tile_position=(0, g * SLOTS))
                            last.then_inc(y_prod, 1) if j % 4 == 3 else None
                        pe.wait_ge(y_ready, 4)

                        def logits_b(c, k):
                            tokens = slice(c * CH, (c + 1) * CH) if isinstance(c, int) else bass.ds(c * CH, CH)
                            bt = (bT[:, 2 * c:2 * c + 2, :] if isinstance(c, int) else bT[:, bass.ds(2 * c, 2), :]).rearrange("p t q -> p (t q)")
                            for n in range(4):
                                if not isinstance(c, int) or c > 0 or n >= 2:
                                    pe.wait_ge(exb, 4 * c + n - 1)
                                for j in range(4):
                                    sl = slice((4 * n + j) * P, (4 * n + j + 1) * P)
                                    dst = lgb(n)[:, j * CH:(j + 1) * CH]
                                    nc.tensor.matmul(dst, ph[:, sl], xh[:, tokens], start=True, stop=False)
                                    nc.tensor.matmul(dst, ph[:, sl], xl[:, tokens], start=False, stop=False)
                                    nc.tensor.matmul(dst, pl[:, sl], xh[:, tokens], start=False, stop=False)
                                    last = nc.tensor.matmul(dst, rows[:, sl], bt, start=False, stop=True)
                                last.then_inc(lgb_ready, 1)

                        def denominators(c, k):
                            pe.wait_ge(sum_ready, c + 1)
                            pe.wait_ge(inv_ready, c + 1)
                            nc.tensor.matmul(den_p, same_slot[:, :, :].rearrange("p g s -> p (g s)"), esum[:, k, :], start=True, stop=True).then_inc(den_ready, 1)

                        def outputs(c, k):
                            pe.wait_ge(yb_out, c + 1)
                            pe.wait_ge(ct, 4 * c + 4)
                            for t in range(2):
                                for jj in range(NPT):
                                    last = nc.tensor.matmul(y_p(k)[:, t * D:(t + 1) * D], E[k][:, jj, t * P:(t + 1) * P], Y[:, jj, :], start=jj == 0, stop=jj == NPT - 1)
                            last.then_inc(yb_ready, 1)

                        pe.sem_inc(inv_ready, 1)
                        pe.sem_inc(yb_out, 2)
                        pe.sem_inc(yb_ready, 2)
                        logits_b(0, 0)
                        with pe.Fori(0, NC // 2 - 1) as i:
                            for k in range(2):
                                c = 2 * i + k
                                denominators(c, k)
                                logits_b(c + 1, 1 - k)
                                outputs(c, k)
                        denominators(NC - 2, 0)
                        logits_b(NC - 1, 1)
                        outputs(NC - 2, 0)
                        denominators(NC - 1, 1)
                        outputs(NC - 1, 1)
                        pe.wait_ge(gated, 1)
                        pe.wait_ge(wout_loaded, 32)
                        for t in range(NT):
                            last = nc.tensor.matmul(lg[:, t // 4, (t % 4) * D:(t % 4 + 1) * D], attT[:, t // 2, (t % 2) * P:(t % 2 + 1) * P], wout, start=True, stop=True)
                            last.then_inc(proj, 1) if t % 4 == 3 else None

        def finish(t):
            with nc.semaphore("dbg") as s, nc.Block() as block:
                @block.sync
                def _(sp):
                    sp.dma_start(tiles(out), t).then_inc(s, 16)
                    sp.wait_ge(s, 16)

        front_block(0)
        if STAGE == "xn":
            return finish(xn[:, :, :])
        with ExitStack() as c:
            wroute, fw = sb("wroute", [P, NE], c=c), sb("fw", [P, NT, NE], c=c)
            wgu, wd = sb("wgu", [P, NE, 2 * FF], c=c), sb("wd", [P, NE, 2, D], c=c)
            wh, wl = (sb(n, [P, NE, 2 * FF], F32R, c=c) for n in ("wh", "wl"))
            xh, xl = (sb(n, [P, TOK], F32R, c=c) for n in ("x0h", "x0l"))
            with nc.semaphore("ffn_loaded") as fl, nc.semaphore("split") as split, nc.Block() as block:
                @block.sync
                def _(sp):
                    sp.dma_start(wroute[:, :], a["router"]).then_inc(fl, 16)
                    sp.dma_start(wgu[:, :, 0:FF], a["gating"].rearrange("e d f -> d e f")).then_inc(fl, 16)
                    sp.dma_start(wgu[:, :, FF:2 * FF], a["up"].rearrange("e d f -> d e f")).then_inc(fl, 16)
                    sp.dma_start(wd[:, :, :, :], a["down"].rearrange("e (c p) d -> p e c d", p=P)).then_inc(fl, 16)
                    sp.wait_ge(fl, 64)

                @block.gpsimd
                def _(pool):
                    link = Chain(pool, split)
                    link(nc.gpsimd.tensor_copy(xh[:, :], xnT[:, :]))
                    nc.gpsimd.tensor_tensor(xl[:, :], xnT[:, :], xh[:, :].bitcast(F32), ALU.subtract)
                    pool.wait_ge(fl, 64)
                    link(nc.gpsimd.tensor_copy(wh[:, :, :], wgu[:, :, :]))
                    nc.gpsimd.tensor_tensor(wl[:, :, :], wgu[:, :, :], wh[:, :, :].bitcast(F32), ALU.subtract)
            router_block(wroute, fw)
            attention0_block()
            if STAGE == "s0":
                return finish(s_att[:, :, :])
            experts0_block(fw, xh, xl, wh, wl, wd)
            if STAGE == "g0":
                return finish(g_ffn[:, :, :])
        layer1_block()


def kernel(L0_attn_hidden_states, L0_attn_Wq, L0_attn_bq, L0_attn_Wk, L0_attn_bk, L0_attn_Wv, L0_attn_bv, L0_attn_Wo,
           L0_attn_bo, L0_ffn_kernel_router_DE, L0_ffn_kernel_gating_EDF, L0_ffn_kernel_up_EDF, L0_ffn_kernel_down_EFD,
           L1_attn_w_qkv, L1_attn_b_qkv, L1_attn_w_out, L1_attn_b_out, L1_attn_w_gate, L1_attn_b_gate, L1_attn_pos_bias,
           L1_ffn_phi_w, L1_ffn_phi_b, L1_ffn_expert_w, L1_ffn_expert_b):
    import numpy as np
    import concourse.bacc as bacc
    from concourse.bass_utils import run_bass_kernel_spmd

    lay = lambda v: np.ascontiguousarray(v)
    halves = lambda v: list(np.asarray(v).reshape(-1, P))
    arrays = {
        "x": lay(np.asarray(L0_attn_hidden_states).reshape(TOK, D)),
        "wq": lay(L0_attn_Wq), "wk": lay(L0_attn_Wk), "wv": lay(L0_attn_Wv), "woT": lay(np.asarray(L0_attn_Wo).T),
        "bo": lay(np.asarray(L0_attn_bo).reshape(1, D)),
        "router": lay(L0_ffn_kernel_router_DE), "gating": lay(L0_ffn_kernel_gating_EDF),
        "up": lay(L0_ffn_kernel_up_EDF), "down": lay(L0_ffn_kernel_down_EFD),
        "w_qkv": lay(L1_attn_w_qkv), "w_gate": lay(L1_attn_w_gate), "w_out": lay(L1_attn_w_out),
        "b_out": lay(np.asarray(L1_attn_b_out).reshape(1, D)),
        "pos_bias": lay(np.tile(np.asarray(L1_attn_pos_bias)[BIAS_ORDER].T, (BATCH, 1))),
        "phiT": lay(np.asarray(L1_ffn_phi_w).T), "phi_b": lay(np.asarray(L1_ffn_phi_b).reshape(1, NP)),
        "expert_w": lay(L1_ffn_expert_w), "expert_b": lay(L1_ffn_expert_b),
        "cols": lay(np.stack(halves(L0_attn_bq) + halves(L0_attn_bk) + halves(L0_attn_bv) + halves(L1_attn_b_qkv)
                             + halves(L1_attn_b_gate), axis=1)),
    }
    arrays["starts"] = np.array([[PAD - o for o in OFFS]], np.int32)
    nc = bacc.Bacc("TRN2", target_bir_lowering=False, num_devices=1)
    args = {n: nc.dram_tensor(f"in_{n}", v.shape, mybir.dt.from_np(v.dtype), kind="ExternalInput").ap() for n, v in arrays.items()}
    out = nc.dram_tensor("out_x", (TOK, D), F32, kind="ExternalOutput").ap()
    build(nc, args, out, None)
    r = run_bass_kernel_spmd(nc, [{f"in_{n}": v for n, v in arrays.items()}], core_ids=[0])
    return r.results[0]["out_x"].reshape(BATCH, SEQ, D)
```

```python
import concourse.bass as bass
from concourse import mybir
from contextlib import ExitStack

F32 = mybir.dt.float32
BF16 = mybir.dt.bfloat16
F32R = mybir.dt.float32r
ALU = mybir.AluOpType
ACT = mybir.ActivationFunctionType
AX = mybir.AxisListType

P = 128
BATCH, SEQ, D = 8, 256, 128
TOK = BATCH * SEQ
NT = TOK // P
TPB = SEQ // P
NE, FF = 8, 256
HEADS, HD = 16, 8
NX, SLOTS, HOUT = 64, 32, 128
NP = NX * SLOTS
NPT = NP // P
XPT = P // SLOTS
BANK = 512
GT = BANK // P
GROUPS = NT // GT
LAST = slice(NT - GT, NT)
EPS = 1e-5
SCALE0 = float(D) ** -0.5
SCALE1 = float(HD) ** -0.5

ALL_OFFSETS = [(1 << j) * tau for j in range(11) for tau in range(4)]
OFFS = sorted({o for o in ALL_OFFSETS if o < SEQ})
NO = len(OFFS)
NS = NO + 1
MEMBERS = [[i for i, o in enumerate(ALL_OFFSETS) if o == off] for off in OFFS]
MEMBERS.append([i for i, o in enumerate(ALL_OFFSETS) if o >= SEQ])
BIAS_ORDER = [i for m in MEMBERS for i in m]
BIAS_START = [sum(len(m) for m in MEMBERS[:s]) for s in range(NS)]

HELPED = (0, 1, 2, 3, 4)
PV_MADE = (0, 3, 2, 2, 3, 3, 3, 0)
PV_ADDED = ((0, 0), (1, 1), (1, 1), (1, 1), (1, 2), (1, 2), (1, 3), (0, 0))
SHARED = [s for s in range(NS) if len(MEMBERS[s]) > 1]

QK_BY = ["pool", "dve", "own"] * 3 + ["pool", "dve", "dve"] + ["pool", "dve", "own", "pool"]
QK_POOL, QK_DVE, QK_OWN = ([s for s in range(NO) if QK_BY[s] == w] for w in ("pool", "dve", "own"))
DVE_ORDER = [s for pair in zip(QK_DVE[2:] + [None] * NO, QK_OWN + [None] * NO) for s in (pair[1], pair[0]) if s is not None]
DVE_ORDER = QK_DVE[:2] + DVE_ORDER
QK_SUMS = [s for s in range(NO) if QK_BY[s] != "own"]

COLS = ["bq0", "bq1", "bk0", "bk1", "bv0", "bv1", "b1q", "b1k", "b1v", "bgate"]
COL = {n: i for i, n in enumerate(COLS)}


def tiles(ap):
    return ap.rearrange("(t p) d -> p t d", p=P)


class Chain:

    def __init__(self, eng, sem):
        self.eng, self.sem, self.n = eng, sem, 0

    def __call__(self, ins):
        self.n += 1
        ins.then_inc(self.sem, 1)
        self.eng.wait_ge(self.sem, self.n)
        return self.n


def build(nc, a, out):
    ctx = ExitStack()
    with ctx:
        def sb(name, shape, dt=F32, c=None):
            return (c or ctx).enter_context(nc.sbuf_tensor(name, shape, dt))

        ident = sb("ident", [P, P])
        cols = sb("cols", [P, len(COLS)])
        x_res = sb("x_res", [P, NT, D])
        xn = sb("xn", [P, NT, D])
        xnT = sb("xnT", [P, TOK])
        s_att = sb("s_att", [P, NT, D])
        g_ffn = sb("g_ffn", [P, NT, D])
        half = sb("half", [P, 1])
        ph, pl = sb("ph", [P, NP], F32R), sb("pl", [P, NP], F32R)
        wh1, wl1 = sb("wh1", [P, 4, P], F32R), sb("wl1", [P, 4, P], F32R)
        rows = sb("rows", [P, NP], BF16)
        onerow = sb("onerow", [P, P], BF16)
        zero = sb("zero", [P, P], BF16)
        identb = sb("identb", [P, P], BF16)
        same_slot = sb("same_slot", [P, XPT, SLOTS])
        mb, W = sb("mb", [P, NS]), sb("W", [P, NS])

        def over(v, *shape):
            return v.unsqueeze(len(shape) - 1).broadcast_to(list(shape))

        l0 = {}
        POOL_WL = NE // 2

        def layer0_front(c0):
            b = c0.enter_context
            sem0 = lambda n: b(nc.semaphore(f"l0_{n}"))
            L = {n: sem0(n) for n in ("x_loaded", "gu_loaded", "small_loaded", "down_loaded")}
            T = {"wgu": sb("wgu", [P, NE, 2 * FF], c=c0), "wd": sb("wd", [P, NE, 2, D], c=c0),
                 "wh": sb("wh", [P, NE, 2 * FF], F32R, c=c0), "wl": sb("wl", [P, NE, 2 * FF], F32R, c=c0),
                 "xh": sb("x0h", [P, TOK], F32R, c=c0), "xl": sb("x0l", [P, TOK], F32R, c=c0),
                 "wroute": sb("wroute", [P, NE], c=c0), "bo": sb("bo", [P, D], c=c0)}
            for n in ("wq", "wk", "wv", "woT"):
                T[n] = sb(n, [P, 2, D], c=c0)
            for n, shape in (("Am", [P, D]), ("VO", [P, D + 1]), ("bprime", [P, D]), ("u", [P, 1]), ("bqbk", [P, 1]),
                             ("pb", [P, len(BIAS_ORDER)]), ("wb", [P, len(BIAS_ORDER)])):
                T[n] = sb(n, shape, c=c0)
            wq, wk, wv, woT, bo, pb, wb = (T[n] for n in ("wq", "wk", "wv", "woT", "bo", "pb", "wb"))
            T["yp"] = b(nc.psum_tensor("yp", [P, BANK], F32))
            T["lp"] = lp = T["yp"][:, 0:NT * NE].rearrange("p (t e) -> p t e", e=NE)
            l0.update(L=L, T=T)
            wgu, wh, wl, xh, xl = (T[n] for n in ("wgu", "wh", "wl", "xh", "xl"))
            with ExitStack() as c:
                sem = lambda n: c.enter_context(nc.semaphore(f"f0_{n}"))
                consts, dve_seq, var_ready, rstd_ready, normed, transposed, xT_ready, xh_ready, wh_ready = map(
                    sem, ("consts", "dve_seq", "var_ready", "rstd_ready", "normed", "transposed", "xT_ready", "xh_ready", "wh_ready"))
                bvb_ready, folded = map(sem, ("bvb_ready", "folded"))
                bvb, bqb = sb("bvb", [P, 2, P], c=c), sb("bqb", [P, 2, P], c=c)
                var, rstd = (sb(f"{n}0", [P, NT], c=c) for n in ("var", "rstd"))
                stats, moments = sb("stats0", [P, NT, 6], c=c), sb("moments0", [P, NT, 2], c=c)
                tp = c.enter_context(nc.psum_tensor("tp0", [P, 4, BANK], F32))
                fd = c.enter_context(nc.psum_tensor("fd0", [P, 3, BANK], F32))
                with nc.Block() as block:
                    @block.sync
                    def _(sp):
                        sp.dma_start(x_res[:, :, :], tiles(a["x"])).then_inc(L["x_loaded"], 16)
                        sp.dma_start(cols[:, :], a["cols"]).then_inc(L["x_loaded"], 16)
                        sp.dma_start(T["wroute"][:, :], a["router"]).then_inc(L["small_loaded"], 16)
                        for n in ("wq", "wk", "wv", "woT"):
                            sp.dma_start(T[n][:, :, :], a[n].rearrange("(c p) d -> p c d", p=P)).then_inc(L["small_loaded"], 16)
                        sp.dma_start(T["bo"][:, :], a["bo"].broadcast_to([P, D])).then_inc(L["small_loaded"], 16)
                        sp.dma_start(pb[:, :], a["pos_bias"]).then_inc(L["small_loaded"], 16)
                        sp.dma_start(wgu[:, :, 0:FF], a["gating"].rearrange("e d f -> d e f")).then_inc(L["gu_loaded"], 16)
                        sp.dma_start(wgu[:, :, FF:2 * FF], a["up"].rearrange("e d f -> d e f")).then_inc(L["gu_loaded"], 16)
                        sp.dma_start(T["wd"][:, :, :, :], a["down"].rearrange("e (c p) d -> p e c d", p=P)).then_inc(L["down_loaded"], 16)

                    @block.gpsimd
                    def _(pool):
                        nc.gpsimd.memset(half[:, :], -0.5).then_inc(consts, 1)
                        nc.gpsimd.memset(ident[:, :], 0.0).then_inc(consts, 1)
                        pool.wait_ge(consts, 2)
                        nc.gpsimd.affine_select(out=ident[:, :], in_=ident[:, :], compare_op=ALU.not_equal, fill=1.0,
                                                base=0, pattern=[[-1, P]], channel_multiplier=1).then_inc(consts, 1)
                        pool.wait_ge(consts, 3)
                        pool.wait_ge(L["x_loaded"], 32)
                        for n in range(2):
                            nc.gpsimd.tensor_copy(bvb[:, n, :], cols[:, COL["bv0"] + n:COL["bv0"] + n + 1].to_broadcast([P, P])).then_inc(bvb_ready, 1)
                            nc.gpsimd.tensor_copy(bqb[:, n, :], cols[:, COL["bq0"] + n:COL["bq0"] + n + 1].to_broadcast([P, P])).then_inc(bvb_ready, 1)
                        pool.wait_ge(var_ready, 1)
                        nc.gpsimd.tensor_tensor(rstd[:, :], var[:, :], half[:, 0:1].to_broadcast([P, NT]), ALU.pow).then_inc(rstd_ready, 1)
                        pool.wait_ge(wh_ready, 1)
                        ex = slice(0, POOL_WL)
                        nc.gpsimd.tensor_tensor(wl[:, ex, :], wgu[:, ex, :], wh[:, ex, :].bitcast(F32), ALU.subtract)

                    @block.vector
                    def _(dve):
                        link = Chain(dve, dve_seq)
                        dve.wait_ge(L["x_loaded"], 32)
                        for t in range(NT):
                            last = nc.vector.bn_stats(stats[:, t, :], x_res[:, t, :])
                        link(last)
                        for t in range(NT):
                            last = nc.vector.bn_aggr(moments[:, t, :], stats[:, t, :])
                        link(last)
                        nc.vector.tensor_scalar(var[:, :], moments[:, :, 1], EPS, None, ALU.add).then_inc(var_ready, 1)
                        dve.wait_ge(folded, 1)
                        nc.vector.tensor_tensor(T["bprime"][:, :], fd[:, 2, 0:D], bo[:, :], ALU.add)
                        for s in range(NS):
                            i0, n = BIAS_START[s], len(MEMBERS[s])
                            last = nc.vector.tensor_reduce(mb[:, s:s + 1], pb[:, i0:i0 + n], AX.X, ALU.max)
                        link(last)
                        dve.wait_ge(rstd_ready, 1)
                        for t in range(NT):
                            last = nc.vector.tensor_scalar(xn[:, t, :], x_res[:, t, :], moments[:, t, 0:1], rstd[:, t:t + 1], ALU.subtract, ALU.mult)
                            last.then_inc(normed, 1) if t % 4 == 3 else None
                        for n in range(4):
                            sl = slice(n * BANK, (n + 1) * BANK)
                            dve.wait_ge(xh_ready, n + 1)
                            nc.vector.tensor_tensor(xl[:, sl], xnT[:, sl], xh[:, sl].bitcast(F32), ALU.subtract)
                        dve.wait_ge(wh_ready, 1)
                        ex = slice(POOL_WL, NE)
                        nc.vector.tensor_tensor(wl[:, ex, :], wgu[:, ex, :], wh[:, ex, :].bitcast(F32), ALU.subtract)

                    @block.scalar
                    def _(act):
                        act.wait_ge(folded, 1)
                        nc.scalar.activation(T["Am"][:, :], fd[:, 0, 0:D], ACT.Copy)
                        nc.scalar.activation(T["VO"][:, 0:D], fd[:, 0, D:2 * D], ACT.Copy)
                        nc.scalar.activation(T["u"][:, :], fd[:, 1, 0:1], ACT.Copy)
                        nc.scalar.activation(T["VO"][:, D:D + 1], fd[:, 1, 1:2], ACT.Copy, scale=SCALE0)
                        nc.scalar.activation(T["bqbk"][:, :], fd[:, 1, 2:3], ACT.Copy, scale=SCALE0)
                        act.wait_ge(L["gu_loaded"], 32)
                        nc.scalar.activation(wh[:, :, :], wgu[:, :, :], ACT.Copy).then_inc(wh_ready, 1)
                        for n in range(4):
                            sl = slice(n * BANK, (n + 1) * BANK)
                            act.wait_ge(transposed, n + 1)
                            nc.scalar.activation(xnT[:, sl], tp[:, n, :], ACT.Copy).then_inc(xT_ready, 1)
                            act.wait_ge(xT_ready, n + 1)
                            nc.scalar.activation(xh[:, sl], xnT[:, sl], ACT.Copy).then_inc(xh_ready, 1)

                    @block.tensor
                    def _(pe):
                        pe.wait_ge(L["small_loaded"], 112)
                        pe.wait_ge(bvb_ready, 4)
                        col = lambda name, n: cols[:, COL[name] + n:COL[name] + n + 1]
                        for dst, left, right in ((fd[:, 0, 0:D], lambda n: wq[:, n, :], lambda n: wk[:, n, :]),
                                                 (fd[:, 0, D:2 * D], lambda n: wv[:, n, :], lambda n: woT[:, n, :]),
                                                 (fd[:, 2, 0:D], lambda n: bvb[:, n, :], lambda n: woT[:, n, :]),
                                                 (fd[:, 1, 0:1], lambda n: wk[:, n, :], lambda n: col("bq0", n)),
                                                 (fd[:, 1, 1:2], lambda n: wq[:, n, :], lambda n: col("bk0", n)),
                                                 (fd[:, 1, 2:3], lambda n: bqb[:, n, :], lambda n: col("bk0", n))):
                            for n in range(2):
                                last = nc.tensor.matmul(dst, left(n), right(n), start=n == 0, stop=n == 1)
                        last.then_inc(folded, 1)
                        pe.wait_ge(consts, 3)
                        for t in range(NT):
                            pe.wait_ge(normed, t // 4 + 1) if t % 4 == 0 else None
                            last = nc.tensor.transpose(tp[:, t // 4, (t % 4) * P:(t % 4 + 1) * P], xn[:, t, :], ident[:, :])
                            last.then_inc(transposed, 1) if t % 4 == 3 else None
                        for t in range(NT):
                            pe.wait_ge(xT_ready, t // 4 + 1) if t % 4 == 0 else None
                            nc.tensor.matmul(lp[:, t, :], xnT[:, t * P:(t + 1) * P], T["wroute"][:, :], start=True, stop=True)

        def layer0_main(c0):
            L, T = l0["L"], l0["T"]
            wgu, wd, wh, wl, xh, xl, Am, VO, bprime, u_, bqbk, pb, wb = (
                T[n] for n in ("wgu", "wd", "wh", "wl", "xh", "xl", "Am", "VO", "bprime", "u", "bqbk", "pb", "wb"))
            UNITS = 2 * NE
            STEP_A, STEP_B, STEP_C, STEP_D = 0, 2, 4, 6
            with ExitStack() as c:
                r = lambda n, s, dt=F32: sb(f"m0_{n}", s, dt, c=c)
                sem = lambda n: c.enter_context(nc.semaphore(f"m0_{n}"))
                tri_ready, wb_ready, dve_seq, shifted, expd, p12, e2 = map(
                    sem, ("tri_ready", "wb_ready", "dve_seq", "shifted", "expd", "p12", "e2"))
                z, pr = r("z", [P, NT, NE]), r("pr", [P, NT, NE])
                m, s = r("m", [P, NT]), r("s", [P, NT])
                g_, q_ = r("g", [P, NT, NE, NE]), r("q", [P, NT, NE, NE])
                tri = r("tri", [P, NE, NE])
                rank, m1, m2, fw = (r(n, [P, NT, NE]) for n in ("rank", "m1", "m2", "fw"))
                pa, pb_, w1, w2 = (r(n, [P, NT]) for n in ("pa", "pb", "w1", "w2"))
                bc = lambda v: v[:, :].unsqueeze(2).broadcast_to([P, NT, NE])
                xt_ready, xt_used = map(sem, ("xt_ready", "xt_used"))
                qg_ready, q_out, g_out, sc_ready, mx_ready, t1_ready, nb_ready = map(
                    sem, ("qg_ready", "q_out", "g_out", "sc_ready", "mx_ready", "t1_ready", "nb_ready"))
                probs, rinv, pt_ready, pt_out, o_ready, o_out = map(sem, ("probs", "rinv", "pt_ready", "pt_out", "o_ready", "o_out"))
                xt = r("xt", [P, 2, SEQ])
                qs, G, prob, pts = r("qs", [P, 2, SEQ]), r("G", [P, 2, TPB, D]), r("prob", [P, 2, TPB, SEQ]), r("pts", [P, 2, TPB, SEQ])
                mz, cs, t1, nb, rs, ri = (r(n, [P, 2, TPB]) for n in ("mz", "cs", "t1", "nb", "rs", "ri"))
                at = c.enter_context(nc.psum_tensor("m0_at", [P, 3, BANK], F32))
                yp = T["yp"]
                lp = T["lp"]
                qp = lambda k: at[:, k, 0:SEQ]
                gp = lambda k, s: at[:, k, SEQ:SEQ + D + 1] if s == 0 else at[:, 2, k * (D + 1):(k + 1) * (D + 1)]
                sc = lambda k: at[:, k, :].rearrange("p (s t) -> p s t", s=TPB)
                pt = lambda k: at[:, k, :].rearrange("p (j s) -> p j s", j=TPB)
                op = lambda k: at[:, 2, k * TPB * D:(k + 1) * TPB * D].rearrange("p (s o) -> p s o", s=TPB)
                gu_ready, sg_ready, fu_ready, y_ready, y_added = map(sem, ("gu_ready", "sg_ready", "fu_ready", "y_ready", "y_added"))
                sg, fu = r("sg", [P, 2, BANK]), r("fu", [P, 2, 2, BANK])
                gu = c.enter_context(nc.psum_tensor("m0_gu", [P, 2, 2, BANK], F32))
                silued, added, mean_sum, mean_ready, centered, squared, var_sum, var_ready, rstd_ready = map(
                    sem, ("silued", "added", "mean_sum", "mean_ready", "centered", "squared", "var_sum", "var_ready", "rstd_ready"))
                mean, var, rstd, sq = r("mean", [P, GT]), r("var", [P, GT]), r("rstd", [P, GT]), r("sq", [P, GT, D])
                before = lambda buf, g: buf[:, bass.ds(GT * (g - 1), GT), :]
                over_g = lambda v: over(v[:, :], P, GT, D)
                l1_loaded, consts, pool_seq = map(sem, ("l1_loaded", "consts", "pool_seq"))
                raw = wgu[:, :, :].rearrange("p e f -> p (e f)")
                phi_raw, phib_raw = raw[:, 0:NP], raw[96:99, NP:2 * NP]
                w1_raw = r("w1_raw", [P, 4, P])
                part_all, mid_all = r("part", [P, NP], BF16), r("mid", [P, NP], BF16)
                part, mid = part_all[96:99, :], mid_all[96:99, :]

                with nc.Block() as block:
                    @block.sync
                    def _(sp):
                        sp.dma_start(w1_raw[:, 0:3, :], a["w_qkv"].rearrange("d (j c) -> d j c", j=3)).then_inc(l1_loaded, 16)
                        sp.dma_start(w1_raw[:, 3, :], a["w_gate"]).then_inc(l1_loaded, 16)
                        sp.dma_start(phi_raw, a["phiT"]).then_inc(l1_loaded, 16)
                        sp.dma_start(phib_raw, a["phi_b"].broadcast_to([3, NP])).then_inc(l1_loaded, 16)

                    @block.gpsimd
                    def _(pool):
                        link = Chain(pool, pool_seq)
                        link(nc.gpsimd.memset(tri[:, :, :], 1.0))
                        nc.gpsimd.affine_select(out=tri[:, :, :], in_=tri[:, :, :], compare_op=ALU.is_gt, fill=0.0, base=0,
                                                pattern=[[1, NE], [-1, NE]], channel_multiplier=0).then_inc(tri_ready, 1)
                        def load_pair(g):
                            if g > 0:
                                pool.wait_ge(xt_used, g)
                            for k in range(2):
                                nc.gpsimd.tensor_copy(xt[:, k, :], xnT[:, (2 * g + k) * SEQ:(2 * g + k + 1) * SEQ]).then_inc(xt_ready, 1)
                            pool.wait_ge(xt_ready, 2 * g + 2)

                        load_pair(0)
                        pool.wait_ge(l1_loaded, 64)
                        link(nc.gpsimd.tensor_copy(wh1[:, :, :], w1_raw[:, :, :]))
                        nc.gpsimd.tensor_tensor(wl1[:, :, :], w1_raw[:, :, :], wh1[:, :, :].bitcast(F32), ALU.subtract)
                        link(nc.gpsimd.tensor_copy(ph[:, :], phi_raw))
                        nc.gpsimd.tensor_tensor(pl[:, :], phi_raw, ph[:, :].bitcast(F32), ALU.subtract)
                        link(nc.gpsimd.memset(same_slot[:, :, :], 0.0))
                        for n in range(XPT):
                            link(nc.gpsimd.affine_select(out=same_slot[:, :, :], in_=same_slot[:, :, :], compare_op=ALU.not_equal, fill=1.0,
                                                         base=-n * SLOTS, pattern=[[0, XPT], [-1, SLOTS]], channel_multiplier=1))
                        nc.gpsimd.memset(zero[:, :], 0.0)
                        nc.gpsimd.memset(onerow[:, :], 0.0)
                        nc.gpsimd.tensor_copy(identb[:, :], ident[:, :])
                        link(nc.gpsimd.memset(rows[:, :], 0.0))
                        link(nc.gpsimd.memset(onerow[96:99, :], 1.0))
                        for n in range(3):
                            link(nc.gpsimd.affine_select(out=rows[32 * n:32 * n + 32, :], in_=rows[32 * n:32 * n + 32, :], compare_op=ALU.not_equal,
                                                         fill=1.0, base=0, pattern=[[0, NX], [1, SLOTS]], channel_multiplier=-1))

                        own = lambda n: ident[96:99, 96 + n:97 + n].to_broadcast([3, NP])

                        def phi_b_part(n):
                            link(nc.gpsimd.tensor_copy(part, phib_raw))
                            if n < 2:
                                link(nc.gpsimd.tensor_tensor(phib_raw, phib_raw, part, ALU.subtract))
                            link(nc.gpsimd.tensor_tensor(mid, part, own(n), ALU.mult))
                            link(nc.gpsimd.tensor_tensor(rows[96:99, :], rows[96:99, :], mid, ALU.add))

                        for g in range(1, GROUPS):
                            h = slice((g - 1) * GT, g * GT)
                            load_pair(g)
                            pool.wait_ge(silued, g)
                            link(nc.gpsimd.tensor_tensor(g_ffn[:, h, :], g_ffn[:, h, :], s_att[:, h, :], ALU.mult))
                            nc.gpsimd.tensor_tensor(x_res[:, h, :], x_res[:, h, :], g_ffn[:, h, :], ALU.add).then_inc(added, 1)
                            pool.wait_ge(added, g)
                            phi_b_part(g - 1)
                            pool.wait_ge(var_ready, g)
                            nc.gpsimd.tensor_tensor(rstd[:, :], var[:, :], half[:, 0:1].to_broadcast([P, GT]), ALU.pow).then_inc(rstd_ready, 1)
                            pool.wait_ge(rstd_ready, g)

                    @block.tensor
                    def _(pe):
                        pe.wait_ge(shifted, 1)
                        pe.wait_ge(L["down_loaded"], 16)

                        def group(g, first):
                            tokens = bass.ds(g * BANK, BANK)

                            def gate_up(u):
                                e, f = divmod(u, 2)
                                pe.wait_ge(fu_ready, UNITS * g + u + 1)
                                for h in range(2):
                                    w = slice(h * FF + f * P, h * FF + (f + 1) * P)
                                    nc.tensor.matmul(gu[:, u % 2, h, :], wh[:, e, w], xh[:, tokens], start=True, stop=False)
                                    nc.tensor.matmul(gu[:, u % 2, h, :], wh[:, e, w], xl[:, tokens], start=False, stop=False)
                                    last = nc.tensor.matmul(gu[:, u % 2, h, :], wl[:, e, w], xh[:, tokens], start=False, stop=True)
                                last.then_inc(gu_ready, 1)

                            def down(e):
                                pe.wait_ge(fu_ready, UNITS * g + 2 * e + 4)
                                pe.wait_ge(y_added, NE * g + e + 1)
                                for j in range(GT):
                                    for f in range(2):
                                        last = nc.tensor.matmul(yp[:, j * D:(j + 1) * D], fu[:, e % 2, f, j * P:(j + 1) * P], wd[:, e, f, :],
                                                                start=f == 0, stop=f == 1)
                                last.then_inc(y_ready, 1)

                            def attend(step, k):
                                b = 2 * g + k
                                if step == STEP_A:
                                    pe.wait_ge(xt_ready, b + 1)
                                    pe.wait_ge(pt_out, b + 1)
                                    pe.wait_ge(o_out, 2 * g + 2)
                                    nc.tensor.matmul(qp(k), Am[:, :], xt[:, k, :], start=True, stop=True)
                                    for s in range(TPB):
                                        last = nc.tensor.matmul(gp(k, s), xt[:, k, s * P:(s + 1) * P], VO[:, :], start=True, stop=True)
                                    last.then_inc(qg_ready, 1)
                                elif step == STEP_B:
                                    pe.wait_ge(q_out, b + 1)
                                    pe.wait_ge(g_out, b + 1)
                                    for s in range(TPB):
                                        last = nc.tensor.matmul(sc(k)[:, s, :], qs[:, k, s * P:(s + 1) * P], xt[:, k, :], start=True, stop=True)
                                    last.then_inc(sc_ready, 1)
                                elif step == STEP_C:
                                    pe.wait_ge(probs, 2 * b + 2)
                                    for s in range(TPB):
                                        for j in range(TPB):
                                            last = nc.tensor.transpose(pt(k)[:, j, s * P:(s + 1) * P], prob[:, k, s, j * P:(j + 1) * P], ident[:, :])
                                    last.then_inc(pt_ready, 1)
                                else:
                                    pe.wait_ge(pt_out, b + 3)
                                    pe.wait_ge(g_out, 2 * g + 2)
                                    for s in range(TPB):
                                        for j in range(TPB):
                                            last = nc.tensor.matmul(op(k)[:, s, :], pts[:, k, j, s * P:(s + 1) * P], G[:, k, j, :], start=j == 0, stop=j == TPB - 1)
                                    last.then_inc(o_ready, 1)

                            for e in range(NE):
                                gate_up(2 * e)
                                gate_up(2 * e + 1)
                                if e > 0:
                                    down(e - 1)
                                if e in (STEP_A, STEP_B, STEP_C, STEP_D):
                                    for k in range(2):
                                        attend(e, k)
                            down(NE - 1)

                        group(0, True)
                        with pe.Fori(0, GROUPS - 1) as i:
                            group(i + 1, False)

                    @block.scalar
                    def _(act):
                        act.wait_ge(shifted, 1)
                        nc.scalar.activation(pr[:, :, :], z[:, :, :], ACT.Exp).then_inc(expd, 1)
                        act.sem_inc(pt_out, 2)
                        def group(g, first):
                            for e in range(NE):
                                for u in (2 * e, 2 * e + 1):
                                    act.wait_ge(gu_ready, UNITS * g + u + 1)
                                    act.wait_ge(fu_ready, UNITS * g + u + 1)
                                    nc.scalar.activation(sg[:, u % 2, :], gu[:, u % 2, 0, :], ACT.Silu).then_inc(sg_ready, 1)
                                if first and e == 1:
                                    act.wait_ge(p12, 1)
                                    nc.scalar.activation(w2[:, :], pb_[:, :], ACT.Exp).then_inc(e2, 1)
                                if not first and e == 0:
                                    act.wait_ge(y_added, NE * g + 1)
                                    nc.scalar.activation(before(g_ffn, g), before(g_ffn, g), ACT.Silu).then_inc(silued, 1)
                                if not first and e == 4:
                                    act.wait_ge(centered, g)
                                    nc.scalar.activation(sq[:, :, :], before(xn, g), ACT.Square).then_inc(squared, 1)
                                for k in range(2):
                                    b = 2 * g + k
                                    if e == STEP_A + 1:
                                        act.wait_ge(qg_ready, 2 * g + 2)
                                        nc.scalar.activation(qs[:, k, :], qp(k), ACT.Identity, bias=u_[:, 0:1]).then_inc(q_out, 1)
                                        for s in range(TPB):
                                            nc.scalar.activation(cs[:, k, s:s + 1], gp(k, s)[:, D:D + 1], ACT.Identity, bias=bqbk[:, 0:1])
                                            last = nc.scalar.activation(G[:, k, s, :], gp(k, s)[:, 0:D], ACT.Copy)
                                        last.then_inc(g_out, 1)
                                    elif e == STEP_B + 1:
                                        act.wait_ge(nb_ready, b + 1)
                                        for s in range(TPB):
                                            nc.scalar.activation(prob[:, k, s, :], sc(k)[:, s, :], ACT.Exp, bias=nb[:, k, s:s + 1], scale=SCALE0,
                                                                 accum_out=rs[:, k, s:s + 1]).then_inc(probs, 1)
                                        if first and k == 1:
                                            act.wait_ge(wb_ready, 1)
                                            nc.scalar.activation(wb[:, :], wb[:, :], ACT.Exp).then_inc(wb_ready, 1)
                                    elif e == STEP_C + 1:
                                        act.wait_ge(pt_ready, b + 1)
                                        nc.scalar.activation(pts[:, k, :, :], pt(k), ACT.Copy).then_inc(pt_out, 1)

                        group(0, True)
                        with act.Fori(0, GROUPS - 1) as i:
                            group(i + 1, False)

                    @block.vector
                    def _(dve):
                        link = Chain(dve, dve_seq)
                        link(nc.vector.tensor_reduce(m[:, :], lp, AX.X, ALU.max))
                        nc.vector.tensor_tensor(z[:, :, :], lp, bc(m), ALU.subtract).then_inc(shifted, 1)
                        dve.sem_inc(o_out, 2)
                        dve.sem_inc(fu_ready, 2)
                        dve.sem_inc(y_added, 1)

                        def ranks():
                            dve.wait_ge(expd, 1)
                            link(nc.vector.tensor_reduce(s[:, :], pr[:, :, :], AX.X, ALU.add))
                            link(nc.vector.reciprocal(s[:, :], s[:, :]))
                            link(nc.vector.tensor_tensor(pr[:, :, :], pr[:, :, :], bc(s), ALU.mult))
                            pj = pr[:, :, :].unsqueeze(2).broadcast_to([P, NT, NE, NE])
                            pe_ = pr[:, :, :].unsqueeze(3).broadcast_to([P, NT, NE, NE])
                            nc.vector.tensor_tensor(g_[:, :, :, :], pj, pe_, ALU.is_gt)
                            link(nc.vector.tensor_tensor(q_[:, :, :, :], pj, pe_, ALU.is_equal))
                            dve.wait_ge(tri_ready, 1)
                            link(nc.vector.tensor_tensor(q_[:, :, :, :], q_[:, :, :, :],
                                                         tri[:, :, :].unsqueeze(1).broadcast_to([P, NT, NE, NE]), ALU.mult))
                            link(nc.vector.tensor_tensor(g_[:, :, :, :], g_[:, :, :, :], q_[:, :, :, :], ALU.add))
                            link(nc.vector.tensor_reduce(rank[:, :, :], g_[:, :, :, :], AX.X, ALU.add))

                        def top_two():
                            nc.vector.tensor_scalar(m1[:, :, :], rank[:, :, :], 0.0, None, ALU.is_equal)
                            link(nc.vector.tensor_scalar(m2[:, :, :], rank[:, :, :], 1.0, None, ALU.is_equal))
                            link(nc.vector.tensor_tensor(z[:, :, :], m1[:, :, :], pr[:, :, :], ALU.mult))
                            link(nc.vector.tensor_reduce(pa[:, :], z[:, :, :], AX.X, ALU.add))
                            link(nc.vector.tensor_tensor(z[:, :, :], m2[:, :, :], pr[:, :, :], ALU.mult))
                            link(nc.vector.tensor_reduce(pb_[:, :], z[:, :, :], AX.X, ALU.add))
                            nc.vector.tensor_tensor(pb_[:, :], pb_[:, :], pa[:, :], ALU.subtract).then_inc(p12, 1)

                        def router_weights():
                            dve.wait_ge(e2, 1)
                            link(nc.vector.tensor_scalar(w1[:, :], w2[:, :], 1.0, None, ALU.add))
                            link(nc.vector.reciprocal(w1[:, :], w1[:, :]))
                            link(nc.vector.tensor_tensor(w2[:, :], w2[:, :], w1[:, :], ALU.mult))
                            nc.vector.tensor_tensor(m1[:, :, :], m1[:, :, :], bc(w1), ALU.mult)
                            link(nc.vector.tensor_tensor(m2[:, :, :], m2[:, :, :], bc(w2), ALU.mult))
                            link(nc.vector.tensor_tensor(fw[:, :, :], m1[:, :, :], m2[:, :, :], ALU.add))

                        def shift_biases():
                            for s in range(NS):
                                i0, n = BIAS_START[s], len(MEMBERS[s])
                                last = nc.vector.tensor_scalar(wb[:, i0:i0 + n], pb[:, i0:i0 + n], mb[:, s:s + 1], None, ALU.subtract)
                            last.then_inc(wb_ready, 1)

                        def sum_biases():
                            dve.wait_ge(wb_ready, 2)
                            for s in range(NS):
                                i0, n = BIAS_START[s], len(MEMBERS[s])
                                nc.vector.tensor_reduce(W[:, s:s + 1], wb[:, i0:i0 + n], AX.X, ALU.add)

                        def group(g, first):
                            def fuse(u):
                                e, f = divmod(u, 2)
                                dve.wait_ge(sg_ready, UNITS * g + u + 1)
                                if e >= 2:
                                    dve.wait_ge(y_ready, NE * g + e - 1)
                                nc.vector.tensor_tensor(fu[:, e % 2, f, :], sg[:, u % 2, :], gu[:, u % 2, 1, :], ALU.mult).then_inc(fu_ready, 1)

                            def add(e):
                                dve.wait_ge(y_ready, NE * g + e + 1)
                                dve.wait_ge(y_added, NE * g + e + 1)
                                for j in range(GT):
                                    dst = g_ffn[:, bass.ds(GT * g + j, 1), :].squeeze(1)
                                    w = fw[:, bass.ds(GT * g + j, 1), e:e + 1].squeeze(1)
                                    y = yp[:, j * D:(j + 1) * D]
                                    if e == 0:
                                        last = nc.vector.tensor_scalar(dst, y, w, None, ALU.mult)
                                    else:
                                        last = nc.vector.scalar_tensor_tensor(dst, y, w, dst, ALU.mult, ALU.add)
                                last.then_inc(y_added, 1)

                            def attend(step, k):
                                b = 2 * g + k
                                if step == STEP_B:
                                    dve.wait_ge(sc_ready, b + 1)
                                    nc.vector.tensor_reduce(mz[:, k, :], sc(k), AX.X, ALU.max).then_inc(mx_ready, 1)
                                    dve.wait_ge(mx_ready, b + 1)
                                    dve.wait_ge(g_out, b + 1)
                                    nc.vector.scalar_tensor_tensor(t1[:, k, :], mz[:, k, :], SCALE0, cs[:, k, :], ALU.mult, ALU.add).then_inc(t1_ready, 1)
                                    dve.wait_ge(t1_ready, b + 1)
                                    nc.vector.tensor_tensor(nb[:, k, :], cs[:, k, :], t1[:, k, :], ALU.subtract).then_inc(nb_ready, 1)
                                elif step == STEP_D:
                                    dve.wait_ge(probs, 2 * b + 2)
                                    nc.vector.reciprocal(ri[:, k, :], rs[:, k, :]).then_inc(rinv, 1)
                                    dve.wait_ge(rinv, b + 1)
                                    dve.wait_ge(o_ready, 2 * g + 2)
                                    for s in range(TPB):
                                        last = nc.vector.scalar_tensor_tensor(s_att[:, bass.ds(TPB * b + s, 1), :].squeeze(1), op(k)[:, s, :], ri[:, k, s:s + 1], bprime[:, :],
                                                                              ALU.mult, ALU.add)
                                    last.then_inc(o_out, 1)

                            def norm_before(step):
                                if step == 2:
                                    dve.wait_ge(added, g)
                                    nc.vector.tensor_reduce(mean[:, :], before(x_res, g), AX.X, ALU.add).then_inc(mean_sum, 1)
                                    dve.wait_ge(mean_sum, g)
                                    nc.vector.tensor_scalar(mean[:, :], mean[:, :], 1.0 / D, None, ALU.mult).then_inc(mean_ready, 1)
                                    dve.wait_ge(mean_ready, g)
                                    nc.vector.tensor_tensor(before(xn, g), before(x_res, g), over_g(mean), ALU.subtract).then_inc(centered, 1)
                                elif step == 5:
                                    dve.wait_ge(squared, g)
                                    nc.vector.tensor_reduce(var[:, :], sq[:, :, :], AX.X, ALU.add).then_inc(var_sum, 1)
                                    dve.wait_ge(var_sum, g)
                                    nc.vector.tensor_scalar(var[:, :], var[:, :], 1.0 / D, EPS, ALU.mult, ALU.add).then_inc(var_ready, 1)
                                elif step == 7:
                                    dve.wait_ge(rstd_ready, g)
                                    nc.vector.tensor_tensor(before(xn, g), before(xn, g), over_g(rstd), ALU.mult)

                            for e in range(NE):
                                fuse(2 * e)
                                fuse(2 * e + 1)
                                if first and e == 0:
                                    ranks()
                                if first and e == 1:
                                    top_two()
                                    router_weights()
                                if e > 0:
                                    add(e - 1)
                                norm_before(e) if not first else None
                                if first and e == 2:
                                    shift_biases()
                                if first and e == 5:
                                    sum_biases()
                                if e in (STEP_B, STEP_D):
                                    for k in range(2):
                                        attend(e, k)
                            dve.sem_inc(xt_used, 1)
                            add(NE - 1)

                        group(0, True)
                        with dve.Fori(0, GROUPS - 1) as i:
                            group(i + 1, False)


        def layer1_block():
            qkv_d = nc.dram_tensor("a1_qkv_d", [3, HEADS, HD, BATCH, SEQ], F32, kind="Internal").ap()
            att_d = nc.dram_tensor("a1_att_d", [BATCH, HEADS, HD, SEQ], F32, kind="Internal").ap()
            with ExitStack() as c:
                r = lambda n, s, dt=F32: sb(f"l1_{n}", s, dt, c=c)
                sem = lambda n: c.enter_context(nc.semaphore(f"l1_{n}"))
                xh, xl = r("xh", [P, TOK], F32R), r("xl", [P, TOK], F32R)
                Z = r("Z", [P, 2, NP])
                xth, xtl = r("xth", [P, 2, P], F32R), r("xtl", [P, 2, P], F32R)
                xs = r("xs", [P, 2, D])
                am, sr = r("am", [P, 2, NX]), r("sr", [P, 2, NX])
                spare = g_ffn[:, :, :].rearrange("p t d -> p (t d)")
                bm = spare[:, 0:NT * 2 * SLOTS].rearrange("p (t h s) -> p t h s", t=NT, h=2)
                brow = spare[:, NT * 2 * SLOTS:].bitcast(BF16).rearrange("p (t c) -> p t c", t=NT)
                bT = r("bT", [P, NT, P], BF16)
                q, kk, vv = (r(n, [P, HD, SEQ]) for n in ("q", "k", "v"))
                acc = q
                prod = r("prod", [P, 2, HD, SEQ])
                sc = r("sc", [P, NS, SEQ])
                m = xs[:, :, :].rearrange("p k d -> p (k d)")
                den = m
                bqs = r("bqs", [P, 1])
                mean, var, rstd = r("mean", [P, GT]), r("var", [P, GT]), r("rstd", [P, GT])
                var2, rstd2 = r("var2", [P, NPT]), r("rstd2", [P, NPT])
                ew = r("ew", [P, NX, HOUT])
                flat_ew = ew[:, :, :].rearrange("p n h -> p (n h)")
                gate = xnT
                Y = s_att
                qkT = sc[:, 0:HD * 2, :].rearrange("p (j a) n -> p j (a n)", j=2)
                vT = prod[:, 0, :, :].rearrange("p d n -> p (d n)")
                sq = prod[:, 1, 0:GT // 2, :].rearrange("p d (a n) -> p (d a) n", n=D)
                attT = prod[:, 0, :, :].rearrange("p d n -> p (d n)").rearrange("p (b n) -> p b n", b=BATCH)
                s2x = xn
                s2 = prod[:, 1, :, :].rearrange("p d n -> p (d n)").rearrange("p (t d) -> p t d", t=NT)
                X2 = Z[:, 1, :].rearrange("p (j d) -> p j d", j=NPT)
                centre = r("centre", [P, D])
                prods = {"pool": (prod[:, 0, :, :], g_ffn[:, :, :].rearrange("p t d -> p (t d)").rearrange("p (h n) -> p h n", h=HD)),
                         "dve": (prod[:, 1, :, :], xn[:, :, :].rearrange("p t d -> p (t d)").rearrange("p (h n) -> p h n", h=HD))}
                XT0 = Z[:, 0, :].rearrange("p (j d) -> p j d", j=NPT)
                acc_p = c.enter_context(nc.psum_tensor("l1_acc", [P, 4, BANK], F32))
                lg = c.enter_context(nc.psum_tensor("l1_lg", [P, 4, BANK], F32))

                NC, CH = TOK // 256, 256
                E = (Z[:, :, :].rearrange("p k z -> p (k z)").rearrange("p (j q) -> p j q", j=NPT),
                     flat_ew[:, 0:NPT * CH].rearrange("p (j q) -> p j q", j=NPT))
                esum, inv = (flat_ew[:, (NPT + 2 * n) * CH:(NPT + 2 * n + 2) * CH].rearrange("p (k q) -> p k q", k=2) for n in range(2))
                wout, b_out = (flat_ew[:, (NPT + 4) * CH + n * D:(NPT + 4) * CH + (n + 1) * D] for n in range(2))
                room = lambda start, n: flat_ew[:, (NPT + 5 + start) * CH:(NPT + 5 + start + n) * CH].rearrange("p (j q) -> p j q", q=CH)
                fours, twos, esum2 = room(0, 4), room(4, 2), room(6, 2)
                den_p = acc_p[:, 0, 0:CH]
                y_p = lambda k: acc_p[:, 1 + k, 0:2 * HOUT]
                lgj = lg[:, :, :].rearrange("p b (j d) -> p (b j) d", d=D)
                lgb = lambda n: lg[:, 2 * (n % 2):2 * (n % 2) + 2, :].rearrange("p b q -> p (b q)")

                (ew_loaded, eb_loaded, consts, dve_seq, pool_seq, silu1, x1_ready, centered, squared, var_ready,
                 rstd_ready, normed, xT_ready, xh_ready, xl_ready, bqs_ready, qkv_ready, qv_out, kg_out, gate_ready, att_stored, qkv_back) = map(sem, (
                    "ew_loaded", "eb_loaded", "consts", "dve_seq", "pool_seq", "silu1", "x1_ready", "centered", "squared", "var_ready",
                    "rstd_ready", "normed", "xT_ready", "xh_ready", "xl_ready", "bqs_ready", "qkv_ready", "qv_out", "kg_out", "gate_ready", "att_stored", "qkv_back"))
                stored = [sem(f"stored_{n}") for n in "qkv"]
                (xt_ready, lg_ready, z_copied, xs_ready, mx, zs, ex, sm, si, dn, xd) = map(sem, (
                    "xt_ready", "lg_ready", "z_copied", "xs_ready", "mx", "zs", "ex", "sm", "si", "dn", "xd"))
                (clipped, slot_tr, sq2, var2_ready, rstd2_ready, tanhed, slot_tr2, xt_out, y_prod, y_ready,
                 br_ready, bT_tr, bT_out, pool_prod, dve_prod, own_red, qk_sum, sum_out, sc_in, sc_sub, sc_exp, sc_ready, m_ready, fin_last, sg_done) = map(sem, (
                    "clipped", "slot_tr", "sq2", "var2_ready", "rstd2_ready", "tanhed", "slot_tr2", "xt_out", "y_prod", "y_ready",
                    "br_ready", "bT_tr", "bT_out", "pool_prod", "dve_prod", "own_red", "qk_sum", "sum_out", "sc_in", "sc_sub", "sc_exp", "sc_ready", "m_ready", "fin_last", "sg_done"))
                (lgb_ready, exb, sum_ready, fours_ready, twos_ready, sum2_ready, den_ready, inv_ready, ct, yb_ready, yb_out, pv_prod, pv_add,
                 att_ready, att_back, gated, proj, silu2, fin, out_stored, wout_loaded) = map(sem, (
                    "lgb_ready", "exb", "sum_ready", "fours_ready", "twos_ready", "sum2_ready", "den_ready", "inv_ready", "ct", "yb_ready", "yb_out", "pv_prod", "pv_add",
                    "att_ready", "att_back", "gated", "proj", "silu2", "fin", "out_stored", "wout_loaded"))

                over_d = lambda x: x[:, :].unsqueeze(2).broadcast_to([P, GT, D])
                over_n = lambda x: x[:, :].unsqueeze(2).broadcast_to([P, NS, SEQ])
                over_s = lambda x, n: x.unsqueeze(1).broadcast_to([P, n, SEQ])
                HX = NX // 2
                HALVES = 2 * NT
                part_of = lambda buf, v: buf[:, v // 2, (v % 2) * HX:(v % 2 + 1) * HX]
                over_slots = lambda buf, v: part_of(buf, v).unsqueeze(2).broadcast_to([P, HX, SLOTS])
                zflat = lambda v: Z[:, v // 2, (v % 2) * NP // 2:(v % 2 + 1) * NP // 2]
                zhalf = lambda v: zflat(v).rearrange("p (n s) -> p n s", s=SLOTS)
                lg_half = lambda v: lg[:, 2 * (v % 2):2 * (v % 2) + 2, :].rearrange("p b q -> p (b q)")
                at_most = lambda u: not isinstance(u, int) or u < HALVES
                tile_index = lambda u, v: (u - v % 2) // 2

                def all_halves(eng, step):
                    with eng.Fori(0, HALVES // 4 - 1) as i:
                        for v in range(4):
                            step(4 * i + v, v)
                    for v in range(4):
                        step(HALVES - 4 + v, v)

                def tile_of(buf, t):
                    return buf[:, t, :] if isinstance(t, int) else buf[:, bass.ds(t, 1), :].squeeze(1)

                with nc.Block() as block:
                    @block.sync
                    def _(sp):
                        for j, dst in enumerate((q[:, :, :], kk[:, :, :], vv[:, :, :])):
                            sp.wait_ge(qv_out, 2 * GROUPS - (1 if j == 0 else 0)) if j != 1 else sp.wait_ge(kg_out, 2 * GROUPS - 1)
                            src = qkT[:, j, :] if j < 2 else vT
                            sp.dma_start(qkv_d[j].rearrange("h d b n -> (h d) (b n)"), src).then_inc(stored[j], 16)
                        for j, dst in enumerate((q[:, :, :], kk[:, :, :], vv[:, :, :])):
                            sp.wait_ge(stored[j], 16)
                            for b in range(BATCH):
                                sp.dma_start(dst[b * HEADS:(b + 1) * HEADS, :, :], qkv_d[j, :, :, b, :]).then_inc(qkv_back, 16)
                        sp.dma_start(ew[:, :, :], a["expert_w"].rearrange("n d h -> d n h")).then_inc(ew_loaded, 16)
                        sp.wait_ge(x1_ready, 1)
                        for g in range(XPT):
                            sp.dma_start(Y[g * SLOTS:(g + 1) * SLOTS, :, :],
                                         a["expert_b"].rearrange("(j g) h -> g j h", g=XPT)[g:g + 1].broadcast_to([SLOTS, NPT, HOUT])).then_inc(eb_loaded, 16)
                        sp.wait_ge(y_prod, 4)
                        sp.dma_start(wout, a["w_out"]).then_inc(wout_loaded, 16)
                        sp.dma_start(b_out, a["b_out"].broadcast_to([P, D])).then_inc(wout_loaded, 16)
                        sp.wait_ge(att_ready, 1)
                        sp.dma_start(att_d.rearrange("b h d n -> (b h) d n"), acc[:, :, :]).then_inc(att_stored, 16)
                        sp.wait_ge(att_stored, 16)
                        for b in range(BATCH):
                            sp.dma_start(attT[:, b, :], att_d[b].rearrange("h d n -> (h d) n")).then_inc(att_back, 16)
                        for n in range(GROUPS):
                            sp.wait_ge(fin, n + 1) if n < GROUPS - 1 else sp.wait_ge(fin_last, 1)
                            sp.dma_start(tiles(out)[:, 4 * n:4 * n + 4, :], x_res[:, 4 * n:4 * n + 4, :]).then_inc(out_stored, 16)
                        sp.wait_ge(out_stored, 64)

                    @block.gpsimd
                    def _(pool):
                        link = Chain(pool, pool_seq)
                        nc.gpsimd.tensor_scalar(centre[:, :], ident[:, :], -1.0 / D, None, ALU.add).then_inc(consts, 1)
                        pool.wait_ge(var_ready, 1)
                        nc.gpsimd.tensor_tensor(rstd[:, :], var[:, :], half[:, 0:1].to_broadcast([P, GT]), ALU.pow).then_inc(rstd_ready, 1)
                        pool.wait_ge(x1_ready, 1)

                        link(nc.gpsimd.memset(brow, 0.0))
                        nc.gpsimd.memset(brow[:, :, 96:99], 1.0).then_inc(consts, 1)

                        def shift(u, v):
                            pool.wait_ge(mx, u + 1)
                            nc.gpsimd.tensor_tensor(zhalf(v), zhalf(v), over_slots(am, v), ALU.subtract).then_inc(zs, 1)

                        def scale(u, v):
                            pool.wait_ge(si, u + 1)
                            nc.gpsimd.tensor_tensor(zhalf(v), zhalf(v), over_slots(sr, v), ALU.mult).then_inc(dn, 1)

                        def step(u, v):
                            shift(u + 1, (v + 1) % 4) if at_most(u + 1) else None
                            scale(u, v)

                        shift(0, 0)
                        all_halves(pool, step)

                        pool.wait_ge(qkv_back, 16 * 3 * BATCH)
                        for n, s in enumerate(QK_POOL):
                            off, w = OFFS[s], SEQ - OFFS[s]
                            if n == 1:
                                pool.wait_ge(bT_out, 2)
                            if n >= 2:
                                pool.wait_ge(qk_sum, QK_SUMS.index(QK_POOL[n - 2]) + 1)
                            nc.gpsimd.tensor_tensor(prods["pool"][n % 2][:, :, 0:w], q[:, :, off:SEQ], kk[:, :, 0:w], ALU.mult).then_inc(pool_prod, 1)
                            if n == 1:
                                pool.wait_ge(var2_ready, 1)
                                nc.gpsimd.tensor_tensor(rstd2[:, :], var2[:, :], half[:, 0:1].to_broadcast([P, NPT]), ALU.pow).then_inc(rstd2_ready, 1)

                        pool.wait_ge(qk_sum, len(QK_SUMS))
                        pool.wait_ge(own_red, len(QK_OWN))
                        nc.gpsimd.memset(acc[:, :, :], 0.0).then_inc(pv_add, 2)

                        def half_sums(c, k):
                            pool.wait_ge(exb, 4 * c + 2)
                            if not isinstance(c, int) or c >= 2:
                                pool.wait_ge(den_ready, c - 1)
                            nc.gpsimd.tensor_tensor(fours, E[k][:, 0:4, :], E[k][:, 4:8, :], ALU.add).then_inc(fours_ready, 1)
                            pool.wait_ge(fours_ready, c + 1)
                            nc.gpsimd.tensor_tensor(twos, fours[:, 0:2, :], fours[:, 2:4, :], ALU.add).then_inc(twos_ready, 1)
                            pool.wait_ge(twos_ready, c + 1)
                            nc.gpsimd.tensor_tensor(esum2[:, k, :], twos[:, 0, :], twos[:, 1, :], ALU.add).then_inc(sum2_ready, 1)

                        def value_products(t, k):
                            off = OFFS[t]
                            pool.wait_ge(pv_add, t + 1)
                            nc.gpsimd.tensor_tensor(prod[:, k, :, off:], sc[:, t:t + 1, off:].broadcast_to([P, HD, SEQ - off]),
                                                    vv[:, :, 0:SEQ - off], ALU.mult).then_inc(pv_prod, 1)

                        half_sums(0, 0)
                        pool.wait_ge(m_ready, 1)
                        nc.gpsimd.tensor_tensor(sc[:, 0:NS // 2, :], sc[:, 0:NS // 2, :], over_s(m, NS // 2), ALU.subtract).then_inc(sc_sub, 1)
                        half_sums(1, 1)
                        pool.wait_ge(sc_ready, 1)
                        for c in range(1, NC):
                            half_sums(c, c % 2) if c > 1 and c in HELPED else None
                            for t in range(sum(PV_MADE[:c]), sum(PV_MADE[:c + 1])):
                                value_products(t, t % 2)
                        pool.wait_ge(wout_loaded, 32)
                        pool.wait_ge(silu2, 1)
                        rest = slice(0, NT - GT)
                        link(nc.gpsimd.tensor_tensor(s2x[:, rest, :], g_ffn[:, rest, :], b_out.unsqueeze(1).broadcast_to([P, NT - GT, D]), ALU.mult))
                        link(nc.gpsimd.tensor_tensor(x_res[:, rest, :], x_res[:, rest, :], s2x[:, rest, :], ALU.add))
                        for n in range(GROUPS - 1):
                            sl = slice(GT * n, GT * n + GT)
                            pool.wait_ge(sg_done, n + 1)
                            nc.gpsimd.tensor_tensor(x_res[:, sl, :], x_res[:, sl, :], s2[:, sl, :], ALU.add).then_inc(fin, 1)

                    @block.scalar
                    def _(act):
                        nc.scalar.activation(g_ffn[:, LAST, :], g_ffn[:, LAST, :], ACT.Silu).then_inc(silu1, 1)

                        def load_xt(t, k):
                            cols_of = slice(t * P, (t + 1) * P) if isinstance(t, int) else bass.ds(t * P, P)
                            nc.scalar.activation(xth[:, k, :], xh[:, cols_of].bitcast(F32), ACT.Copy)
                            nc.scalar.activation(xtl[:, k, :], xl[:, cols_of].bitcast(F32), ACT.Copy).then_inc(xt_ready, 1)

                        def take_xh(n):
                            act.wait_ge(xT_ready, n + 1)
                            nc.scalar.activation(xh[:, n * BANK:(n + 1) * BANK], lg[:, n, :], ACT.Copy).then_inc(xh_ready, 1)

                        def take_qv(n):
                            sl = slice(n * BANK, (n + 1) * BANK)
                            act.wait_ge(qkv_ready, 4 * n + 1)
                            nc.scalar.activation(qkT[:, 0, sl], acc_p[:, 0, :], ACT.Identity, bias=bqs[:, 0:1], scale=SCALE1).then_inc(qv_out, 1)
                            act.wait_ge(qkv_ready, 4 * n + 3)
                            nc.scalar.activation(vT[:, sl], acc_p[:, 2, :], ACT.Identity, bias=cols[:, COL["b1v"]:COL["b1v"] + 1]).then_inc(qv_out, 1)

                        take_xh(0)
                        take_xh(1)
                        take_xh(2)
                        act.wait_ge(centered, 1)
                        nc.scalar.activation(sq, xn[:, LAST, :], ACT.Square).then_inc(squared, 1)
                        act.wait_ge(bqs_ready, 1)
                        take_qv(0)
                        take_qv(1)
                        take_xh(3)
                        take_qv(2)
                        act.wait_ge(xl_ready, 4)
                        load_xt(0, 0)
                        load_xt(1, 1)
                        take_qv(3)
                        act.sem_inc(z_copied, 2)
                        nc.scalar.preload_act_table(ACT.Exp)

                        def copy_out(u, v):
                            act.wait_ge(lg_ready, u + 1)
                            act.wait_ge(xd, u + 1)
                            nc.scalar.activation(zflat(v), lg_half(v), ACT.Copy).then_inc(z_copied, 1)
                            if v % 2:
                                t = u // 2 if isinstance(u, int) else tile_index(u, v)
                                nc.scalar.activation(xs[:, v // 2, :], tile_of(xn, t), ACT.Copy).then_inc(xs_ready, 1)

                        def expo(u, v):
                            act.wait_ge(zs, u + 1)
                            nc.scalar.activation(zhalf(v), zhalf(v), ACT.Exp).then_inc(ex, 1)

                        def step(u, v):
                            copy_out(u + 2, (v + 2) % 4) if at_most(u + 2) else None
                            expo(u + 1, (v + 1) % 4) if at_most(u + 1) else None
                            if v % 2 == 0 and at_most(u + 4):
                                act.wait_ge(lg_ready, u + 2)
                                load_xt(tile_index(u, v) + 2, v // 2)

                        copy_out(0, 0)
                        copy_out(1, 1)
                        expo(0, 0)
                        all_halves(act, step)
                        act.wait_ge(stored[1], 16)
                        nc.scalar.activation(sc[:, :, :], over_n(mb), ACT.Copy).then_inc(sc_in, 1)
                        for n in range(2):
                            act.wait_ge(bT_tr, n + 1)
                            nc.scalar.activation(bT[:, 8 * n:8 * n + 8, :].rearrange("p t q -> p (t q)"),
                                                 acc_p[:, n, :].bitcast(BF16), ACT.Copy).then_inc(bT_out, 1)

                        def take_sums(count):
                            for _ in range(count):
                                i = taken[0]
                                s = QK_SUMS[i]
                                off, w = OFFS[s], SEQ - OFFS[s]
                                act.wait_ge(qk_sum, i + 1)
                                ins = nc.scalar.activation(sc[:, s, off:SEQ], acc_p[:, 2 + i % 2, 0:w], ACT.Identity, bias=mb[:, s:s + 1])
                                ins.then_inc(sum_out, 1)
                                taken[0] += 1

                        taken = [0]
                        act.wait_ge(sc_in, 1)
                        for j in range(NPT):
                            act.wait_ge(slot_tr, j // 4 + 1) if j % 4 == 0 else None
                            last = nc.scalar.activation(XT0[:, j, :], lgj[:, j, :], ACT.Square, accum_out=var2[:, j:j + 1])
                        last.then_inc(sq2, 1)
                        take_sums(2)
                        act.wait_ge(rstd2_ready, 1)
                        for j in range(NPT):
                            last = nc.scalar.activation(X2[:, j, :], lgj[:, j, :], ACT.Tanh, scale=rstd2[:, j:j + 1])
                        last.then_inc(tanhed, 1)
                        take_sums(2)
                        for n in range(4):
                            act.wait_ge(slot_tr2, n + 1)
                            nc.scalar.activation(Z[:, 0, n * BANK:(n + 1) * BANK], lg[:, n, :], ACT.Copy).then_inc(xt_out, 1)
                        take_sums(len(QK_SUMS) - 4)
                        for n, s in enumerate(QK_OWN):
                            off = OFFS[s]
                            act.wait_ge(own_red, n + 1)
                            nc.scalar.activation(sc[:, s, off:SEQ], sc[:, s, off:SEQ], ACT.Identity, bias=mb[:, s:s + 1]).then_inc(sc_in, 1)
                        act.wait_ge(y_prod, 4)

                        def exp_b(c, k):
                            for n in range(4):
                                act.wait_ge(lgb_ready, 4 * c + n + 1)
                                act.wait_ge(yb_ready, c + 1) if n == 0 else None
                                nc.scalar.activation(E[k][:, 4 * n:4 * n + 4, :].rearrange("p j q -> p (j q)"), lgb(n), ACT.Exp).then_inc(exb, 1)

                        def y_copy(c, k):
                            act.wait_ge(yb_ready, c + 3)
                            dst = g_ffn[:, 2 * c:2 * c + 2, :] if isinstance(c, int) else g_ffn[:, bass.ds(2 * c, 2), :]
                            nc.scalar.activation(dst, y_p(k).rearrange("p (j d) -> p j d", j=2), ACT.Copy).then_inc(yb_out, 1)

                        exp_b(0, 0)
                        exp_b(1, 1)
                        act.wait_ge(sc_sub, 2)
                        nc.scalar.activation(sc[:, :, :], sc[:, :, :], ACT.Exp).then_inc(sc_exp, 1)
                        act.wait_ge(sc_exp, 1)
                        for s in SHARED:
                            last = nc.scalar.activation(sc[:, s, :], sc[:, s, :], ACT.Copy, scale=W[:, s:s + 1])
                        last.then_inc(sc_ready, 1)
                        y_copy(0, 0)
                        with act.Fori(0, NC // 2 - 2) as i:
                            for k in (1, 0):
                                c = 2 * i + 2 - k
                                exp_b(c + 1, 1 - k)
                                y_copy(c, k)
                        exp_b(NC - 2, 0)
                        y_copy(NC - 3, 1)
                        exp_b(NC - 1, 1)
                        nc.scalar.activation(gate[:, :], gate[:, :], ACT.Sigmoid).then_inc(gate_ready, 1)
                        act.wait_ge(yb_out, NC)
                        nc.scalar.activation(g_ffn[:, 0:NT - GT, :], g_ffn[:, 0:NT - GT, :], ACT.Silu).then_inc(silu2, 1)
                        y_copy(NC - 2, 0)
                        y_copy(NC - 1, 1)
                        act.wait_ge(yb_out, NC + 2)
                        nc.scalar.activation(g_ffn[:, LAST, :], g_ffn[:, LAST, :], ACT.Silu).then_inc(silu2, 1)

                    @block.vector
                    def _(dve):
                        link = Chain(dve, dve_seq)
                        nc.vector.tensor_scalar(bqs[:, :], cols[:, COL["b1q"]:COL["b1q"] + 1], SCALE1, None, ALU.mult).then_inc(bqs_ready, 1)
                        dve.wait_ge(silu1, 1)
                        link(nc.vector.tensor_tensor(g_ffn[:, LAST, :], g_ffn[:, LAST, :], s_att[:, LAST, :], ALU.mult))
                        link(nc.vector.tensor_tensor(x_res[:, LAST, :], x_res[:, LAST, :], g_ffn[:, LAST, :], ALU.add))
                        nc.vector.tensor_reduce(mean[:, :], x_res[:, LAST, :], AX.X, ALU.add).then_inc(x1_ready, 1)
                        dve.wait_ge(x1_ready, 1)
                        link(nc.vector.tensor_scalar(mean[:, :], mean[:, :], 1.0 / D, None, ALU.mult))
                        nc.vector.tensor_tensor(xn[:, LAST, :], x_res[:, LAST, :], over_d(mean), ALU.subtract).then_inc(centered, 1)

                        def take_xl(n):
                            dve.wait_ge(xh_ready, n + 1)
                            sl = slice(n * BANK, (n + 1) * BANK)
                            nc.vector.tensor_tensor(xl[:, sl], lg[:, n, :], xh[:, sl].bitcast(F32), ALU.subtract).then_inc(xl_ready, 1)

                        def take_kg(n):
                            sl = slice(n * BANK, (n + 1) * BANK)
                            dve.wait_ge(qkv_ready, 4 * n + 2)
                            nc.vector.tensor_scalar(qkT[:, 1, sl], acc_p[:, 1, :], cols[:, COL["b1k"]:COL["b1k"] + 1], None, ALU.add).then_inc(kg_out, 1)
                            dve.wait_ge(qkv_ready, 4 * n + 4)
                            nc.vector.tensor_scalar(gate[:, sl], acc_p[:, 3, :], cols[:, COL["bgate"]:COL["bgate"] + 1], None, ALU.add).then_inc(kg_out, 1)

                        for n in range(3):
                            take_xl(n)
                        dve.wait_ge(squared, 1)
                        link(nc.vector.tensor_reduce(var[:, :], sq, AX.X, ALU.add))
                        nc.vector.tensor_scalar(var[:, :], var[:, :], 1.0 / D, EPS, ALU.mult, ALU.add).then_inc(var_ready, 1)
                        take_kg(0)
                        dve.wait_ge(rstd_ready, 1)
                        nc.vector.tensor_tensor(xn[:, LAST, :], xn[:, LAST, :], over_d(rstd), ALU.mult).then_inc(normed, 1)
                        take_kg(1)
                        take_xl(3)
                        take_kg(2)
                        take_kg(3)
                        def maxima(u, v):
                            dve.wait_ge(z_copied, u + 3)
                            nc.vector.tensor_reduce(part_of(am, v), zhalf(v), AX.X, ALU.max)
                            t = tile_index(u, v)
                            bh = bm[:, t, v % 2, :] if isinstance(t, int) else bm[:, bass.ds(t, 1), v % 2, :].squeeze(1)
                            nc.vector.tensor_reduce(bh, zhalf(v).rearrange("p n s -> p s n"), AX.X, ALU.max).then_inc(mx, 1)

                        def sums(u, v):
                            dve.wait_ge(ex, u + 1)
                            nc.vector.tensor_reduce(part_of(sr, v), zhalf(v), AX.X, ALU.add).then_inc(sm, 1)
                            dve.wait_ge(sm, u + 1)
                            nc.vector.reciprocal(part_of(sr, v), part_of(sr, v)).then_inc(si, 1)

                        def step(u, v):
                            maxima(u + 1, (v + 1) % 4) if at_most(u + 1) else None
                            sums(u, v)

                        maxima(0, 0)
                        all_halves(dve, step)

                        dve.wait_ge(xd, 2 * NT + 4)
                        for n in range(4):
                            nc.vector.tensor_scalar(Z[:, 0, n * BANK:(n + 1) * BANK], acc_p[:, n, :], -33000.0, 65000.0, ALU.max, ALU.min).then_inc(clipped, 1)
                        bn, bres = bm[:, :, 0, :], bm[:, :, 1, :]
                        link(nc.vector.tensor_tensor(bn, bn, bres, ALU.max))
                        link(nc.vector.tensor_scalar(brow[:, :, 0:SLOTS], bn, -1.0, None, ALU.mult))
                        link(nc.vector.scalar_tensor_tensor(bres, bn, -1.0, brow[:, :, 0:SLOTS], ALU.mult, ALU.subtract))
                        link(nc.vector.tensor_copy(brow[:, :, SLOTS:2 * SLOTS], bres))
                        link(nc.vector.tensor_tensor(bres, bres, brow[:, :, SLOTS:2 * SLOTS], ALU.subtract))
                        nc.vector.tensor_copy(brow[:, :, 2 * SLOTS:3 * SLOTS], bres).then_inc(br_ready, 1)

                        def score_product(k):
                            s = DVE_ORDER[k]
                            off, w = OFFS[s], SEQ - OFFS[s]
                            buf = prods["dve"][k % 2]
                            if k >= 2 and DVE_ORDER[k - 2] in QK_SUMS:
                                dve.wait_ge(qk_sum, QK_SUMS.index(DVE_ORDER[k - 2]) + 1)
                            ins = nc.vector.tensor_tensor(buf[:, :, 0:w], q[:, :, off:SEQ], kk[:, :, 0:w], ALU.mult)
                            if s in QK_SUMS:
                                ins.then_inc(dve_prod, 1)
                            else:
                                n = QK_OWN.index(s)
                                link(ins)
                                nc.vector.tensor_reduce(sc[:, s, off:SEQ], buf[:, :, 0:w].rearrange("p d n -> p n d"), AX.X, ALU.add).then_inc(own_red, 1)
                                dve.wait_ge(own_red, n + 1)

                        dve.wait_ge(qkv_back, 16 * 3 * BATCH)
                        score_product(0)
                        score_product(1)
                        dve.wait_ge(sq2, 1)
                        nc.vector.tensor_scalar(var2[:, :], var2[:, :], 1.0 / D, EPS, ALU.mult, ALU.add).then_inc(var2_ready, 1)
                        dve.wait_ge(sc_in, 1)
                        for k in range(2, len(DVE_ORDER)):
                            score_product(k)
                        dve.wait_ge(eb_loaded, 16 * XPT)
                        for n in range(4):
                            dve.wait_ge(y_prod, n + 1)
                            Yn = Y[:, 4 * n:4 * n + 4, :].rearrange("p t d -> p (t d)")
                            nc.vector.tensor_tensor(Yn, lg[:, n, :], Yn, ALU.add).then_inc(y_ready, 1)
                        dve.wait_ge(sum_out, len(QK_SUMS))
                        dve.wait_ge(sc_in, 1 + len(QK_OWN))
                        nc.vector.tensor_reduce(m, sc[:, :, :].rearrange("p s n -> p n s"), AX.X, ALU.max).then_inc(m_ready, 1)
                        dve.wait_ge(m_ready, 1)
                        nc.vector.tensor_tensor(sc[:, NS // 2:, :], sc[:, NS // 2:, :], over_s(m, NS - NS // 2), ALU.subtract).then_inc(sc_sub, 1)

                        def add_pv(t, k):
                            dve.wait_ge(pv_prod, t + 1)
                            dve.wait_ge(pv_add, t + 2)
                            off = OFFS[t]
                            nc.vector.tensor_tensor(acc[:, :, off:], acc[:, :, off:], prod[:, k, :, off:], ALU.add).then_inc(pv_add, 1)

                        def sums_b(c, k):
                            dve.wait_ge(exb, 4 * c + 4)
                            mine = slice(NPT // 2 if c in HELPED else 0, NPT)
                            nc.vector.tensor_reduce(esum[:, k, :], E[k][:, mine, :].rearrange("p j q -> p q j"), AX.X, ALU.add).then_inc(sum_ready, 1)

                        def weigh(c, k):
                            dve.wait_ge(den_ready, c + 1)
                            nc.vector.reciprocal(inv[:, k, :], den_p).then_inc(inv_ready, 1)
                            dve.wait_ge(inv_ready, c + 2)
                            for n in range(4):
                                part = E[k][:, 4 * n:4 * n + 4, :]
                                nc.vector.tensor_tensor(part, part, inv[:, k, :].unsqueeze(1).broadcast_to([P, 4, CH]), ALU.mult).then_inc(ct, 1)

                        sums_b(0, 0)
                        weigh(0, 0)
                        dve.wait_ge(sc_ready, 1)
                        link(nc.vector.tensor_reduce(den, sc[:, :, :].rearrange("p s n -> p n s"), AX.X, ALU.add))
                        link(nc.vector.reciprocal(den, den))
                        added = 0
                        for c in range(1, NC):
                            before, after = PV_ADDED[c]
                            if c == NC - 1:
                                dve.wait_ge(pv_add, NT + 2)
                                nc.vector.tensor_tensor(acc[:, :, :], acc[:, :, :], den.unsqueeze(1).broadcast_to([P, HD, SEQ]), ALU.mult).then_inc(att_ready, 1)
                            sums_b(c, c % 2)
                            for t in range(added, added + before):
                                add_pv(t, t % 2)
                            weigh(c, c % 2)
                            for t in range(added + before, added + before + after):
                                add_pv(t, t % 2)
                            added += before + after
                        dve.wait_ge(att_back, 16 * BATCH)
                        dve.wait_ge(gate_ready, 1)
                        nc.vector.tensor_tensor(attT, attT, gate[:, :].rearrange("p (b n) -> p b n", b=BATCH), ALU.mult).then_inc(gated, 1)
                        dve.wait_ge(silu2, 1)
                        for n in range(GROUPS - 1):
                            dve.wait_ge(proj, n + 1)
                            sl = slice(GT * n, GT * n + GT)
                            nc.vector.tensor_tensor(s2[:, sl, :], lg[:, n, :].rearrange("p (j d) -> p j d", j=GT), g_ffn[:, sl, :], ALU.mult).then_inc(sg_done, 1)
                        dve.wait_ge(proj, GROUPS)
                        dve.wait_ge(silu2, 2)
                        link(nc.vector.tensor_tensor(s2[:, LAST, :], lg[:, GROUPS - 1, :].rearrange("p (j d) -> p j d", j=GT), b_out.unsqueeze(1).broadcast_to([P, GT, D]), ALU.add))
                        link(nc.vector.tensor_tensor(s2[:, LAST, :], s2[:, LAST, :], g_ffn[:, LAST, :], ALU.mult))
                        nc.vector.tensor_tensor(x_res[:, LAST, :], x_res[:, LAST, :], s2[:, LAST, :], ALU.add).then_inc(fin_last, 1)

                    @block.tensor
                    def _(pe):
                        def turn(n):
                            for t in range(4 * n, 4 * n + 4):
                                last = nc.tensor.transpose(lg[:, n, (t % 4) * P:(t % 4 + 1) * P], xn[:, t, :], ident[:, :])
                            last.then_inc(xT_ready, 1)

                        def project(n):
                            sl = slice(n * BANK, (n + 1) * BANK)
                            pe.wait_ge(xl_ready, n + 1)
                            for j in range(4):
                                if n > 0:
                                    pe.wait_ge(qv_out if j % 2 == 0 else kg_out, 2 * n - 1 + j // 2)
                                nc.tensor.matmul(acc_p[:, j, :], wh1[:, j, :], xh[:, sl], start=True, stop=False)
                                nc.tensor.matmul(acc_p[:, j, :], wh1[:, j, :], xl[:, sl], start=False, stop=False)
                                nc.tensor.matmul(acc_p[:, j, :], wl1[:, j, :], xh[:, sl], start=False, stop=True).then_inc(qkv_ready, 1)

                        for n in range(3):
                            turn(n)
                        project(0)
                        project(1)
                        pe.wait_ge(normed, 1)
                        turn(3)
                        project(2)
                        project(3)
                        pe.wait_ge(qv_out, 2 * GROUPS)
                        pe.wait_ge(kg_out, 2 * GROUPS)
                        for n in range(4):
                            nc.tensor.matmul(acc_p[:, n, :], zero[:, :], rows[:, n * BANK:(n + 1) * BANK], start=True, stop=True, skip_group_check=True)
                        pe.sem_inc(xd, 4)

                        def logits(u, v):
                            if v % 2 == 0:
                                pe.wait_ge(xt_ready, tile_index(u, v) + 1)
                            pe.wait_ge(z_copied, u + 1)
                            k = v // 2
                            for n in (2 * (v % 2), 2 * (v % 2) + 1):
                                sl = slice(n * BANK, (n + 1) * BANK)
                                nc.tensor.matmul(lg[:, n, :], xth[:, k, :], ph[:, sl], start=True, stop=False)
                                nc.tensor.matmul(lg[:, n, :], xth[:, k, :], pl[:, sl], start=False, stop=False)
                                nc.tensor.matmul(lg[:, n, :], xtl[:, k, :], ph[:, sl], start=False, stop=False)
                                last = nc.tensor.matmul(lg[:, n, :], onerow[:, :], rows[:, sl], start=False, stop=True)
                            last.then_inc(lg_ready, 1)

                        def slot_inputs(u, v):
                            if v % 2 == 0:
                                pe.wait_ge(xs_ready, tile_index(u, v) + 1)
                            pe.wait_ge(dn, u + 1)
                            k = v // 2
                            for n in (2 * (v % 2), 2 * (v % 2) + 1):
                                last = nc.tensor.matmul(acc_p[:, n, :], xs[:, k, :], Z[:, k, n * BANK:(n + 1) * BANK], start=False, stop=True, skip_group_check=True)
                            last.then_inc(xd, 1)

                        def step(u, v):
                            logits(u + 3, (v + 3) % 4) if at_most(u + 3) else None
                            slot_inputs(u, v)

                        for u in range(3):
                            logits(u, u)
                        all_halves(pe, step)

                        pe.wait_ge(z_copied, 2 * NT + 2)
                        pe.wait_ge(consts, 1)
                        for j in range(NPT):
                            if j % 4 == 0:
                                pe.wait_ge(clipped, j // 4 + 1)
                            last = nc.tensor.matmul(lgj[:, j, :], Z[:, 0, j * P:(j + 1) * P], centre[:, :], start=True, stop=True)
                            last.then_inc(slot_tr, 1) if j % 4 == 3 else None
                        pe.wait_ge(br_ready, 1)
                        for n in range(2):
                            bank = acc_p[:, n, :].bitcast(BF16)
                            for t in range(8):
                                last = nc.tensor.transpose(bank[:, t * P:(t + 1) * P], brow[:, 8 * n + t, :], identb[:, :])
                            last.then_inc(bT_tr, 1)

                        def score_sums(start, stop):
                            for i in range(start, stop):
                                s = QK_SUMS[i]
                                w, by = SEQ - OFFS[s], QK_BY[s]
                                n = (QK_POOL if by == "pool" else QK_DVE).index(s)
                                buf = prods[by][(QK_POOL if by == "pool" else DVE_ORDER).index(s) % 2]
                                pe.wait_ge(pool_prod if by == "pool" else dve_prod, n + 1)
                                if i >= 2:
                                    pe.wait_ge(sum_out, i - 1)
                                for d in range(HD):
                                    last = nc.tensor.matmul(acc_p[:, 2 + i % 2, 0:w], ident[:, :], buf[:, d, 0:w], start=d == 0, stop=d == HD - 1)
                                last.then_inc(qk_sum, 1)

                        score_sums(0, 4)
                        pe.wait_ge(tanhed, 1)
                        for j in range(NPT):
                            last = nc.tensor.transpose(lgj[:, j, :], X2[:, j, :], ident[:, :])
                            last.then_inc(slot_tr2, 1) if j % 4 == 3 else None
                        score_sums(4, 6)
                        pe.wait_ge(ew_loaded, 16)
                        for j in range(NPT):
                            if j % 4 == 0:
                                pe.wait_ge(xt_out, j // 4 + 1)
                            for g in range(XPT):
                                last = nc.tensor.matmul(lg[g * SLOTS:(g + 1) * SLOTS, j // 4, (j % 4) * HOUT:(j % 4 + 1) * HOUT],
                                                        XT0[:, j, g * SLOTS:(g + 1) * SLOTS], ew[:, XPT * j + g, :], start=True, stop=True,
                                                        tile_position=(0, g * SLOTS))
                            last.then_inc(y_prod, 1) if j % 4 == 3 else None
                        score_sums(6, len(QK_SUMS))
                        pe.wait_ge(y_ready, 4)

                        def logits_b(c, k):
                            tokens = slice(c * CH, (c + 1) * CH) if isinstance(c, int) else bass.ds(c * CH, CH)
                            bt = (bT[:, 2 * c:2 * c + 2, :] if isinstance(c, int) else bT[:, bass.ds(2 * c, 2), :]).rearrange("p t q -> p (t q)")
                            for n in range(4):
                                if not isinstance(c, int) or c > 0 or n >= 2:
                                    pe.wait_ge(exb, 4 * c + n - 1)
                                for j in range(4):
                                    sl = slice((4 * n + j) * P, (4 * n + j + 1) * P)
                                    dst = lgb(n)[:, j * CH:(j + 1) * CH]
                                    nc.tensor.matmul(dst, ph[:, sl], xh[:, tokens], start=True, stop=False)
                                    nc.tensor.matmul(dst, ph[:, sl], xl[:, tokens], start=False, stop=False)
                                    nc.tensor.matmul(dst, pl[:, sl], xh[:, tokens], start=False, stop=False)
                                    last = nc.tensor.matmul(dst, rows[:, sl], bt, start=False, stop=True)
                                last.then_inc(lgb_ready, 1)

                        def denominators(c, k, helped=True):
                            pe.wait_ge(inv_ready, c + 1)
                            same = same_slot[:, :, :].rearrange("p g s -> p (g s)")
                            if helped:
                                pe.wait_ge(sum2_ready, c + 1)
                                nc.tensor.matmul(den_p, same, esum2[:, k, :], start=True, stop=False)
                            pe.wait_ge(sum_ready, c + 1)
                            nc.tensor.matmul(den_p, same, esum[:, k, :], start=not helped, stop=True).then_inc(den_ready, 1)

                        def outputs(c, k, tiles_of=(0, 1)):
                            pe.wait_ge(yb_out, c + 1)
                            for t in tiles_of:
                                for jj in range(NPT):
                                    if t == 0 and jj % 4 == 0:
                                        pe.wait_ge(ct, 4 * c + jj // 4 + 1)
                                    last = nc.tensor.matmul(y_p(k)[:, t * D:(t + 1) * D], E[k][:, jj, t * P:(t + 1) * P], Y[:, jj, :], start=jj == 0, stop=jj == NPT - 1)
                            last.then_inc(yb_ready, 1) if 1 in tiles_of else None

                        pe.sem_inc(inv_ready, 1)
                        pe.sem_inc(yb_out, 2)
                        pe.sem_inc(yb_ready, 2)
                        logits_b(0, 0)
                        logits_b(1, 1)
                        denominators(0, 0)
                        outputs(0, 0)
                        with pe.Fori(0, len(HELPED) // 2) as i:
                            for k in (1, 0):
                                c = 2 * i + 2 - k
                                denominators(c, k)
                                logits_b(c + 1, 1 - k)
                                outputs(c, k)
                        denominators(NC - 3, 1, False)
                        logits_b(NC - 2, 0)
                        outputs(NC - 3, 1)
                        denominators(NC - 2, 0, False)
                        logits_b(NC - 1, 1)
                        outputs(NC - 2, 0, (0,))
                        denominators(NC - 1, 1, False)
                        outputs(NC - 2, 0, (1,))
                        outputs(NC - 1, 1)
                        pe.wait_ge(gated, 1)
                        pe.wait_ge(wout_loaded, 32)
                        for t in range(NT):
                            last = nc.tensor.matmul(lg[:, t // 4, (t % 4) * D:(t % 4 + 1) * D], attT[:, t // 2, (t % 2) * P:(t % 2 + 1) * P], wout, start=True, stop=True)
                            last.then_inc(proj, 1) if t % 4 == 3 else None

        with ExitStack() as c0:
            layer0_front(c0)
            layer0_main(c0)
        layer1_block()


def kernel(L0_attn_hidden_states, L0_attn_Wq, L0_attn_bq, L0_attn_Wk, L0_attn_bk, L0_attn_Wv, L0_attn_bv, L0_attn_Wo,
           L0_attn_bo, L0_ffn_kernel_router_DE, L0_ffn_kernel_gating_EDF, L0_ffn_kernel_up_EDF, L0_ffn_kernel_down_EFD,
           L1_attn_w_qkv, L1_attn_b_qkv, L1_attn_w_out, L1_attn_b_out, L1_attn_w_gate, L1_attn_b_gate, L1_attn_pos_bias,
           L1_ffn_phi_w, L1_ffn_phi_b, L1_ffn_expert_w, L1_ffn_expert_b):
    import numpy as np
    import concourse.bacc as bacc
    from concourse.bass_utils import run_bass_kernel_spmd

    lay = lambda v: np.ascontiguousarray(v)
    halves = lambda v: list(np.asarray(v).reshape(-1, P))
    arrays = {
        "x": lay(np.asarray(L0_attn_hidden_states).reshape(TOK, D)),
        "wq": lay(L0_attn_Wq), "wk": lay(L0_attn_Wk), "wv": lay(L0_attn_Wv), "woT": lay(np.asarray(L0_attn_Wo).T),
        "bo": lay(np.asarray(L0_attn_bo).reshape(1, D)),
        "router": lay(L0_ffn_kernel_router_DE), "gating": lay(L0_ffn_kernel_gating_EDF),
        "up": lay(L0_ffn_kernel_up_EDF), "down": lay(L0_ffn_kernel_down_EFD),
        "w_qkv": lay(L1_attn_w_qkv), "w_gate": lay(L1_attn_w_gate), "w_out": lay(L1_attn_w_out),
        "b_out": lay(np.asarray(L1_attn_b_out).reshape(1, D)),
        "pos_bias": lay(np.tile(np.asarray(L1_attn_pos_bias)[BIAS_ORDER].T, (BATCH, 1))),
        "phiT": lay(np.asarray(L1_ffn_phi_w).T), "phi_b": lay(np.asarray(L1_ffn_phi_b).reshape(1, NP)),
        "expert_w": lay(L1_ffn_expert_w), "expert_b": lay(L1_ffn_expert_b),
        "cols": lay(np.stack(halves(L0_attn_bq) + halves(L0_attn_bk) + halves(L0_attn_bv) + halves(L1_attn_b_qkv)
                             + halves(L1_attn_b_gate), axis=1)),
    }
    nc = bacc.Bacc("TRN2", target_bir_lowering=False, num_devices=1)
    args = {n: nc.dram_tensor(f"in_{n}", v.shape, mybir.dt.from_np(v.dtype), kind="ExternalInput").ap() for n, v in arrays.items()}
    out = nc.dram_tensor("out_x", (TOK, D), F32, kind="ExternalOutput").ap()
    build(nc, args, out)
    r = run_bass_kernel_spmd(nc, [{f"in_{n}": v for n, v in arrays.items()}], core_ids=[0])
    return r.results[0]["out_x"].reshape(BATCH, SEQ, D)
```
